# Optimizing a Trainium2 kernel written in Bass

```python
import numpy as np
import jax
import jax.numpy as jnp

def _softmax(x, axis=-1):
    return jax.nn.softmax(x, axis=axis)

def _gelu(x):
    return jax.nn.gelu(x, approximate=True)

def _silu(x):
    return jax.nn.silu(x)

def _sigmoid(x):
    return jax.nn.sigmoid(x)

def _layernorm(x, axis=-1, eps=1e-05):
    m = jnp.mean(x, axis=axis, keepdims=True)
    v = jnp.var(x, axis=axis, keepdims=True)
    return (x - m) / jnp.sqrt(v + eps)

def _scatter_add(tgt, idx, src, axis=0):
    return tgt.at[idx].add(src)

def _segment_sum(src, seg, n):
    return jax.ops.segment_sum(src, seg, n)
kernel_name = 'mk_sandwich_d4_jaxref_r8_c25b3a'

def setup_inputs(seed: int=0):
    np.random.seed(seed)
    _w = jnp.asarray

    def _L0_attn_setup():
        import jax, jax.numpy as jnp
        import numpy as np
        B, T, C, FFN, N_LAYER, LAYER_ID = (4, 256, 128, 512, 24, 1)
        EPS = 1e-05

        def _ln(z, g, b):
            m = jnp.mean(z, axis=-1, keepdims=True)
            v = jnp.mean(jnp.square(z - m), axis=-1, keepdims=True)
            return (z - m) * jax.lax.rsqrt(v + EPS) * g + b

        def _shift(z):
            return jnp.pad(z, ((0, 0), (1, 0), (0, 0)))[:, :-1]

        def _wkv(time_decay, u, k, v):
            w = -jnp.exp(time_decay)
            kt = jnp.moveaxis(k, 1, 0)
            vt = jnp.moveaxis(v, 1, 0)
            aa = jnp.zeros_like(kt[0])
            bb = jnp.zeros_like(kt[0])
            pp = jnp.full_like(kt[0], -1e+38)

            def step(carry, kv):
                aa, bb, pp = carry
                kk, vv = kv
                ww = u + kk
                p = jnp.maximum(pp, ww)
                e1 = jnp.exp(pp - p)
                e2 = jnp.exp(ww - p)
                out = (e1 * aa + e2 * vv) / (e1 * bb + e2)
                ww2 = pp + w
                p2 = jnp.maximum(ww2, kk)
                e1b = jnp.exp(ww2 - p2)
                e2b = jnp.exp(kk - p2)
                return ((e1b * aa + e2b * vv, e1b * bb + e2b, p2), out)
            _, out = jax.lax.scan(step, (aa, bb, pp), (kt, vt))
            return jnp.moveaxis(out, 0, 1)
        key = jax.random.key(seed)
        ks = jax.random.split(key, 10)
        scale = 0.02

        def w(k, shape):
            return jax.random.normal(k, shape, jnp.float32) * scale
        r01 = LAYER_ID / (N_LAYER - 1)
        r10 = 1.0 - LAYER_ID / N_LAYER
        ddd = np.arange(C, dtype=np.float64) / C
        h = np.arange(C, dtype=np.float64)
        decay = -5.0 + 8.0 * (h / (C - 1)) ** (0.7 + 1.3 * r01)
        zigzag = np.array([(i + 1) % 3 - 1 for i in range(C)], dtype=np.float64) * 0.5
        tfirst = np.log(0.3) + zigzag
        return {'x': jax.random.normal(ks[0], (B, T, C), jnp.float32), 'ln1_w': jnp.ones((C,), jnp.float32), 'ln1_b': jnp.zeros((C,), jnp.float32), 'ln2_w': jnp.ones((C,), jnp.float32), 'ln2_b': jnp.zeros((C,), jnp.float32), 'time_decay': jnp.asarray(decay, jnp.float32), 'time_first': jnp.asarray(tfirst, jnp.float32), 'tmk': jnp.asarray(ddd ** r10, jnp.float32), 'tmv': jnp.asarray(ddd ** r10 + 0.3 * r01, jnp.float32), 'tmr': jnp.asarray(ddd ** (0.5 * r10), jnp.float32), 'att_kw': w(ks[1], (C, C)), 'att_vw': w(ks[2], (C, C)), 'att_rw': w(ks[3], (C, C)), 'att_ow': w(ks[4], (C, C)), 'f_tmk': jnp.asarray(ddd ** r10, jnp.float32), 'f_tmr': jnp.asarray(ddd ** r10, jnp.float32), 'f_kw': w(ks[5], (FFN, C)), 'f_rw': w(ks[6], (C, C)), 'f_vw': w(ks[7], (C, FFN))}
    _L0_attn_in = _L0_attn_setup()

    def _L0_ffn_setup():
        import jax, jax.numpy as jnp
        import numpy as np
        D_MODEL = 128
        M = 64
        INNER = 16
        key = jax.random.key(seed)
        ks = jax.random.split(key, 9)

        def init(k, shape, fan_in):
            bound = 1.0 / np.sqrt(fan_in)
            return jax.random.uniform(k, shape, jnp.float32, -bound, bound)
        x = jax.random.normal(ks[0], (16, 512, D_MODEL), dtype=jnp.float32)
        Win = init(ks[1], (D_MODEL, M), D_MODEL)
        bin_ = init(ks[2], (M,), D_MODEL)
        W1 = init(ks[3], (M, INNER), 1)
        b1 = init(ks[4], (M, INNER), 1)
        W2 = init(ks[5], (M, INNER), INNER)
        b2 = init(ks[6], (M,), INNER)
        Wout = init(ks[7], (M, D_MODEL), M)
        bout = init(ks[8], (D_MODEL,), M)
        return {'x': x, 'Win': Win, 'bin_': bin_, 'W1': W1, 'b1': b1, 'W2': W2, 'b2': b2, 'Wout': Wout, 'bout': bout}
    _L0_ffn_in = _L0_ffn_setup()

    def _L1_attn_setup():
        import jax, jax.numpy as jnp
        import numpy as np
        H = 16
        BASE = 10000.0
        EPS = 1e-06
        key = jax.random.key(seed)
        ks = jax.random.split(key, 8)
        b, n, d = (2, 256, 128)
        hd = d // H
        s = 1.0 / np.sqrt(d)
        x = jax.random.normal(ks[0], (b, n, d), jnp.float32)
        wq = jax.random.normal(ks[1], (d, d), jnp.float32) * s
        wk = jax.random.normal(ks[2], (d, d), jnp.float32) * s
        wv = jax.random.normal(ks[3], (d, d), jnp.float32) * s
        wo = jax.random.normal(ks[4], (d, d), jnp.float32) * s
        wg1 = jax.random.normal(ks[5], (d, hd), jnp.float32) * s
        wg2 = jax.random.normal(ks[6], (hd, d), jnp.float32) * (1.0 / np.sqrt(hd))
        norm_w = jnp.ones((d,), jnp.float32)
        return {'x': x, 'wq': wq, 'wk': wk, 'wv': wv, 'wo': wo, 'wg1': wg1, 'wg2': wg2, 'norm_w': norm_w}
    _L1_attn_in = _L1_attn_setup()

    def _L1_ffn_setup():
        import jax, jax.numpy as jnp
        import numpy as np
        import math
        D_IN = 128
        FEATURES = (512, 512, 128)
        BATCH, SEQ = (8, 256)

        def _conn_dense(kernel_bool, x):
            w = jnp.where(kernel_bool, jnp.float32(1.0), jnp.float32(-1.0))
            return x @ w
        key = jax.random.key(seed)
        kx, kk0, kk1, kk2 = jax.random.split(key, 4)
        x = jax.random.normal(kx, (BATCH, SEQ, D_IN), dtype=jnp.float32)
        k0 = jax.random.randint(kk0, (2 * D_IN, FEATURES[0]), 0, 2).astype(jnp.bool_)
        k1 = jax.random.randint(kk1, (FEATURES[0], FEATURES[1]), 0, 2).astype(jnp.bool_)
        k2 = jax.random.randint(kk2, (FEATURES[1], FEATURES[2]), 0, 2).astype(jnp.bool_)
        s0 = jnp.asarray(1.0 / math.sqrt(2 * D_IN), dtype=jnp.float32)
        s1 = jnp.asarray(1.0 / math.sqrt(FEATURES[0]), dtype=jnp.float32)
        s2 = jnp.asarray(1.0 / math.sqrt(FEATURES[1]), dtype=jnp.float32)
        return {'x': x, 'k0': k0, 'k1': k1, 'k2': k2, 's0': s0, 's1': s1, 's2': s2}
    _L1_ffn_in = _L1_ffn_setup()

    def _L2_attn_setup():
        import jax, jax.numpy as jnp
        import numpy as np
        S, B, F = (256, 2, 128)
        H, D = (16, 64)
        P = H * D
        key = jax.random.key(seed)
        k1, k2, k3 = jax.random.split(key, 3)
        return {'src': jax.random.normal(k1, (S, B, F), dtype=jnp.float32), 'in_proj_weight': jax.random.normal(k2, (3 * P, F), dtype=jnp.float32) * (1.0 / np.sqrt(F)), 'in_proj_bias': jnp.zeros((3 * P,), dtype=jnp.float32), 'out_proj_weight': jax.random.normal(k3, (F, P), dtype=jnp.float32) * (1.0 / np.sqrt(P)), 'out_proj_bias': jnp.zeros((F,), dtype=jnp.float32)}
    _L2_attn_in = _L2_attn_setup()

    def _L2_ffn_setup():
        import jax, jax.numpy as jnp
        import numpy as np
        H = 128
        I = 64
        E = 64
        G = 8
        TOPK_GROUP = 4
        K = 8
        I_SH = 128
        SCALE = 2.5

        def _route(x, router_w, e_bias):
            T = x.shape[0]
            scores = jax.nn.sigmoid(x.astype(jnp.float32) @ router_w.T.astype(jnp.float32))
            sfc = jax.lax.stop_gradient(scores) + e_bias[None, :]
            group_scores = jax.lax.top_k(sfc.reshape(T, G, E // G), 2)[0].sum(-1)
            _, gidx = jax.lax.top_k(group_scores, TOPK_GROUP)
            gmask = jax.nn.one_hot(gidx, G, dtype=sfc.dtype).sum(1)
            smask = jnp.repeat(gmask, E // G, axis=1)
            masked = jnp.where(smask > 0, sfc, 0.0)
            _, topk_idx = jax.lax.top_k(masked, K)
            w = jnp.take_along_axis(scores, topk_idx, axis=1)
            w = w / (w.sum(-1, keepdims=True) + 1e-20)
            return (topk_idx, w * SCALE)
        key = jax.random.key(seed)
        ks = jax.random.split(key, 9)
        s = 0.02
        return {'hidden_states': jax.random.normal(ks[0], (2, 128, H), jnp.float32), 'router_w': jax.random.normal(ks[1], (E, H), jnp.float32) * s, 'e_bias': jnp.zeros((E,), jnp.float32), 'Wg': jax.random.normal(ks[2], (E, H, I), jnp.float32) * s, 'Wu': jax.random.normal(ks[3], (E, H, I), jnp.float32) * s, 'Wd': jax.random.normal(ks[4], (E, I, H), jnp.float32) * s, 'SWg': jax.random.normal(ks[5], (H, I_SH), jnp.float32) * s, 'SWu': jax.random.normal(ks[6], (H, I_SH), jnp.float32) * s, 'SWd': jax.random.normal(ks[7], (I_SH, H), jnp.float32) * s}
    _L2_ffn_in = _L2_ffn_setup()

    def _L3_attn_setup():
        import jax, jax.numpy as jnp
        import numpy as np
        D_MODEL = 128
        D_STATE = 16
        D_CONV = 4
        EXPAND = 2
        D_INNER = EXPAND * D_MODEL
        BATCH = 2
        SEQ = 256
        key = jax.random.key(seed)
        ks = jax.random.split(key, 7)
        s = 0.02
        x = jax.random.normal(ks[0], (BATCH, SEQ, D_MODEL), jnp.float32)
        in_proj_w = jax.random.normal(ks[1], (2 * D_INNER, D_MODEL), jnp.float32) * s
        conv_w = jax.random.normal(ks[2], (D_INNER, 1, D_CONV), jnp.float32) * s
        conv_b = jnp.zeros((D_INNER,), jnp.float32)
        x_proj_w = jax.random.normal(ks[3], (2 * D_STATE, D_INNER), jnp.float32) * s
        dt_proj_w = jax.random.normal(ks[4], (D_INNER, D_INNER), jnp.float32) * s
        dt_proj_b = jnp.zeros((D_INNER,), jnp.float32)
        A_log = jnp.log(jnp.tile(jnp.arange(1, D_STATE + 1, dtype=jnp.float32), (D_INNER, 1)))
        D_param = jnp.ones((D_INNER,), jnp.float32)
        out_proj_w = jax.random.normal(ks[5], (D_MODEL, D_INNER), jnp.float32) * s
        return {'x': x, 'in_proj_w': in_proj_w, 'conv_w': conv_w, 'conv_b': conv_b, 'x_proj_w': x_proj_w, 'dt_proj_w': dt_proj_w, 'dt_proj_b': dt_proj_b, 'A_log': A_log, 'D_param': D_param, 'out_proj_w': out_proj_w}
    _L3_attn_in = _L3_attn_setup()

    def _L3_ffn_setup():
        import jax, jax.numpy as jnp
        import numpy as np
        DIM = 128
        INTER = 64
        E = 16
        TOPK = 4
        N_GROUPS = 4
        TOPK_GROUPS = 2
        ROUTE_SCALE = 1.0
        INIT_STD = 0.02
        B, S = (2, 128)
        key = jax.random.key(seed)
        ks = jax.random.split(key, 8)
        return {'x': jax.random.normal(ks[0], (B, S, DIM), jnp.float32), 'gate_w': jax.random.normal(ks[1], (E, DIM), jnp.float32) * INIT_STD, 'gate_bias': jnp.zeros((E,), jnp.float32), 'w1': jax.random.normal(ks[2], (E, INTER, DIM), jnp.float32) * INIT_STD, 'w2': jax.random.normal(ks[3], (E, DIM, INTER), jnp.float32) * INIT_STD, 'w3': jax.random.normal(ks[4], (E, INTER, DIM), jnp.float32) * INIT_STD, 'ws1': jax.random.normal(ks[5], (INTER, DIM), jnp.float32) * INIT_STD, 'ws2': jax.random.normal(ks[6], (DIM, INTER), jnp.float32) * INIT_STD, 'ws3': jax.random.normal(ks[7], (INTER, DIM), jnp.float32) * INIT_STD}
    _L3_ffn_in = _L3_ffn_setup()
    _d = {'L0_attn_x': _L0_attn_in['x'], 'L0_attn_ln1_w': _L0_attn_in['ln1_w'], 'L0_attn_ln1_b': _L0_attn_in['ln1_b'], 'L0_attn_ln2_w': _L0_attn_in['ln2_w'], 'L0_attn_ln2_b': _L0_attn_in['ln2_b'], 'L0_attn_time_decay': _L0_attn_in['time_decay'], 'L0_attn_time_first': _L0_attn_in['time_first'], 'L0_attn_tmk': _L0_attn_in['tmk'], 'L0_attn_tmv': _L0_attn_in['tmv'], 'L0_attn_tmr': _L0_attn_in['tmr'], 'L0_attn_att_kw': _L0_attn_in['att_kw'], 'L0_attn_att_vw': _L0_attn_in['att_vw'], 'L0_attn_att_rw': _L0_attn_in['att_rw'], 'L0_attn_att_ow': _L0_attn_in['att_ow'], 'L0_attn_f_tmk': _L0_attn_in['f_tmk'], 'L0_attn_f_tmr': _L0_attn_in['f_tmr'], 'L0_attn_f_kw': _L0_attn_in['f_kw'], 'L0_attn_f_rw': _L0_attn_in['f_rw'], 'L0_attn_f_vw': _L0_attn_in['f_vw'], 'L0_ffn_Win': _L0_ffn_in['Win'], 'L0_ffn_bin_': _L0_ffn_in['bin_'], 'L0_ffn_W1': _L0_ffn_in['W1'], 'L0_ffn_b1': _L0_ffn_in['b1'], 'L0_ffn_W2': _L0_ffn_in['W2'], 'L0_ffn_b2': _L0_ffn_in['b2'], 'L0_ffn_Wout': _L0_ffn_in['Wout'], 'L0_ffn_bout': _L0_ffn_in['bout'], 'L1_attn_wq': _L1_attn_in['wq'], 'L1_attn_wk': _L1_attn_in['wk'], 'L1_attn_wv': _L1_attn_in['wv'], 'L1_attn_wo': _L1_attn_in['wo'], 'L1_attn_wg1': _L1_attn_in['wg1'], 'L1_attn_wg2': _L1_attn_in['wg2'], 'L1_attn_norm_w': _L1_attn_in['norm_w'], 'L1_ffn_k0': _L1_ffn_in['k0'], 'L1_ffn_k1': _L1_ffn_in['k1'], 'L1_ffn_k2': _L1_ffn_in['k2'], 'L1_ffn_s0': _L1_ffn_in['s0'], 'L1_ffn_s1': _L1_ffn_in['s1'], 'L1_ffn_s2': _L1_ffn_in['s2'], 'L2_attn_in_proj_weight': _L2_attn_in['in_proj_weight'], 'L2_attn_in_proj_bias': _L2_attn_in['in_proj_bias'], 'L2_attn_out_proj_weight': _L2_attn_in['out_proj_weight'], 'L2_attn_out_proj_bias': _L2_attn_in['out_proj_bias'], 'L2_ffn_router_w': _L2_ffn_in['router_w'], 'L2_ffn_e_bias': _L2_ffn_in['e_bias'], 'L2_ffn_Wg': _L2_ffn_in['Wg'], 'L2_ffn_Wu': _L2_ffn_in['Wu'], 'L2_ffn_Wd': _L2_ffn_in['Wd'], 'L2_ffn_SWg': _L2_ffn_in['SWg'], 'L2_ffn_SWu': _L2_ffn_in['SWu'], 'L2_ffn_SWd': _L2_ffn_in['SWd'], 'L3_attn_in_proj_w': _L3_attn_in['in_proj_w'], 'L3_attn_conv_w': _L3_attn_in['conv_w'], 'L3_attn_conv_b': _L3_attn_in['conv_b'], 'L3_attn_x_proj_w': _L3_attn_in['x_proj_w'], 'L3_attn_dt_proj_w': _L3_attn_in['dt_proj_w'], 'L3_attn_dt_proj_b': _L3_attn_in['dt_proj_b'], 'L3_attn_A_log': _L3_attn_in['A_log'], 'L3_attn_D_param': _L3_attn_in['D_param'], 'L3_attn_out_proj_w': _L3_attn_in['out_proj_w'], 'L3_ffn_gate_w': _L3_ffn_in['gate_w'], 'L3_ffn_gate_bias': _L3_ffn_in['gate_bias'], 'L3_ffn_w1': _L3_ffn_in['w1'], 'L3_ffn_w2': _L3_ffn_in['w2'], 'L3_ffn_w3': _L3_ffn_in['w3'], 'L3_ffn_ws1': _L3_ffn_in['ws1'], 'L3_ffn_ws2': _L3_ffn_in['ws2'], 'L3_ffn_ws3': _L3_ffn_in['ws3']}
    _x0 = _d['L0_attn_x']
    _d['L0_attn_x'] = jax.random.normal(jax.random.fold_in(jax.random.key(seed), 1), (1, 2048, 128), dtype=_x0.dtype)
    del _x0
    return _d

def reference(L0_attn_x, L0_attn_ln1_w, L0_attn_ln1_b, L0_attn_ln2_w, L0_attn_ln2_b, L0_attn_time_decay, L0_attn_time_first, L0_attn_tmk, L0_attn_tmv, L0_attn_tmr, L0_attn_att_kw, L0_attn_att_vw, L0_attn_att_rw, L0_attn_att_ow, L0_attn_f_tmk, L0_attn_f_tmr, L0_attn_f_kw, L0_attn_f_rw, L0_attn_f_vw, L0_ffn_Win, L0_ffn_bin_, L0_ffn_W1, L0_ffn_b1, L0_ffn_W2, L0_ffn_b2, L0_ffn_Wout, L0_ffn_bout, L1_attn_wq, L1_attn_wk, L1_attn_wv, L1_attn_wo, L1_attn_wg1, L1_attn_wg2, L1_attn_norm_w, L1_ffn_k0, L1_ffn_k1, L1_ffn_k2, L1_ffn_s0, L1_ffn_s1, L1_ffn_s2, L2_attn_in_proj_weight, L2_attn_in_proj_bias, L2_attn_out_proj_weight, L2_attn_out_proj_bias, L2_ffn_router_w, L2_ffn_e_bias, L2_ffn_Wg, L2_ffn_Wu, L2_ffn_Wd, L2_ffn_SWg, L2_ffn_SWu, L2_ffn_SWd, L3_attn_in_proj_w, L3_attn_conv_w, L3_attn_conv_b, L3_attn_x_proj_w, L3_attn_dt_proj_w, L3_attn_dt_proj_b, L3_attn_A_log, L3_attn_D_param, L3_attn_out_proj_w, L3_ffn_gate_w, L3_ffn_gate_bias, L3_ffn_w1, L3_ffn_w2, L3_ffn_w3, L3_ffn_ws1, L3_ffn_ws2, L3_ffn_ws3):

    def _L0_attn_ref(x, ln1_w, ln1_b, ln2_w, ln2_b, time_decay, time_first, tmk, tmv, tmr, att_kw, att_vw, att_rw, att_ow, f_tmk, f_tmr, f_kw, f_rw, f_vw):
        import jax, jax.numpy as jnp
        import numpy as np
        B, T, C, FFN, N_LAYER, LAYER_ID = (4, 256, 128, 512, 24, 1)
        EPS = 1e-05

        def _ln(z, g, b):
            m = jnp.mean(z, axis=-1, keepdims=True)
            v = jnp.mean(jnp.square(z - m), axis=-1, keepdims=True)
            return (z - m) * jax.lax.rsqrt(v + EPS) * g + b

        def _shift(z):
            return jnp.pad(z, ((0, 0), (1, 0), (0, 0)))[:, :-1]

        def _wkv(time_decay, u, k, v):
            w = -jnp.exp(time_decay)
            kt = jnp.moveaxis(k, 1, 0)
            vt = jnp.moveaxis(v, 1, 0)
            aa = jnp.zeros_like(kt[0])
            bb = jnp.zeros_like(kt[0])
            pp = jnp.full_like(kt[0], -1e+38)

            def step(carry, kv):
                aa, bb, pp = carry
                kk, vv = kv
                ww = u + kk
                p = jnp.maximum(pp, ww)
                e1 = jnp.exp(pp - p)
                e2 = jnp.exp(ww - p)
                out = (e1 * aa + e2 * vv) / (e1 * bb + e2)
                ww2 = pp + w
                p2 = jnp.maximum(ww2, kk)
                e1b = jnp.exp(ww2 - p2)
                e2b = jnp.exp(kk - p2)
                return ((e1b * aa + e2b * vv, e1b * bb + e2b, p2), out)
            _, out = jax.lax.scan(step, (aa, bb, pp), (kt, vt))
            return jnp.moveaxis(out, 0, 1)
        h = _ln(x, ln1_w, ln1_b)
        hx = _shift(h)
        xk = h * tmk + hx * (1.0 - tmk)
        xv = h * tmv + hx * (1.0 - tmv)
        xr = h * tmr + hx * (1.0 - tmr)
        k = jnp.einsum('btc,dc->btd', xk, att_kw)
        v = jnp.einsum('btc,dc->btd', xv, att_vw)
        sr = jax.nn.sigmoid(jnp.einsum('btc,dc->btd', xr, att_rw))
        rwkv = sr * _wkv(time_decay, time_first, k, v)
        x = x + jnp.einsum('btd,cd->btc', rwkv, att_ow)
        h = _ln(x, ln2_w, ln2_b)
        hx = _shift(h)
        xk = h * f_tmk + hx * (1.0 - f_tmk)
        xr = h * f_tmr + hx * (1.0 - f_tmr)
        kk = jnp.square(jax.nn.relu(jnp.einsum('btc,fc->btf', xk, f_kw)))
        kv = jnp.einsum('btf,cf->btc', kk, f_vw)
        x = x + jax.nn.sigmoid(jnp.einsum('btc,dc->btd', xr, f_rw)) * kv
        return x

    def _L0_ffn_ref(x, Win, bin_, W1, b1, W2, b2, Wout, bout):
        import jax, jax.numpy as jnp
        import numpy as np
        D_MODEL = 128
        M = 64
        INNER = 16
        s = jnp.einsum('btd,dm->btm', x, Win) + bin_
        h = jax.nn.relu(s[..., None] * W1 + b1)
        g = jnp.einsum('btmh,mh->btm', h, W2) + b2
        out = jnp.einsum('btm,md->btd', g, Wout) + bout
        return out

    def _L1_attn_ref(x, wq, wk, wv, wo, wg1, wg2, norm_w):
        import jax, jax.numpy as jnp
        import numpy as np
        H = 16
        BASE = 10000.0
        EPS = 1e-06
        b, n, d = x.shape
        hd = d // H
        q = jax.nn.silu(x @ wq).reshape(b, n, H, hd)
        k = (x @ wk).reshape(b, n, H, hd)
        v = (x @ wv).reshape(b, n, H, hd)
        f = jnp.concatenate([jnp.zeros((b, 1, H, hd), x.dtype), k], axis=1)
        z = jax.lax.cumlogsumexp(f, axis=1)
        log_f = z[:, :-1] - z[:, 1:]
        k = jnp.exp(k - z[:, 1:])
        theta = BASE ** (-2.0 / (H * hd) * jnp.arange(H * hd, dtype=x.dtype))
        theta = theta.reshape(H, hd)
        ang = jnp.arange(n, dtype=x.dtype)[:, None, None] * theta[None]
        c, s_ = (jnp.cos(ang), jnp.sin(ang))
        q = jnp.concatenate([q * c, q * s_], axis=-1)
        k = jnp.concatenate([k * c, k * s_], axis=-1)
        ld = jnp.concatenate([log_f, log_f], axis=-1)

        def step(S, inp):
            qt, kt, vt, lt = inp
            S = jnp.exp(lt)[..., None] * S + kt[..., None] * vt[..., None, :]
            o = jnp.einsum('bhe,bhev->bhv', qt, S)
            return (S, o)
        S0 = jnp.zeros((b, H, 2 * hd, hd), x.dtype)
        seq = (jnp.moveaxis(q, 1, 0), jnp.moveaxis(k, 1, 0), jnp.moveaxis(v, 1, 0), jnp.moveaxis(ld, 1, 0))
        _, o = jax.lax.scan(step, S0, seq)
        o = jnp.moveaxis(o, 0, 1).reshape(b, n, d)
        gate = x @ wg1 @ wg2
        g = o * jax.nn.sigmoid(gate)
        gg = g.reshape(b, n, H, hd)
        rms = jnp.sqrt(jnp.mean(gg * gg, axis=-1, keepdims=True) + EPS)
        normed = (gg / rms).reshape(b, n, d) * norm_w
        return normed @ wo

    def _L1_ffn_ref(x, k0, k1, k2, s0, s1, s2):
        import jax, jax.numpy as jnp
        import numpy as np
        import math
        D_IN = 128
        FEATURES = (512, 512, 128)
        BATCH, SEQ = (8, 256)

        def _conn_dense(kernel_bool, x):
            w = jnp.where(kernel_bool, jnp.float32(1.0), jnp.float32(-1.0))
            return x @ w
        h = jnp.concatenate([x, -x], axis=-1)
        h = s0 * _conn_dense(k0, h)
        h = jax.nn.relu(h) * 2
        h = s1 * _conn_dense(k1, h)
        h = jax.nn.relu(h) * 2
        h = s2 * _conn_dense(k2, h)
        return h

    def _L2_attn_ref(src, in_proj_weight, in_proj_bias, out_proj_weight, out_proj_bias):
        import jax, jax.numpy as jnp
        import numpy as np
        S, B, F = (256, 2, 128)
        H, D = (16, 64)
        P = H * D
        s, b, f = src.shape
        h, d = (H, D)
        qkv = jnp.einsum('sbf,pf->sbp', src, in_proj_weight) + in_proj_bias
        q, k, v = jnp.split(qkv, 3, axis=-1)

        def to_heads(x):
            return jnp.swapaxes(x.reshape(s, b * h, d), 0, 1)
        q = to_heads(q) / np.sqrt(d)
        k = to_heads(k)
        v = to_heads(v)
        attn = jnp.einsum('nsd,ntd->nst', q, k)
        attn = jax.nn.softmax(attn, axis=-1)
        out = jnp.einsum('nst,ntd->nsd', attn, v)
        out = jnp.swapaxes(out, 0, 1).reshape(s * b, h * d)
        out = out @ out_proj_weight.T + out_proj_bias
        return out.reshape(s, b, f)

    def _L2_ffn_ref(hidden_states, router_w, e_bias, Wg, Wu, Wd, SWg, SWu, SWd):
        import jax, jax.numpy as jnp
        import numpy as np
        H = 128
        I = 64
        E = 64
        G = 8
        TOPK_GROUP = 4
        K = 8
        I_SH = 128
        SCALE = 2.5

        def _route(x, router_w, e_bias):
            T = x.shape[0]
            scores = jax.nn.sigmoid(x.astype(jnp.float32) @ router_w.T.astype(jnp.float32))
            sfc = jax.lax.stop_gradient(scores) + e_bias[None, :]
            group_scores = jax.lax.top_k(sfc.reshape(T, G, E // G), 2)[0].sum(-1)
            _, gidx = jax.lax.top_k(group_scores, TOPK_GROUP)
            gmask = jax.nn.one_hot(gidx, G, dtype=sfc.dtype).sum(1)
            smask = jnp.repeat(gmask, E // G, axis=1)
            masked = jnp.where(smask > 0, sfc, 0.0)
            _, topk_idx = jax.lax.top_k(masked, K)
            w = jnp.take_along_axis(scores, topk_idx, axis=1)
            w = w / (w.sum(-1, keepdims=True) + 1e-20)
            return (topk_idx, w * SCALE)
        orig_shape = hidden_states.shape
        x = hidden_states.reshape(-1, orig_shape[-1])
        T = x.shape[0]
        topk_idx, topk_w = _route(x, router_w, e_bias)
        coef = jnp.zeros((T, E), topk_w.dtype).at[jnp.arange(T)[:, None], topk_idx].add(topk_w)
        g = jnp.einsum('th,ehi->tei', x, Wg)
        u = jnp.einsum('th,ehi->tei', x, Wu)
        h = jax.nn.silu(g) * u * coef[:, :, None]
        moe_out = jnp.einsum('tei,eih->th', h, Wd)
        shared = jax.nn.silu(x @ SWg) * (x @ SWu) @ SWd
        return (moe_out + shared).reshape(orig_shape)

    def _L3_attn_ref(x, in_proj_w, conv_w, conv_b, x_proj_w, dt_proj_w, dt_proj_b, A_log, D_param, out_proj_w):
        import jax, jax.numpy as jnp
        import numpy as np
        D_MODEL = 128
        D_STATE = 16
        D_CONV = 4
        EXPAND = 2
        D_INNER = EXPAND * D_MODEL
        BATCH = 2
        SEQ = 256
        B, L, _ = x.shape
        xz = x @ in_proj_w.T
        x_ssm, z = jnp.split(xz, 2, axis=-1)
        xc = jnp.transpose(x_ssm, (0, 2, 1))
        xc = jnp.pad(xc, ((0, 0), (0, 0), (D_CONV - 1, 0)))
        xc = jax.lax.conv_general_dilated(xc, conv_w, window_strides=(1,), padding='VALID', dimension_numbers=('NCH', 'OIH', 'NCH'), feature_group_count=D_INNER)
        xc = xc + conv_b[None, :, None]
        x_act = jax.nn.silu(jnp.transpose(xc, (0, 2, 1)))
        delta = jax.nn.softplus(x_act @ dt_proj_w.T + dt_proj_b)
        bc = x_act @ x_proj_w.T
        B_p, C_p = jnp.split(bc, 2, axis=-1)
        A = -jnp.exp(A_log)

        def step(h, inp):
            u_i, d_i, B_i, C_i = inp
            dA = jnp.exp(d_i[..., None] * A)
            h = dA * h + (d_i * u_i)[..., None] * B_i[:, None, :]
            y = jnp.einsum('bdn,bn->bd', h, C_i)
            return (h, y)
        h0 = jnp.zeros((B, D_INNER, D_STATE), x.dtype)
        seq = (jnp.swapaxes(x_act, 0, 1), jnp.swapaxes(delta, 0, 1), jnp.swapaxes(B_p, 0, 1), jnp.swapaxes(C_p, 0, 1))
        _, ys = jax.lax.scan(step, h0, seq)
        y_ssm = jnp.swapaxes(ys, 0, 1) + x_act * D_param
        y = y_ssm * jax.nn.silu(z)
        return y @ out_proj_w.T

    def _L3_ffn_ref(x, gate_w, gate_bias, w1, w2, w3, ws1, ws2, ws3):
        import jax, jax.numpy as jnp
        import numpy as np
        DIM = 128
        INTER = 64
        E = 16
        TOPK = 4
        N_GROUPS = 4
        TOPK_GROUPS = 2
        ROUTE_SCALE = 1.0
        INIT_STD = 0.02
        B, S = (2, 128)
        Bx, Sx, D = x.shape
        T = Bx * Sx
        xf = x.reshape(T, D)
        scores = jax.nn.sigmoid(xf @ gate_w.T)
        original_scores = scores
        s = scores + gate_bias
        sg = s.reshape(T, N_GROUPS, E // N_GROUPS)
        group_scores = sg.max(axis=-1)
        _, gidx = jax.lax.top_k(group_scores, TOPK_GROUPS)
        keep = jnp.zeros((T, N_GROUPS), bool).at[jnp.arange(T)[:, None], gidx].set(True)
        s_masked = jnp.where(keep[:, :, None], sg, -jnp.inf).reshape(T, E)
        _, idx = jax.lax.top_k(s_masked, TOPK)
        weights = jnp.take_along_axis(original_scores, idx, axis=1) * ROUTE_SCALE
        comb = jnp.zeros((T, E), x.dtype).at[jnp.arange(T)[:, None], idx].add(weights)
        h1 = jnp.einsum('td,eid->tei', xf, w1)
        h3 = jnp.einsum('td,eid->tei', xf, w3)
        h = jax.nn.silu(h1) * h3
        y = jnp.einsum('tei,edi,te->td', h, w2, comb)
        z = jax.nn.silu(xf @ ws1.T) * (xf @ ws3.T) @ ws2.T
        return (y + z).reshape(Bx, Sx, D)
    x = L0_attn_x
    x = x + _layernorm(_L0_attn_ref(_layernorm(x, axis=-1), L0_attn_ln1_w, L0_attn_ln1_b, L0_attn_ln2_w, L0_attn_ln2_b, L0_attn_time_decay, L0_attn_time_first, L0_attn_tmk, L0_attn_tmv, L0_attn_tmr, L0_attn_att_kw, L0_attn_att_vw, L0_attn_att_rw, L0_attn_att_ow, L0_attn_f_tmk, L0_attn_f_tmr, L0_attn_f_kw, L0_attn_f_rw, L0_attn_f_vw), axis=-1)
    x = x + _layernorm(_L0_ffn_ref(_layernorm(x, axis=-1), L0_ffn_Win, L0_ffn_bin_, L0_ffn_W1, L0_ffn_b1, L0_ffn_W2, L0_ffn_b2, L0_ffn_Wout, L0_ffn_bout), axis=-1)
    x = x + _layernorm(_L1_attn_ref(_layernorm(x, axis=-1), L1_attn_wq, L1_attn_wk, L1_attn_wv, L1_attn_wo, L1_attn_wg1, L1_attn_wg2, L1_attn_norm_w), axis=-1)
    x = x + _layernorm(_L1_ffn_ref(_layernorm(x, axis=-1), L1_ffn_k0, L1_ffn_k1, L1_ffn_k2, L1_ffn_s0, L1_ffn_s1, L1_ffn_s2), axis=-1)
    x = x + _layernorm(_L2_attn_ref(_layernorm(x, axis=-1), L2_attn_in_proj_weight, L2_attn_in_proj_bias, L2_attn_out_proj_weight, L2_attn_out_proj_bias), axis=-1)
    x = x + _layernorm(_L2_ffn_ref(_layernorm(x, axis=-1), L2_ffn_router_w, L2_ffn_e_bias, L2_ffn_Wg, L2_ffn_Wu, L2_ffn_Wd, L2_ffn_SWg, L2_ffn_SWu, L2_ffn_SWd), axis=-1)
    x = x + _layernorm(_L3_attn_ref(_layernorm(x, axis=-1), L3_attn_in_proj_w, L3_attn_conv_w, L3_attn_conv_b, L3_attn_x_proj_w, L3_attn_dt_proj_w, L3_attn_dt_proj_b, L3_attn_A_log, L3_attn_D_param, L3_attn_out_proj_w), axis=-1)
    x = x + _layernorm(_L3_ffn_ref(_layernorm(x, axis=-1), L3_ffn_gate_w, L3_ffn_gate_bias, L3_ffn_w1, L3_ffn_w2, L3_ffn_w3, L3_ffn_ws1, L3_ffn_ws2, L3_ffn_ws3), axis=-1)
    return x

_drawn_inputs = setup_inputs


def setup_inputs(seed=0):
    import zlib

    import numpy as np

    out = dict(_drawn_inputs(seed))
    spreads = {'L0_attn_ln1_w': (1.0, 0.6),
     'L0_attn_ln1_b': (0.0, 0.8),
     'L0_attn_ln2_w': (1.0, 0.6),
     'L0_attn_ln2_b': (0.0, 0.8),
     'L1_attn_norm_w': (1.0, 0.2),
     'L2_attn_in_proj_bias': (0.0, 0.1),
     'L2_attn_out_proj_bias': (0.0, 0.1),
     'L2_ffn_e_bias': (0.0, 0.1),
     'L3_attn_conv_b': (0.0, 0.1),
     'L3_attn_dt_proj_b': (0.0, 2.0),
     'L3_attn_D_param': (1.0, 0.2),
     'L3_ffn_gate_bias': (0.0, 0.1)}
    factors = {'L0_attn_time_decay': 3.031,
     'L0_attn_time_first': 8.0,
     'L0_attn_tmk': 8.0,
     'L0_attn_tmv': 4.266,
     'L0_attn_tmr': 8.0,
     'L0_attn_att_kw': 8.0,
     'L0_attn_att_rw': 8.0,
     'L0_attn_f_tmk': 4.129,
     'L0_attn_f_tmr': 8.0,
     'L0_attn_f_kw': 3.133,
     'L0_attn_f_rw': 7.772,
     'L0_attn_f_vw': 3.06,
     'L3_attn_x_proj_w': 27.594,
     'L3_attn_dt_proj_w': 64.0,
     'L3_attn_A_log': 64.0}
    for name, (base, spread) in spreads.items():
        noise = np.random.default_rng([zlib.crc32(name.encode()), seed]).standard_normal(out[name].shape)
        drawn = base * np.exp(spread * noise) if base else spread * noise
        out[name] = jnp.asarray(drawn.astype(out[name].dtype))
    for name, factor in factors.items():
        out[name] = (out[name] * factor).astype(out[name].dtype)
    return out
```

```python
from contextlib import ExitStack, contextmanager

import concourse.bass as bass
import numpy as np
from concourse import mybir

P = 128
T = 2048
N = 512
CHUNKS = T // N
TILES = N // P
PAD = 4
LEAD = 3
F32 = mybir.dt.float32
BF16 = mybir.dt.bfloat16
U8 = mybir.dt.uint8
ALU = mybir.AluOpType
ACT = mybir.ActivationFunctionType
AX_X = mybir.AxisListType.X
LAYERS = 8

NORMS = ["pre0", "ln1", "ln2", "post0", "pre1", "post1", "pre2", "rms", "post2", "pre3", "post3",
         "pre4", "post4", "pre5", "post5", "pre6", "post6", "pre7", "post7"]
NORM = {name: i for i, name in enumerate(NORMS)}
ACT_SQUARES = [n for n in NORMS if n.startswith("post") or n in ("ln2", "rms")]
POOL_SQUARES = [n for n in NORMS if n not in ACT_SQUARES]
BIG = 1e30

LAYOUT = [
    [("kw", 128), ("vw", 128), ("rw", 128), ("ow", 128), ("frw", 128), ("fkw", 512), ("fvw", 512),
     ("vec", 12)],
    [("win", 128), ("wout", 128), ("w1", 8), ("b1", 8), ("w2", 8), ("bin", 1), ("b2", 1), ("bout", 1)],
    [("wq", 128), ("wk", 128), ("wv", 1024), ("wg1", 8), ("wg2", 128), ("wo", 128), ("norm_w", 1),
     ("head_sum", 1024), ("head_mean", 128)],
    [("s", 3)],
    [("wv", 1024), ("wo", 1024), ("bv", 8), ("bo", 1)],
    [("router", 64), ("bias", 64), ("before", 64)],
    [("wx", 256), ("conv", 1024), ("wz", 256), ("wbc", 192), ("wdt", 512), ("wout", 256),
     ("conv_b", 2), ("dt_b", 2), ("a_log", 32), ("d", 2)],
    [("router", 16), ("bias", 16), ("before", 64)],
]
AT = []
for _cols in LAYOUT:
    _at, _o = {}, 0
    for _name, _w in _cols:
        _at[_name] = (_o, _o + _w)
        _o += _w
    AT.append(_at)
WIDTH = [sum(w for _, w in cols) for cols in LAYOUT]
PAIR = 3 * 128
DERIVED = 1024
ARENA = [4 * 1024, 4 * 1024]


def cols(c, off=0, n=N):
    return bass.ds(c * N + off, n) if not isinstance(c, int) else slice(c * N + off, c * N + off + n)


class Chain:

    def __init__(self, eng, sem):
        self.eng, self.sem, self.n, self.reg = eng, sem, 0, 0

    def __call__(self, ins):
        ins.then_inc(self.sem, 1)
        self.n += 1

    def wait(self):
        self.eng.wait_ge(self.sem, self.reg + self.n)

    @contextmanager
    def each(self, count, per):
        start, reg = self.n, self.reg
        with self.eng.Fori(0, count) as i:
            self.reg = reg + i * per
            yield i
        assert self.n - start == per, (self.n - start, per)
        self.reg = reg
        self.n = start + count * per


def hold(eng, sem, value):
    if not isinstance(value, int) or value > 0:
        eng.wait_ge(sem, value)
        if not isinstance(value, int):
            eng.nop(nofuse=True)


def at_least(eng, sem, value):
    if not isinstance(value, int) or value > 0:
        eng.wait_ge(sem, value)


def sandwich(nc, x, out, weights, bools, moe0, moe1, consts, selectors, rope):
    ctx = ExitStack()
    with ctx:
        def sb(name, shape, dt=F32):
            return ctx.enter_context(nc.sbuf_tensor(name, shape, dt))

        names = """w_loaded bools_loaded sel_loaded consts_loaded x_loaded rope_loaded pair_loaded0 pair_loaded1
            out_stored y_ready x_ready h_ready centred sq_act sq_pool var_ready rstd_ready
            dve_chain act_chain pool_chain zeroed raw_ready
            h1_ready d_ready mix_ready k_bank v_bank r_bank kv_ready sr_ready pp_ready d12_ready
            p_ready d34_ready eb_ready ee_ready den_ready rd_ready rw_ready decay_ready ow_bank x1_ready
            fr_bank fk_bank relu_ready kk_ready fv_bank sr2_ready
            nam_s_bank nam_relu nam_done nam_setup nam_bias_bank nam_bias
            q_bank2 k_bank2 g1_bank g2_bank k2_ready sigq_ready q_used g1_ready gate_ready
            m_ready md_ready me_ready s_ready rs_ready kcs_ready vb_bank vb_used st_ready
            qm_ready qm_used og_ready nrm_ready wo_bank setup2
            f_setup a1_bank a1_relu a2_bank a2_relu a3_bank
            comb_bank comb_ready l2_bank
            lg_bank lg_ready sc_bank parts_ready ct_bank ct_ready
            g_bank u_bank c_bank sg_ready t_ready hid_ready e_done
            conv_setup a_ready xa_bank xa_ready z_bank z_ready dt_bank dt_ready dl_ready du_ready bc_bank bcp_ready
            bb_bank cb_bank bs_ready da_ready db_ready hs_done hc_ready sum_done
            yt_ready yg_ready mo_bank sum_ready back_ready""".split()
        s = {n: ctx.enter_context(nc.semaphore(n)) for n in names}

        resid = sb("resid", [P, T])
        mean0 = sb("mean0", [P, T])
        normed = sb("normed", [P, LEAD + T + 1])
        y = sb("y", [P, T])
        sq = sb("sq", [P, T])
        rstd = sb("rstd", [P, T])
        tmp = sb("tmp", [P, T])
        g = sb("g", [P, 13, T + PAD])
        arena = [sb(f"arena{i}", [P, ARENA[i]]) for i in range(2)]
        kbool_words = arena[1][:, 3100:3100 + 896].bitcast(mybir.dt.uint32)
        kbool = arena[1][:, 3100:3100 + 896].bitcast(U8)
        const = sb("const", [P, 3 * 128])
        sel = sb("sel", [96, 48, 128], BF16)
        ident_bf = sb("ident_bf", [P, P], BF16)
        small = sb("small", [P, 64])
        carry = sb("carry", [P, 32])
        ps = ctx.enter_context(nc.psum_tensor("ps", [P, 8, N], F32))

        ident, centring, averaging = (const[:, i * 128:(i + 1) * 128] for i in range(3))
        sel_bc, sel_coef = sel[:, 0:32, :], sel[:, 32:48, :]

        def W(layer, name, a=0, b=None):
            lo, hi = AT[layer][name]
            return arena[layer % 2][:, lo + a:(hi if b is None else lo + b)]

        def derived(layer, a, b):
            return arena[layer % 2][:, WIDTH[layer] + a:WIDTH[layer] + b]

        def G(i, c, off=0, n=N):
            return g[:, i, cols(c, off, n)]

        def H(c):
            return normed[:, cols(c, LEAD)]

        nam_wout = [derived(1, j * 128, (j + 1) * 128) for j in range(8)]
        nam_b1, nam_bout = small[:, 0:8], small[:, 8:9]
        scales = small[:, 9:12]
        comb_bias = small[:, 12:13]
        one = small[:, 13:14]
        eps5, eps6 = small[:, 49:50], small[:, 50:51]
        ffn_w = arena[1][:, 16:16 + 3072]
        comb = derived(4, 0, 128)
        wo_normed = derived(2, 0, 128)
        neg_a = small[:, 16:48]
        diag_d = g[:, 12, 1536:1792].rearrange("p (i n) -> p i n", i=2)
        conv_w = derived(6, 0, 1024).rearrange("p (j n) -> p j n", j=4)
        sc_rows = g[:, 0, 0:N]
        coef_parts = g[:, 3, 0:384].bitcast(BF16).rearrange("p (a t r) -> p a t r", a=TILES, t=2)
        coef_rows = g[0:96, 4, 0:T].bitcast(BF16).rearrange("p (t n) -> p t n", t=2)
        bc_rows = g[0:96, 12, 0:1536].bitcast(BF16)
        pair_w = [g[:, 7, i * PAIR:(i + 1) * PAIR] for i in range(2)]

        x_tiles = x.rearrange("(c a p) f -> p c a f", a=TILES, p=P)
        out_tiles = out.rearrange("(c a p) f -> p c a f", a=TILES, p=P)
        x_in = g[:, 11:13, 0:1024]

        block = ctx.enter_context(nc.Block())

        @block.sync
        def _(sp):
            for c in range(CHUNKS):
                sp.dma_start(x_in[:, c // 2, (c % 2) * 512:(c % 2 + 1) * 512]
                             .rearrange("p (a f) -> p a f", a=TILES), x_tiles[:, c]).then_inc(s["x_loaded"], 16)
                if c == 0:
                    sp.dma_start(const[:, :], consts[:, :]).then_inc(s["consts_loaded"], 16)
            lo = 0
            for layer in range(LAYERS):
                if layer >= 2:
                    sp.wait_ge(s["y_ready"], CHUNKS * layer)
                sp.dma_start(arena[layer % 2][:, 0:WIDTH[layer]],
                             weights[:, lo:lo + WIDTH[layer]]).then_inc(s["w_loaded"], 16)
                sp.wait_ge(s["w_loaded"], 16 * (layer + 1))
                lo += WIDTH[layer]
                if layer == 3:
                    sp.dma_start(kbool_words, bools[:, :]).then_inc(s["bools_loaded"], 16)
                if layer == 4:
                    sp.dma_start(sel[:, :, :], selectors[:, :, :]).then_inc(s["sel_loaded"], 16)
                if layer == 2:
                    sp.dma_start(g[:, 10:12, 0:T], rope[:, :, :]).then_inc(s["rope_loaded"], 16)
                for moe_layer, dram, pairs, first in ((5, moe0, 32, 0), (7, moe1, 8, 33)):
                    if layer != moe_layer:
                        continue
                    if moe_layer == 7:
                        sp.wait_ge(s["yg_ready"], CHUNKS + 1)
                    sp.dma_start(pair_w[1], dram[0, :, :]).then_inc(s["pair_loaded1"], 16)
                    sp.dma_start(pair_w[0], dram[1, :, :]).then_inc(s["pair_loaded0"], 16)
                    with sp.Fori(0, pairs // 2 - 1) as i:
                        for k in (0, 1):
                            sp.wait_ge(s["e_done"], CHUNKS * (first + 1 + k) + i * 2 * CHUNKS)
                            sp.dma_start(pair_w[1 - k], dram[bass.ds(2 * i + 2 + k, 1), :, :]
                                         .rearrange("a p n -> p (a n)"))\
                              .then_inc(s["pair_loaded1" if k == 0 else "pair_loaded0"], 16)
                    sp.wait_ge(s["e_done"], CHUNKS * (first + pairs - 1))
                    sp.dma_start(pair_w[1], dram[pairs, :, :]).then_inc(s["pair_loaded1"], 16)
            for c in range(CHUNKS):
                sp.wait_ge(s["back_ready"], c + 1)
                sp.dma_start(out_tiles[:, c], g[:, 10, cols(c)].rearrange("p (a f) -> p a f", a=TILES))\
                  .then_inc(s["out_stored"], 16)
            sp.wait_ge(s["out_stored"], 16 * CHUNKS)

        @block.tensor
        def _(pe):
            def mm(o, lhsT, rhs, start=True, stop=True, **kw):
                return nc.tensor.matmul(o, lhsT, rhs, start=start, stop=stop, **kw)

            def centre(boundary, src, bank, ready="y_ready"):
                for c in range(CHUNKS):
                    pe.wait_ge(s[ready], boundary * CHUNKS + c + 1)
                    mm(ps[:, bank + c, :], centring, src(c)).then_inc(s["centred"], 1)

            def variance(name, bank=4, matrix=averaging):
                by = "sq_act" if name in ACT_SQUARES else "sq_pool"
                k = (ACT_SQUARES if name in ACT_SQUARES else POOL_SQUARES).index(name)
                for c in range(CHUNKS):
                    pe.wait_ge(s[by], k * CHUNKS + c + 1)
                    mm(ps[:, bank + c, :], matrix, sq[:, cols(c)]).then_inc(s["var_ready"], 1)

            def boundary(layer):
                centre(layer + 1, lambda c: y[:, cols(c)], 0)
                variance(f"post{layer}")
                if layer + 1 < LAYERS:
                    variance(f"pre{layer + 1}")

            def h(layer, c):
                pe.wait_ge(s["h_ready"], layer * CHUNKS + c + 1)

            pe.wait_ge(s["consts_loaded"], 16)
            for c in range(CHUNKS):
                pe.wait_ge(s["x_loaded"], 16 * CHUNKS)
                for a in range(TILES):
                    last = nc.tensor.transpose(ps[:, c, a * P:(a + 1) * P],
                                               x_in[:, c // 2, (c % 2) * 512 + a * P:(c % 2) * 512 + (a + 1) * P],
                                               ident)
                last.then_inc(s["raw_ready"], 1)
            centre(0, lambda c: y[:, cols(c)], 4)
            variance("pre0", 0)
            variance("ln1", 0)

            pe.wait_ge(s["w_loaded"], 16)
            for c in range(CHUNKS):
                pe.wait_ge(s["mix_ready"], c + 1)
                mm(ps[:, c, :], W(0, "kw"), G(2, c)).then_inc(s["k_bank"], 1)
                mm(ps[:, 4 + c, :], W(0, "vw"), G(3, c)).then_inc(s["v_bank"], 1)
            for c in range(CHUNKS):
                pe.wait_ge(s["kv_ready"], c + 1)
                mm(ps[:, c, :], W(0, "rw"), G(4, c)).then_inc(s["r_bank"], 1)
            for c in range(CHUNKS):
                pe.wait_ge(s["rw_ready"], c + 1)
                mm(ps[:, c, :], W(0, "ow"), G(4, c)).then_inc(s["ow_bank"], 1)
            for c in range(CHUNKS):
                pe.wait_ge(s["x1_ready"], c + 1)
                mm(ps[:, 4 + c, :], centring, G(5, c)).then_inc(s["centred"], 1)
            variance("ln2", 0)
            for c in range(CHUNKS):
                pe.wait_ge(s["mix_ready"], CHUNKS + c + 1)
                mm(ps[:, c, :], W(0, "frw"), G(4, c)).then_inc(s["fr_bank"], 1)
            pe.wait_ge(s["sr2_ready"], CHUNKS)
            for c in range(CHUNKS):
                pe.wait_ge(s["relu_ready"], 4 * c)
                for m in range(4):
                    mm(ps[:, m, :], W(0, "fkw", m * 128, m * 128 + 128), G(2, c)).then_inc(s["fk_bank"], 1)
                for m in range(4):
                    pe.wait_ge(s["kk_ready"], 4 * c + m + 1)
                    last = mm(ps[:, 4 + c, :], W(0, "fvw", m * 128, m * 128 + 128),
                              g[:, 7, m * N:(m + 1) * N], m == 0, m == 3)
                last.then_inc(s["fv_bank"], 1)
            boundary(0)

            if LAYERS > 1:
                pe.wait_ge(s["w_loaded"], 32)
                pe.wait_ge(s["nam_setup"], 1)
                h(1, 3)
                mm(ps[:, 7, 0:1], W(1, "wout")[0:64], W(1, "b2")[0:64]).then_inc(s["nam_bias_bank"], 1)
                for c in range(CHUNKS):
                    h(1, c)
                    mm(ps[:, c, :], W(1, "win"), H(c)).then_inc(s["nam_s_bank"], 1)
                pe.wait_ge(s["nam_bias"], 1)
                for c in range(CHUNKS):
                    for j in range(8):
                        pe.wait_ge(s["nam_relu"], 8 * c + j + 1)
                        last = mm(ps[:, 4 + c, :], nam_wout[j], g[:, j // 4, (j % 4) * N:(j % 4 + 1) * N],
                                  j == 0, j == 7)
                    last.then_inc(s["nam_done"], 1)
                boundary(1)

            if LAYERS > 2:
                pe.wait_ge(s["w_loaded"], 48)
                for c in range(CHUNKS):
                    h(2, c)
                    mm(ps[:, c, :], W(2, "wk"), H(c)).then_inc(s["k_bank2"], 1)
                    mm(ps[:, 4 + c, :], W(2, "wq"), H(c)).then_inc(s["q_bank2"], 1)
                for c in range(CHUNKS):
                    pe.wait_ge(s["k2_ready"], c + 1)
                    mm(ps[0:8, c, :], W(2, "wg1"), H(c)).then_inc(s["g1_bank"], 1)
                for c in range(CHUNKS):
                    pe.wait_ge(s["q_used"], c + 1)
                    pe.wait_ge(s["g1_ready"], c + 1)
                    mm(ps[:, 4 + c, :], W(2, "wg2")[0:8], tmp[0:8, cols(c)]).then_inc(s["g2_bank"], 1)
                pe.wait_ge(s["gate_ready"], CHUNKS)

                def spread_v(e, c):
                    pe.wait_ge(s["vb_used"], 8 * c + e + 1)
                    mm(ps[:, e % 2, :], W(2, "wv", e * 128, e * 128 + 128), H(c)).then_inc(s["vb_bank"], 1)

                pe.sem_inc(s["qm_used"], 2)
                with pe.Fori(0, CHUNKS) as c:
                    spread_v(0, c)
                    for e in range(8):
                        if e < 7:
                            spread_v(e + 1, c)
                        pe.wait_ge(s["qm_ready"], 8 * c + e + 3)
                        for r in range(2):
                            last = mm(ps[:, 4 + c, :], W(2, "head_sum", e * 128, e * 128 + 128),
                                      g[:, 2, (2 * (e % 2) + r) * N:(2 * (e % 2) + r + 1) * N],
                                      e == 0 and r == 0, e == 7 and r == 1)
                        last.then_inc(s["qm_used"], 1)
                variance("rms", 0, W(2, "head_mean"))
                pe.wait_ge(s["setup2"], 1)
                for c in range(CHUNKS):
                    pe.wait_ge(s["nrm_ready"], c + 1)
                    mm(ps[:, 4 + c, :], wo_normed, G(5, c)).then_inc(s["wo_bank"], 1)
                boundary(2)

            if LAYERS > 3:
                pe.wait_ge(s["f_setup"], 1)
                h(3, 3)
                for c in range(CHUNKS):
                    pe.wait_ge(s["a1_relu"], 4 * c)
                    pe.wait_ge(s["y_ready"], 4 * CHUNKS + c)
                    for m in range(4):
                        mm(ps[:, m, :], ffn_w[:, m * 128:m * 128 + 128], H(c)).then_inc(s["a1_bank"], 1)
                    pe.wait_ge(s["a2_relu"], 4 * c)
                    for m in range(4):
                        for k in range(4):
                            if m == 0:
                                pe.wait_ge(s["a1_relu"], 4 * c + k + 1)
                            last = mm(ps[:, 4 + m, :],
                                      ffn_w[:, 512 + k * 512 + m * 128:512 + k * 512 + m * 128 + 128],
                                      g[:, 0, k * N:(k + 1) * N], k == 0, k == 3)
                        last.then_inc(s["a2_bank"], 1)
                    for k in range(4):
                        pe.wait_ge(s["a2_relu"], 4 * c + k + 1)
                        last = mm(ps[:, c, :], ffn_w[:, 2560 + k * 128:2560 + k * 128 + 128],
                                  g[:, 1, k * N:(k + 1) * N], k == 0, k == 3)
                    last.then_inc(s["a3_bank"], 1)
                if LAYERS > 4:
                    pe.wait_ge(s["w_loaded"], 80)
                    for k in range(8):
                        mm(ps[:, 7, 0:128], W(4, "wv", k * 128, k * 128 + 128),
                           W(4, "wo", k * 128, k * 128 + 128), k == 0, k == 7)
                    for k in range(8):
                        last = mm(ps[:, 6, 0:1], W(4, "wo", k * 128, k * 128 + 128),
                                  W(4, "bv", k, k + 1), k == 0, k == 7)
                    last.then_inc(s["comb_bank"], 1)
                    pe.wait_ge(s["comb_ready"], 1)
                boundary(3)

            if LAYERS > 4:
                for c in range(CHUNKS):
                    h(4, c)
                    mm(ps[:, c, :], comb, H(c)).then_inc(s["l2_bank"], 1)
                boundary(4)

            def experts(layer, n_experts, pairs, chunk0, rounds):
                pe.wait_ge(s["w_loaded"], 16 * (layer + 1))
                pe.wait_ge(s["sel_loaded"], 16)
                h(layer, 3)
                for c in range(CHUNKS):
                    mm(ps[0:n_experts, c, :], W(layer, "router"), H(c)).then_inc(s["lg_bank"], 1)
                    pe.wait_ge(s["lg_ready"], chunk0 + c + 1)
                    for a in range(TILES):
                        last = nc.tensor.transpose(ps[:, 4, a * n_experts:(a + 1) * n_experts],
                                                   sc_rows[0:n_experts, a * P:(a + 1) * P],
                                                   ident[0:n_experts, 0:n_experts])
                    last.then_inc(s["sc_bank"], 1)
                    pe.wait_ge(s["parts_ready"], chunk0 + c + 1)
                    pe.wait_ge(s["ct_ready"], chunk0 + c)
                    for t in range(2):
                        for a in range(TILES):
                            last = nc.tensor.transpose(
                                ps[0:96, 5, :].bitcast(BF16)[:, t * N + a * P:t * N + (a + 1) * P],
                                coef_parts[:, a, t, :], ident_bf[:, :])
                    last.then_inc(s["ct_bank"], 1)
                pe.wait_ge(s["ct_ready"], chunk0 + CHUNKS)

                def gate_up(n, w, gb, c, chunk_coef=None):
                    at_least(pe, s["sg_ready"], n - 1)
                    mm(ps[:, gb, :], w[:, 0:128], H(c)).then_inc(s["g_bank"], 1)
                    at_least(pe, s["t_ready"], n)
                    mm(ps[:, 5, :], w[:, 128:256], H(c)).then_inc(s["u_bank"], 1)
                    if chunk_coef is not None:
                        t, q = chunk_coef
                        pe.wait_ge(s["hid_ready"], n)
                        mm(ps[:, 6, :], sel_coef[:, q, :].rearrange("p a n -> p (a n)"),
                           coef_rows[:, t, cols(c)]).then_inc(s["c_bank"], 1)

                def down(n, w, c, start=False, stop=False):
                    pe.wait_ge(s["hid_ready"], n + 1)
                    mm(ps[:, c, :], w[:, 256:384], g[:, 6, (c % 2) * N:(c % 2 + 1) * N], start, stop,
                       skip_group_check=True).then_inc(s["e_done"], 1)

                n0 = rounds * CHUNKS
                base1, base0 = (0, 0) if layer == 5 else (17, 16)
                pe.wait_ge(s["pair_loaded1"], 16 * (base1 + 1))
                for c in range(CHUNKS):
                    gate_up(n0 + c, pair_w[1], 4 if c % 2 == 0 else 7, c)
                    if c:
                        down(n0 + c - 1, pair_w[1], c - 1, True)
                down(n0 + 3, pair_w[1], 3, True)
                pe.wait_ge(s["pair_loaded0"], 16 * (base0 + 1))
                for c in range(CHUNKS):
                    gate_up(n0 + 4 + c, pair_w[0], 4 if c % 2 == 0 else 7, c, (0, bass.ds(0, 1)))
                    if c:
                        down(n0 + 3 + c, pair_w[0], c - 1)
                with pe.Fori(0, pairs // 2 - 1) as i:
                    for k in (0, 1):
                        pe.wait_ge(s["pair_loaded1" if k == 0 else "pair_loaded0"],
                                   16 * ((base1 if k == 0 else base0) + 2) + 16 * i)
                        for c in range(CHUNKS):
                            n = 8 * i + (n0 + 8 + 4 * k + c)
                            gate_up(n, pair_w[1 - k], 4 if c % 2 == 0 else 7, c,
                                    (1 - k, bass.ds(i + k, 1)))
                            down(n - 1, pair_w[1 - k] if c else pair_w[k], (c - 1) % 4)
                n1 = n0 + 4 * pairs
                pe.wait_ge(s["pair_loaded1"], 16 * (base1 + pairs // 2 + 1))
                for c in range(CHUNKS):
                    gate_up(n1 + c, pair_w[1], 4 if c % 2 == 0 else 7, c, (1, bass.ds(pairs // 2 - 1, 1)))
                    down(n1 + c - 1, pair_w[1] if c else pair_w[0], (c - 1) % 4, stop=c > 0)
                down(n1 + 3, pair_w[1], 3, stop=True)

            if LAYERS > 5:
                experts(5, 64, 32, 0, 0)
                boundary(5)

            if LAYERS > 6:
                pe.wait_ge(s["conv_setup"], 1)
                for c in range(CHUNKS):
                    h(6, c)
                    for i in range(2):
                        for j in range(4):
                            last = mm(ps[:, 4 * i + c, :], conv_w[:, j, i * 128:i * 128 + 128],
                                      normed[:, cols(c, j)], j == 0, j == 3)
                        last.then_inc(s["xa_bank"], 1)
                for c in range(CHUNKS):
                    pe.wait_ge(s["xa_ready"], 2 * c + 2)
                    for i in range(2):
                        mm(ps[:, 4 * i + c, :], W(6, "wz", i * 128, i * 128 + 128), H(c)).then_inc(s["z_bank"], 1)
                for c in range(CHUNKS):
                    pe.wait_ge(s["z_ready"], 2 * c + 2)
                    for i in range(2):
                        for k in range(2):
                            last = mm(ps[:, 4 * i + c, :],
                                      W(6, "wdt", k * 256 + i * 128, k * 256 + i * 128 + 128), G(k, c),
                                      k == 0, k == 1)
                        last.then_inc(s["dt_bank"], 1)
                for c in range(CHUNKS):
                    pe.wait_ge(s["dt_ready"], 2 * c + 2)
                    for k in range(2):
                        last = mm(ps[0:96, c, :], W(6, "wbc", k * 96, k * 96 + 96), G(k, c), k == 0, k == 1)
                    last.then_inc(s["bc_bank"], 1)
                pe.wait_ge(s["bcp_ready"], CHUNKS)

                def row(n):
                    return sel_bc[:, bass.ds(n, 1), :].rearrange("p a n -> p (a n)")

                def spread(nb, n, c, step):
                    at_least(pe, s["bs_ready"], step - 1)
                    mm(ps[:, 2 + nb, :], row(n), bc_rows[:, cols(c)]).then_inc(s["bb_bank"], 1)
                    at_least(pe, s["hc_ready"], step - 1)
                    mm(ps[:, 4 + nb, :], row(n + 16), bc_rows[:, cols(c)]).then_inc(s["cb_bank"], 1)

                def sum_n(nb, step, stop=False):
                    pe.wait_ge(s["hc_ready"], step + 1)
                    for i in range(2):
                        last = mm(ps[:, i, :], ident, tmp[:, (2 * nb + i) * N:(2 * nb + i + 1) * N], False, stop,
                                  skip_group_check=True)
                    last.then_inc(s["sum_done"], 1)

                spread(0, 0, 0, 0)
                spread(1, 1, 0, 1)
                pe.sem_inc(s["sum_done"], 2)
                with pe.Fori(0, CHUNKS) as c:
                    pe.wait_ge(s["yt_ready"], 2 * c + 1)
                    for i in range(2):
                        mm(ps[:, i, :], diag_d[:, i, :], G(i, c), True, False, skip_group_check=True)
                    with pe.Fori(0, 7) as m:
                        for nb in range(2):
                            sum_n(nb, 16 * c + 2 * m + nb)
                            spread(nb, 2 * m + 2 + nb, c, 16 * c + 2 * m + 2 + nb)
                    for nb in range(2):
                        sum_n(nb, 16 * c + 14 + nb, True)
                        spread(nb, nb, c + 1, 16 * c + 16 + nb)
                pe.wait_ge(s["yt_ready"], 2 * CHUNKS + 1)
                for c in range(CHUNKS):
                    pe.wait_ge(s["yg_ready"], c + 2)
                    for k in range(2):
                        last = mm(ps[:, c, :], W(6, "wout", k * 128, k * 128 + 128), G(2 + k, c), k == 0, k == 1)
                    last.then_inc(s["mo_bank"], 1)
                boundary(6)

            if LAYERS > 7:
                experts(7, 16, 8, CHUNKS, 33)
                boundary(7)

            for c in range(CHUNKS):
                pe.wait_ge(s["sum_ready"], c + 1)
                for a in range(TILES):
                    last = nc.tensor.transpose(ps[:, 4 + c, a * P:(a + 1) * P],
                                               g[:, 9, c * N + a * P:c * N + (a + 1) * P], ident)
                last.then_inc(s["raw_ready"], 1)

        @block.scalar
        def _(act):
            chain = Chain(act, s["act_chain"])

            def f(o, i, func, **kw):
                return nc.scalar.activation(o, i, func, **kw)

            def use_log_exp():
                act.preload_act_table_set("natural_log_exp_and_others")

            def square(name, src, sem, base):
                k = ACT_SQUARES.index(name)
                for c in range(CHUNKS):
                    act.wait_ge(s[sem], base + c + 1)
                    f(sq[:, cols(c)], src(c), ACT.Square).then_inc(s["sq_act"], 1)

            def rstd_of(name, eps, bank=4):
                k = NORM[name]
                for c in range(CHUNKS):
                    act.wait_ge(s["var_ready"], k * CHUNKS + c + 1)
                    chain(f(rstd[:, cols(c)], ps[:, bank + c, :], ACT.Ln, bias=eps))
                    chain.wait()
                    f(rstd[:, cols(c)], rstd[:, cols(c)], ACT.Exp, scale=-0.5).then_inc(s["rstd_ready"], 1)

            def boundary(layer):
                square(f"post{layer}", lambda c: ps[:, c, :], "centred", CHUNKS * (layer + 2))
                rstd_of(f"post{layer}", eps5)
                if layer + 1 < LAYERS:
                    rstd_of(f"pre{layer + 1}", eps5)

            def evacuate(sem, bank, **kw):
                for c in range(CHUNKS):
                    act.wait_ge(s[sem], c + 1)
                    f(y[:, cols(c)], ps[:, bank + c, :], ACT.Identity, **kw).then_inc(s["y_ready"], 1)

            use_log_exp()
            act.wait_ge(s["zeroed"], 1)
            for c in range(CHUNKS):
                act.wait_ge(s["raw_ready"], c + 1)
                f(y[:, cols(c)], ps[:, c, :], ACT.Copy).then_inc(s["y_ready"], 1)
            rstd_of("pre0", eps5, 0)
            rstd_of("ln1", eps5, 0)

            act.wait_ge(s["w_loaded"], 16)
            f(small[:, 15:16], W(0, "vec", 10, 11), ACT.Exp).then_inc(s["decay_ready"], 1)
            for c in range(CHUNKS):
                act.wait_ge(s["k_bank"], c + 1)
                f(G(5, c), ps[:, c, :], ACT.Copy)
                act.wait_ge(s["v_bank"], c + 1)
                f(G(6, c), ps[:, 4 + c, :], ACT.Copy).then_inc(s["kv_ready"], 1)
            for c in range(CHUNKS):
                act.wait_ge(s["r_bank"], c + 1)
                f(G(7, c), ps[:, c, :], ACT.Sigmoid).then_inc(s["sr_ready"], 1)
            use_log_exp()
            for c in range(CHUNKS):
                act.wait_ge(s["d12_ready"], c + 1)
                f(G(11, c), G(11, c), ACT.Exp, bias=small[:, 14:15])
                f(G(12, c), G(12, c), ACT.Exp).then_inc(s["eb_ready"], 1)
                act.wait_ge(s["d34_ready"], c + 1)
                f(G(1, c), G(1, c), ACT.Exp)
                f(G(2, c), G(2, c), ACT.Exp, bias=W(0, "vec", 7, 8)).then_inc(s["ee_ready"], 1)
            for c in range(CHUNKS):
                act.wait_ge(s["den_ready"], c + 1)
                chain(f(y[:, cols(c)], y[:, cols(c)], ACT.Ln))
                chain.wait()
                f(y[:, cols(c)], y[:, cols(c)], ACT.Exp, scale=-1.0).then_inc(s["rd_ready"], 1)
            square("ln2", lambda c: ps[:, 4 + c, :], "centred", CHUNKS)
            rstd_of("ln2", eps5, 0)
            for c in range(CHUNKS):
                act.wait_ge(s["fr_bank"], c + 1)
                f(G(8, c), ps[:, c, :], ACT.Sigmoid).then_inc(s["sr2_ready"], 1)
            use_log_exp()
            for c in range(CHUNKS):
                act.wait_ge(s["kk_ready"], 4 * c)
                for m in range(4):
                    act.wait_ge(s["fk_bank"], 4 * c + m + 1)
                    f(g[:, 6, m * N:(m + 1) * N], ps[:, m, :], ACT.Relu).then_inc(s["relu_ready"], 1)
            boundary(0)

            if LAYERS > 1:
                act.wait_ge(s["nam_bias_bank"], 1)
                f(nam_bout, ps[:, 7, 0:1], ACT.Identity, bias=W(1, "bout")).then_inc(s["nam_bias"], 1)
                for c in range(CHUNKS):
                    act.wait_ge(s["nam_s_bank"], c + 1)
                    act.wait_ge(s["nam_done"], c)
                    for j in range(8):
                        f(g[:, j // 4, (j % 4) * N:(j % 4 + 1) * N], ps[:, c, :], ACT.Relu,
                          scale=W(1, "w1", j, j + 1), bias=nam_b1[:, j:j + 1]).then_inc(s["nam_relu"], 1)
                act.wait_ge(s["nam_bias"], 1)
                evacuate("nam_done", 4, bias=nam_bout)
                boundary(1)

            if LAYERS > 2:
                for c in range(CHUNKS):
                    act.wait_ge(s["k_bank2"], c + 1)
                    f(G(0, c), ps[:, c, :], ACT.Copy).then_inc(s["k2_ready"], 1)
                    act.wait_ge(s["q_bank2"], c + 1)
                    f(G(5, c), ps[:, 4 + c, :], ACT.Sigmoid).then_inc(s["sigq_ready"], 1)
                for c in range(CHUNKS):
                    act.wait_ge(s["g1_bank"], c + 1)
                    f(tmp[0:8, cols(c)], ps[0:8, c, :], ACT.Copy).then_inc(s["g1_ready"], 1)
                for c in range(CHUNKS):
                    act.wait_ge(s["g2_bank"], c + 1)
                    f(G(12, c), ps[:, 4 + c, :], ACT.Sigmoid).then_inc(s["gate_ready"], 1)
                use_log_exp()
                for c in range(CHUNKS):
                    act.wait_ge(s["md_ready"], c + 1)
                    f(G(3, c), G(3, c), ACT.Exp)
                    f(G(4, c), G(4, c), ACT.Exp).then_inc(s["me_ready"], 1)
                for c in range(CHUNKS):
                    act.wait_ge(s["s_ready"], c + 1)
                    chain(f(rstd[:, cols(c)], G(2, c, 1), ACT.Ln))
                    chain.wait()
                    f(rstd[:, cols(c)], rstd[:, cols(c)], ACT.Exp, scale=-1.0).then_inc(s["rs_ready"], 1)
                square("rms", lambda c: G(4, c), "og_ready", 0)
                rstd_of("rms", eps6, 0)
                evacuate("wo_bank", 4)
                boundary(2)

            if LAYERS > 3:
                act.wait_ge(s["f_setup"], 1)
                for c in range(CHUNKS):
                    for m in range(4):
                        act.wait_ge(s["a1_bank"], 4 * c + m + 1)
                        f(g[:, 0, m * N:(m + 1) * N], ps[:, m, :], ACT.Relu, scale=scales[:, 0:1])\
                            .then_inc(s["a1_relu"], 1)
                    for m in range(4):
                        act.wait_ge(s["a2_bank"], 4 * c + m + 1)
                        f(g[:, 1, m * N:(m + 1) * N], ps[:, 4 + m, :], ACT.Relu, scale=scales[:, 1:2])\
                            .then_inc(s["a2_relu"], 1)
                    act.wait_ge(s["a3_bank"], c + 1)
                    f(y[:, cols(c)], ps[:, c, :], ACT.Copy, scale=scales[:, 2:3]).then_inc(s["y_ready"], 1)
                if LAYERS > 4:
                    act.wait_ge(s["comb_bank"], 1)
                    f(comb, ps[:, 7, 0:128], ACT.Copy)
                    f(comb_bias, ps[:, 6, 0:1], ACT.Identity, bias=W(4, "bo")).then_inc(s["comb_ready"], 1)
                boundary(3)

            if LAYERS > 4:
                act.wait_ge(s["comb_ready"], 1)
                evacuate("l2_bank", 0, bias=comb_bias)
                boundary(4)

            def experts(layer, n_experts, pairs, chunk0, rounds):
                for c in range(CHUNKS):
                    act.wait_ge(s["lg_bank"], chunk0 + c + 1)
                    act.wait_ge(s["sc_bank"], chunk0 + c)
                    f(sc_rows[0:n_experts], ps[0:n_experts, c, :], ACT.Sigmoid).then_inc(s["lg_ready"], 1)
                    act.wait_ge(s["ct_bank"], chunk0 + c + 1)
                    f(coef_rows[:, :, cols(c)], ps[0:96, 5, :].bitcast(BF16).rearrange("p (t n) -> p t n", t=2),
                      ACT.Copy).then_inc(s["ct_ready"], 1)

                def silu(n, par):
                    act.wait_ge(s["g_bank"], n + 1)
                    at_least(act, s["t_ready"], n - 1)
                    f(g[:, 5, par * N:(par + 1) * N], ps[:, 4 if par == 0 else 7, :], ACT.Silu)\
                        .then_inc(s["sg_ready"], 1)

                for c in range(CHUNKS):
                    silu(rounds * CHUNKS + c, c % 2)
                with act.Fori(0, pairs) as p:
                    for c in range(CHUNKS):
                        silu(p * CHUNKS + ((rounds + 1) * CHUNKS + c), c % 2)
                use_log_exp()
                for c in range(CHUNKS):
                    act.wait_ge(s["e_done"], CHUNKS * (rounds + pairs) + c + 1)
                    f(y[:, cols(c)], ps[:, c, :], ACT.Copy).then_inc(s["y_ready"], 1)

            if LAYERS > 5:
                experts(5, 64, 32, 0, 0)
                boundary(5)

            if LAYERS > 6:
                act.wait_ge(s["w_loaded"], 7 * 16)
                act.wait_ge(s["a_ready"], 1)
                f(neg_a, W(6, "a_log"), ACT.Exp).then_inc(s["a_ready"], 1)
                for c in range(CHUNKS):
                    for i in range(2):
                        act.wait_ge(s["xa_bank"], 2 * c + i + 1)
                        f(G(i, c), ps[:, 4 * i + c, :], ACT.Silu, bias=W(6, "conv_b", i, i + 1))\
                            .then_inc(s["xa_ready"], 1)
                for c in range(CHUNKS):
                    for i in range(2):
                        act.wait_ge(s["z_bank"], 2 * c + i + 1)
                        f(G(2 + i, c), ps[:, 4 * i + c, :], ACT.Silu).then_inc(s["z_ready"], 1)
                use_log_exp()
                for c in range(CHUNKS):
                    for i in range(2):
                        act.wait_ge(s["dt_bank"], 2 * c + i + 1)
                        f(G(10 + i, c), ps[:, 4 * i + c, :], ACT.Relu, bias=W(6, "dt_b", i, i + 1))
                        chain(f(G(8 + i, c), ps[:, 4 * i + c, :], ACT.Abs, bias=W(6, "dt_b", i, i + 1)))
                        chain.wait()
                        chain(f(G(8 + i, c), G(8 + i, c), ACT.Exp, scale=-1.0))
                        chain.wait()
                        f(G(8 + i, c), G(8 + i, c), ACT.Ln, bias=one).then_inc(s["dt_ready"], 1)
                act.wait_ge(s["dl_ready"], CHUNKS)
                act.wait_ge(s["a_ready"], 3)

                act.sem_inc(s["yt_ready"], 1)
                with act.Fori(0, CHUNKS) as c:
                    with act.Fori(0, 8) as m:
                        for nb in range(2):
                            step = 16 * c + 2 * m + nb
                            act.wait_ge(s["bb_bank"], step + 1)
                            act.wait_ge(s["db_ready"], step + 1)
                            f(g[:, 8, nb * N:(nb + 1) * N], ps[:, 2 + nb, :], ACT.Copy).then_inc(s["bs_ready"], 1)
                            hold(act, s["hs_done"], step + 1)
                            for i in range(2):
                                f(g[:, 9, (2 * nb + i) * N:(2 * nb + i + 1) * N], G(4 + i, c), ACT.Exp,
                                  scale=neg_a[:, bass.ds(2 * m + (16 * i + nb), 1)]).then_inc(s["da_ready"], 1)
                    act.wait_ge(s["sum_done"], 16 * c + 18)
                    act.wait_ge(s["yg_ready"], c + 1)
                    for i in range(2):
                        f(sq[:, i * N:(i + 1) * N], ps[:, i, :], ACT.Copy).then_inc(s["yt_ready"], 1)
                evacuate("mo_bank", 0)
                boundary(6)

            if LAYERS > 7:
                experts(7, 16, 8, CHUNKS, 33)
                boundary(7)

            for c in range(CHUNKS):
                act.wait_ge(s["raw_ready"], CHUNKS + c + 1)
                f(G(10, c), ps[:, 4 + c, :], ACT.Copy).then_inc(s["back_ready"], 1)

        @block.gpsimd
        def _(pool):
            pv = nc.gpsimd

            def square(name, src, sem, base):
                for c in range(CHUNKS):
                    pool.wait_ge(s[sem], base + c + 1)
                    pv.tensor_tensor(sq[:, cols(c)], src(c), src(c), ALU.mult).then_inc(s["sq_pool"], 1)

            def R(c):
                return resid[:, cols(c)]

            square("pre0", R, "x_ready", 0)
            square("ln1", H, "h_ready", 0)

            def token_shift(base):
                for c in range(CHUNKS):
                    pool.wait_ge(s["h1_ready"], base + c + 1)
                    pv.tensor_tensor(G(1, c), G(0, c, 1), G(0, c, 0), ALU.subtract).then_inc(s["d_ready"], 1)

            token_shift(0)
            for c in range(CHUNKS):
                pool.wait_ge(s["pp_ready"], c + 1)
                pv.tensor_tensor(G(11, c), G(8, c, 0), G(8, c, 1), ALU.subtract)
                pv.tensor_tensor(G(12, c), G(5, c), G(8, c, 1), ALU.subtract).then_inc(s["d12_ready"], 1)
                pool.wait_ge(s["p_ready"], c + 1)
                pv.tensor_tensor(G(1, c), G(8, c, 0), G(3, c), ALU.subtract)
                pv.tensor_tensor(G(2, c), G(5, c), G(3, c), ALU.subtract).then_inc(s["d34_ready"], 1)
            token_shift(CHUNKS)

            for layer in range(1, LAYERS):
                square(f"pre{layer}", R, "x_ready", CHUNKS * layer)
                if layer == 2:
                    for c in range(CHUNKS):
                        pool.wait_ge(s["m_ready"], c + 1)
                        pv.tensor_tensor(G(3, c), G(1, c, 0), G(1, c, 1), ALU.subtract)
                        pv.tensor_tensor(G(4, c), G(0, c), G(1, c, 1), ALU.subtract).then_inc(s["md_ready"], 1)
                    pool.sem_inc(s["qm_ready"], 2)
                    with pool.Fori(0, CHUNKS) as c:
                        for e in range(8):
                            par = e % 2
                            pool.wait_ge(s["st_ready"], 8 * c + e + 1)
                            hold(pool, s["qm_used"], 8 * c + e + 1)
                            pv.tensor_tensor(
                                g[:, 2, 2 * par * N:(2 * par + 2) * N].rearrange("p (r n) -> p r n", r=2),
                                g[:, 1, 2 * par * N:(2 * par + 2) * N].rearrange("p (r n) -> p r n", r=2),
                                g[:, 8:10, cols(c)], ALU.mult).then_inc(s["qm_ready"], 1)
                if layer == 6:
                    pool.wait_ge(s["du_ready"], CHUNKS)
                    pool.sem_inc(s["db_ready"], 2)
                    pool.sem_inc(s["yg_ready"], 1)
                    with pool.Fori(0, CHUNKS) as c:
                        with pool.Fori(0, 8) as m:
                            for nb in range(2):
                                step = 16 * c + 2 * m + nb
                                pool.wait_ge(s["bs_ready"], step + 1)
                                hold(pool, s["hs_done"], step + 1)
                                pv.tensor_tensor(
                                    g[:, 10, 2 * nb * N:(2 * nb + 2) * N].rearrange("p (i n) -> p i n", i=2),
                                    g[:, 6:8, cols(c)],
                                    g[:, 8:9, nb * N:(nb + 1) * N].to_broadcast([P, 2, N]),
                                    ALU.mult).then_inc(s["db_ready"], 1)
                        hold(pool, s["yt_ready"], 2 * c + 3)
                        pv.tensor_tensor(g[:, 2:4, cols(c)], sq[:, 0:2 * N].rearrange("p (i n) -> p i n", i=2),
                                         g[:, 2:4, cols(c)], ALU.mult).then_inc(s["yg_ready"], 1)

        @block.vector
        def _(dve):
            v = nc.vector
            chain = Chain(dve, s["dve_chain"])

            def tt(o, a, b, op=ALU.mult):
                return v.tensor_tensor(o, a, b, op)

            def scale_by_rstd(name, o, src, done):
                for c in range(CHUNKS):
                    dve.wait_ge(s["rstd_ready"], NORM[name] * CHUNKS + c + 1)
                    tt(o(c), src(c), rstd[:, cols(c)]).then_inc(s[done], 1)

            def R(c):
                return resid[:, cols(c)]

            def boundary(layer):
                for c in range(CHUNKS):
                    dve.wait_ge(s["rstd_ready"], NORM[f"post{layer}"] * CHUNKS + c + 1)
                    chain(tt(tmp[:, cols(c)], ps[:, c, :], rstd[:, cols(c)]))
                    chain.wait()
                    tt(R(c), R(c), tmp[:, cols(c)], ALU.add).then_inc(s["x_ready"], 1)
                if layer + 1 < LAYERS:
                    scale_by_rstd(f"pre{layer + 1}", H, R, "h_ready")

            for k, value in ((13, 1.0), (49, 1e-5), (50, 1e-6)):
                v.memset(small[:, k:k + 1], value)
            v.memset(normed[:, 0:LEAD], 0.0)
            v.memset(g[:, 0, 0:1], 0.0)
            v.memset(g[:, 8, 0:1], -1e38)
            v.memset(g[:, 9:11, 0:1], 0.0)
            chain(v.memset(carry[:, :], 0.0))
            v.memset(small[:, 51:52], 0.0).then_inc(s["zeroed"], 1)
            dve.wait_ge(s["consts_loaded"], 16)
            chain(v.tensor_copy(ident_bf[:, :], ident))

            for c in range(CHUNKS):
                dve.wait_ge(s["centred"], c + 1)
                tt(mean0[:, cols(c)], y[:, cols(c)], ps[:, 4 + c, :], ALU.subtract)
                v.tensor_copy(R(c), ps[:, 4 + c, :]).then_inc(s["x_ready"], 1)
            scale_by_rstd("pre0", H, R, "h_ready")

            vec = [W(0, "vec", k, k + 1) for k in range(12)]
            ln1_w, ln1_b, ln2_w, ln2_b, tmk, tmv, tmr, bonus, f_tmk, f_tmr = vec[:10]
            w_decay = small[:, 14:15]
            dve.wait_ge(s["decay_ready"], 1)
            chain(v.tensor_scalar(w_decay, small[:, 15:16], -1.0, None, ALU.mult))

            for c in range(CHUNKS):
                dve.wait_ge(s["rstd_ready"], NORM["ln1"] * CHUNKS + c + 1)
                chain(tt(tmp[:, cols(c)], H(c), rstd[:, cols(c)]))
                chain.wait()
                v.tensor_scalar(G(0, c, 1), tmp[:, cols(c)], ln1_w, ln1_b, ALU.mult, ALU.add)\
                    .then_inc(s["h1_ready"], 1)

            def mix(o, amount, c):
                return v.scalar_tensor_tensor(o, G(1, c), amount, G(0, c, 0), ALU.mult, ALU.add)

            for c in range(CHUNKS):
                dve.wait_ge(s["d_ready"], c + 1)
                mix(G(2, c), tmk, c)
                mix(G(3, c), tmv, c)
                mix(G(4, c), tmr, c).then_inc(s["mix_ready"], 1)
            for c in range(CHUNKS):
                dve.wait_ge(s["kv_ready"], c + 1)
                v.tensor_tensor_scan(G(8, c, 1), w_decay.to_broadcast([P, N]), G(5, c),
                                     g[:, 8, cols(c, 0, 1)], ALU.add, ALU.max).then_inc(s["pp_ready"], 1)
                dve.wait_ge(s["pp_ready"], c + 1)
                v.scalar_tensor_tensor(G(3, c), G(5, c), bonus, G(8, c, 0), ALU.add, ALU.max)\
                    .then_inc(s["p_ready"], 1)
            for c in range(CHUNKS):
                dve.wait_ge(s["eb_ready"], c + 1)
                dve.wait_ge(s["ee_ready"], c + 1)
                dve.wait_ge(s["sr_ready"], c + 1)
                chain(tt(G(3, c), G(12, c), G(6, c)))
                chain(v.tensor_tensor_scan(G(10, c, 1), G(11, c), G(12, c), g[:, 10, cols(c, 0, 1)],
                                           ALU.mult, ALU.add))
                chain.wait()
                chain(v.tensor_tensor_scan(G(9, c, 1), G(11, c), G(3, c), g[:, 9, cols(c, 0, 1)],
                                           ALU.mult, ALU.add))
                chain(tt(y[:, cols(c)], G(1, c), G(10, c, 0)))
                chain.wait()
                tt(y[:, cols(c)], y[:, cols(c)], G(2, c), ALU.add).then_inc(s["den_ready"], 1)
                chain(tt(G(4, c), G(1, c), G(9, c, 0)))
                chain(tt(tmp[:, cols(c)], G(2, c), G(6, c)))
                chain.wait()
                chain(tt(G(4, c), G(4, c), tmp[:, cols(c)], ALU.add))
            for c in range(CHUNKS):
                chain.wait()
                dve.wait_ge(s["rd_ready"], c + 1)
                chain(tt(G(4, c), G(4, c), y[:, cols(c)]))
                chain.wait()
                tt(G(4, c), G(4, c), G(7, c)).then_inc(s["rw_ready"], 1)
            for c in range(CHUNKS):
                dve.wait_ge(s["ow_bank"], c + 1)
                tt(G(5, c), H(c), ps[:, c, :], ALU.add).then_inc(s["x1_ready"], 1)
            for c in range(CHUNKS):
                dve.wait_ge(s["rstd_ready"], NORM["ln2"] * CHUNKS + c + 1)
                chain(tt(tmp[:, cols(c)], ps[:, 4 + c, :], rstd[:, cols(c)]))
                chain.wait()
                v.tensor_scalar(G(0, c, 1), tmp[:, cols(c)], ln2_w, ln2_b, ALU.mult, ALU.add)\
                    .then_inc(s["h1_ready"], 1)
            for c in range(CHUNKS):
                dve.wait_ge(s["d_ready"], CHUNKS + c + 1)
                mix(G(2, c), f_tmk, c)
                mix(G(4, c), f_tmr, c).then_inc(s["mix_ready"], 1)
            for c in range(CHUNKS):
                dve.wait_ge(s["fv_bank"], c)
                for m in range(4):
                    dve.wait_ge(s["relu_ready"], 4 * c + m + 1)
                    tt(g[:, 7, m * N:(m + 1) * N], g[:, 6, m * N:(m + 1) * N], g[:, 6, m * N:(m + 1) * N])\
                        .then_inc(s["kk_ready"], 1)
            for c in range(CHUNKS):
                dve.wait_ge(s["sr2_ready"], c + 1)
                dve.wait_ge(s["fv_bank"], c + 1)
                chain(tt(tmp[:, cols(c)], G(8, c), ps[:, 4 + c, :]))
                chain.wait()
                tt(y[:, cols(c)], G(5, c), tmp[:, cols(c)], ALU.add).then_inc(s["y_ready"], 1)

            if LAYERS > 1:
                dve.wait_ge(s["w_loaded"], 32)
                v.scalar_tensor_tensor(nam_b1, W(1, "w1"), W(1, "bin"), W(1, "b1"), ALU.mult, ALU.add)
                for j in range(8):
                    last = v.tensor_scalar(nam_wout[j], W(1, "wout"), W(1, "w2", j, j + 1), None, ALU.mult)
                last.then_inc(s["nam_setup"], 1)
            boundary(0)
            if LAYERS > 1:
                boundary(1)

            if LAYERS > 2:
                dve.wait_ge(s["w_loaded"], 48)
                v.tensor_scalar(wo_normed, W(2, "wo"), W(2, "norm_w"), None, ALU.mult).then_inc(s["setup2"], 1)
                v.memset(g[:, 1, 0:1], 0.0)
                chain(v.memset(g[:, 2, 0:1], 1.0))
                chain.wait()
                for c in range(CHUNKS):
                    dve.wait_ge(s["k2_ready"], c + 1)
                    v.tensor_tensor_scan(G(1, c, 1), G(0, c), G(0, c), g[:, 1, cols(c, 0, 1)],
                                         ALU.max, ALU.max).then_inc(s["m_ready"], 1)
                    dve.wait_ge(s["m_ready"], c + 1)
                for c in range(CHUNKS):
                    dve.wait_ge(s["sigq_ready"], c + 1)
                    tt(G(5, c), G(5, c), ps[:, 4 + c, :]).then_inc(s["q_used"], 1)
                for c in range(CHUNKS):
                    dve.wait_ge(s["me_ready"], c + 1)
                    v.tensor_tensor_scan(G(2, c, 1), G(3, c), G(4, c), g[:, 2, cols(c, 0, 1)],
                                         ALU.mult, ALU.add).then_inc(s["s_ready"], 1)
                    dve.wait_ge(s["s_ready"], c + 1)
                dve.wait_ge(s["rope_loaded"], 16)
                for c in range(CHUNKS):
                    dve.wait_ge(s["rs_ready"], c + 1)
                    dve.wait_ge(s["q_used"], c + 1)
                    chain(tt(G(4, c), G(4, c), rstd[:, cols(c)]))
                    tt(G(8, c), G(5, c), G(10, c))
                    tt(G(9, c), G(5, c), G(11, c))
                    chain.wait()
                    chain(v.tensor_scalar(G(3, c), G(4, c), -1.0, 1.0, ALU.mult, ALU.add))
                    tt(G(6, c), G(4, c), G(10, c))
                    chain(tt(G(7, c), G(4, c), G(11, c)))
                chain.wait()
                dve.sem_inc(s["vb_used"], 2)
                with chain.each(CHUNKS, 8 * 2) as c:
                    chain.wait()
                    for e in range(8):
                        par = e % 2
                        b2 = g[:, 0, 2 * par * N:(2 * par + 2) * N].rearrange("p (r n) -> p r n", r=2)
                        st2 = g[:, 1, 2 * par * N:(2 * par + 2) * N].rearrange("p (r n) -> p r n", r=2)
                        dve.wait_ge(s["vb_bank"], 8 * c + e + 1)
                        tt(b2, g[:, 6:8, cols(c)],
                           ps[:, e % 2:e % 2 + 1, :].to_broadcast([P, 2, N])).then_inc(s["vb_used"], 1)
                        dve.wait_ge(s["vb_used"], 8 * c + e + 3)
                        dve.wait_ge(s["qm_ready"], 8 * c + e + 1)
                        chain(v.tensor_tensor_scan(st2[:, 0, :], G(3, c), b2[:, 0, :],
                                                   carry[:, 2 * e:2 * e + 1], ALU.mult, ALU.add))
                        v.tensor_tensor_scan(st2[:, 1, :], G(3, c), b2[:, 1, :],
                                             carry[:, 2 * e + 1:2 * e + 2], ALU.mult, ALU.add)\
                            .then_inc(s["st_ready"], 1)
                        dve.wait_ge(s["st_ready"], 8 * c + e + 1)
                        chain(v.tensor_copy(carry[:, 2 * e:2 * e + 2], st2[:, :, N - 1]))
                for c in range(CHUNKS):
                    dve.wait_ge(s["qm_used"], 8 * c + 10)
                    tt(G(4, c), G(12, c), ps[:, 4 + c, :]).then_inc(s["og_ready"], 1)
                scale_by_rstd("rms", lambda c: G(5, c), lambda c: G(4, c), "nrm_ready")
            if LAYERS > 3:
                dve.wait_ge(s["w_loaded"], 64)
                dve.wait_ge(s["bools_loaded"], 16)
                tt(ffn_w[:, 0:512], kbool[:, 0:512], kbool[:, 512:1024], ALU.subtract)
                v.tensor_scalar(ffn_w[:, 512:3072], kbool[:, 1024:3584], 2.0, -1.0, ALU.mult, ALU.add)
                v.tensor_scalar(scales[:, 0:1], W(3, "s", 0, 1), 4.0, None, ALU.mult)
                v.tensor_scalar(scales[:, 1:2], W(3, "s", 1, 2), 2.0, None, ALU.mult)
                v.tensor_copy(scales[:, 2:3], W(3, "s", 2, 3)).then_inc(s["f_setup"], 1)
            for layer in (2, 3, 4):
                if LAYERS > layer:
                    boundary(layer)

            def experts(layer, E, pairs, groups, keep_groups, top, chunk0, rounds):
                size = E // groups
                w = TILES * E
                A = g[:, 1, 0:T].rearrange("p (k n) -> p k n", k=8)
                B = g[:, 2, 0:T].rearrange("p (k n) -> p k n", k=8)
                score, biased, equal, others, kept, replaced, coef, rest = (A[:, k, 0:w] for k in range(8))
                better, ahead = B[:, 0, 0:TILES * groups * groups], B[:, 1, 0:TILES * groups * groups]
                sm = B[:, 2, :]
                G1 = TILES * groups
                best, count, second, group, two, keep = (sm[:, 32 * k:32 * k + G1] for k in range(6))
                top8 = B[:, 3, 0:32].rearrange("p (a n) -> p a n", a=TILES)
                total, share = B[:, 3, 32:36], B[:, 3, 36:40]
                wide = TILES * (E + (4 if layer == 7 else 0))
                padded = B[:, 4, 0:wide].rearrange("p (a n) -> p a n", a=TILES)
                out_padded = B[:, 5, 0:wide].rearrange("p (a n) -> p a n", a=TILES)
                before = W(layer, "before", 0, groups * groups)
                bias = W(layer, "bias", 0, E)

                def by(ap, k):
                    return ap.rearrange("p (a e) -> p a e", e=k)

                def over(ap, n):
                    return by(ap, 1).to_broadcast([P, ap.shape[1], n])

                def square_of(ap, axis):
                    q = by(ap, groups)
                    q = q.unsqueeze(3) if axis == 2 else q.unsqueeze(2)
                    return q.to_broadcast([P, TILES, groups, groups])

                def step(ins):
                    chain(ins)
                    chain.wait()

                dve.wait_ge(s["w_loaded"], 16 * (layer + 1))
                step(v.memset(g[:, 3, 0:384], 0.0))
                for c in range(CHUNKS):
                    dve.wait_ge(s["sc_bank"], chunk0 + c + 1)
                    step(v.tensor_copy(score, ps[:, 4, 0:w]))
                    step(tt(by(biased, E), by(score, E), bias.unsqueeze(1).to_broadcast([P, TILES, E]), ALU.add))
                    step(v.tensor_reduce(best, by(biased, size), AX_X, ALU.max))
                    if layer == 5:
                        step(tt(by(equal, size), by(biased, size), over(best, size), ALU.is_equal))
                        step(v.tensor_reduce(count, by(equal, size), AX_X, ALU.add))
                        step(v.scalar_tensor_tensor(others, equal, -BIG, biased, ALU.mult, ALU.add))
                        step(v.tensor_reduce(second, by(others, size), AX_X, ALU.max))
                        step(v.tensor_scalar(two, count, 2.0, None, ALU.is_ge))
                        step(tt(group, two, best))
                        step(v.tensor_scalar(two, two, -1.0, BIG, ALU.add, ALU.mult))
                        step(tt(group, group, two, ALU.add))
                        step(tt(second, second, group, ALU.max))
                        step(tt(group, best, second, ALU.add))
                    else:
                        group = best
                    b4 = better.rearrange("p (a i j) -> p a i j", i=groups, j=groups)
                    a4 = ahead.rearrange("p (a i j) -> p a i j", i=groups, j=groups)
                    chain(tt(b4, square_of(group, 3), square_of(group, 2), ALU.is_gt))
                    step(tt(a4, square_of(group, 3), square_of(group, 2), ALU.is_equal))
                    step(tt(by(ahead, groups * groups), by(ahead, groups * groups),
                            before.unsqueeze(1).to_broadcast([P, TILES, groups * groups])))
                    step(tt(better, better, ahead, ALU.add))
                    step(v.tensor_reduce(keep, by(better, groups), AX_X, ALU.add))
                    step(v.tensor_scalar(keep, keep, float(keep_groups), None, ALU.is_lt))
                    step(tt(by(kept, size), by(biased, size), over(keep, size)))
                    if layer == 5:
                        for a in range(TILES):
                            last = v.max(top8[:, a, :], kept[:, a * E:(a + 1) * E])
                        step(last)
                        for a in range(TILES):
                            last = v.match_replace(replaced[:, a * E:(a + 1) * E], top8[:, a, :],
                                                   kept[:, a * E:(a + 1) * E], BIG)
                        step(last)
                        chosen = replaced
                    else:
                        step(v.tensor_scalar(keep, keep, -1.0, BIG, ALU.add, ALU.mult))
                        step(tt(by(kept, size), by(kept, size), over(keep, size), ALU.add))
                        chain(v.memset(padded[:, :, E:E + 4], -2 * BIG))
                        step(v.tensor_copy(padded[:, :, 0:E], by(kept, E)))
                        for a in range(TILES):
                            last = v.max(top8[:, a, :], kept[:, a * E:(a + 1) * E])
                        step(last)
                        step(v.memset(top8[:, :, 4:8], -2 * BIG))
                        for a in range(TILES):
                            last = v.match_replace(out_padded[:, a, :], top8[:, a, :], padded[:, a, :], BIG)
                        step(last)
                        step(v.tensor_copy(by(replaced, E), out_padded[:, :, 0:E]))
                    step(v.scalar_tensor_tensor(coef, replaced, BIG, score, ALU.is_equal, ALU.mult))
                    if layer == 5:
                        step(v.tensor_reduce(total, by(coef, E), AX_X, ALU.add))
                        step(v.tensor_scalar(total, total, 1e-20, None, ALU.add))
                        step(v.reciprocal(share, total))
                        step(v.tensor_scalar(share, share, 2.5, None, ALU.mult))
                        step(tt(by(coef, E), by(coef, E), over(share, E)))
                    at_least(dve, s["ct_bank"], chunk0 + c)
                    for part in range(3):
                        for t in range(2):
                            view = coef.rearrange("p (a q t r) -> p a q t r", a=TILES, t=2, r=2)[:, :, :, t, :]
                            dst = coef_parts[:, :, t, 32 * part:32 * part + E // 2]\
                                .rearrange("p a (q r) -> p a q r", r=2)
                            if part < 2:
                                chain(v.tensor_copy(dst, view))
                            else:
                                last = v.tensor_copy(dst, view)
                        if part < 2:
                            chain.wait()
                            for t in range(2):
                                view = coef.rearrange("p (a q t r) -> p a q t r", a=TILES, t=2, r=2)[:, :, :, t, :]
                                dst = coef_parts[:, :, t, 32 * part:32 * part + E // 2]\
                                    .rearrange("p a (q r) -> p a q r", r=2)
                                chain(tt(view, view, dst, ALU.subtract))
                            chain.wait()
                    last.then_inc(s["parts_ready"], 1)

                def glu(n, c, coef_no=None):
                    par = c % 2
                    silu_n = g[:, 5, par * N:(par + 1) * N]
                    prod = g[:, 5, (2 + par) * N:(3 + par) * N]
                    hidden = g[:, 6, par * N:(par + 1) * N]
                    dve.wait_ge(s["sg_ready"], n + 1)
                    dve.wait_ge(s["u_bank"], n + 1)
                    if coef_no is None:
                        at_least(dve, s["e_done"], n - 1)
                        tt(prod, silu_n, ps[:, 5, :]).then_inc(s["t_ready"], 1)
                        dve.wait_ge(s["t_ready"], n + 1)
                        v.tensor_copy(hidden, prod).then_inc(s["hid_ready"], 1)
                        return
                    tt(prod, silu_n, ps[:, 5, :]).then_inc(s["t_ready"], 1)
                    dve.wait_ge(s["t_ready"], n + 1)
                    dve.wait_ge(s["c_bank"], coef_no)
                    dve.wait_ge(s["e_done"], n - 1)
                    tt(hidden, prod, ps[:, 6, :]).then_inc(s["hid_ready"], 1)

                n0 = rounds * CHUNKS
                c0 = 0 if layer == 5 else 32 * CHUNKS
                for c in range(CHUNKS):
                    glu(n0 + c, c)
                with dve.Fori(0, pairs) as p:
                    for c in range(CHUNKS):
                        glu(p * CHUNKS + (n0 + CHUNKS + c), c, p * CHUNKS + (c0 + c + 1))

            if LAYERS > 5:
                experts(5, 64, 32, 8, 4, 8, 0, 0)
                if LAYERS > 6:
                    dve.wait_ge(s["w_loaded"], 7 * 16)
                    conv = W(6, "conv").rearrange("p (j n) -> p j n", j=4)
                    for j in range(4):
                        last = tt(conv_w[:, j, :], W(6, "wx"), conv[:, j, :])
                    last.then_inc(s["conv_setup"], 1)
                boundary(5)

            if LAYERS > 6:
                v.tensor_scalar(W(6, "a_log"), W(6, "a_log"), 80.0, None, ALU.min).then_inc(s["a_ready"], 1)
                dve.wait_ge(s["a_ready"], 2)
                v.tensor_scalar(neg_a, neg_a, -1.0, None, ALU.mult).then_inc(s["a_ready"], 1)
                for i in range(2):
                    v.tensor_scalar(diag_d[:, i, :], ident, W(6, "d", i, i + 1), None, ALU.mult)
                v.memset(g[0:96, 12, T // 2:T // 2 + N // 2], 0.0)
                chain(v.memset(carry[:, :], 0.0))
                for c in range(CHUNKS):
                    dve.wait_ge(s["dt_ready"], 2 * c + 2)
                    tt(g[:, 4:6, cols(c)], g[:, 8:10, cols(c)], g[:, 10:12, cols(c)], ALU.add)\
                        .then_inc(s["dl_ready"], 1)
                    dve.wait_ge(s["dl_ready"], c + 1)
                    tt(g[:, 6:8, cols(c)], g[:, 4:6, cols(c)], g[:, 0:2, cols(c)]).then_inc(s["du_ready"], 1)
                part = [tmp[0:96, k * N:(k + 1) * N] for k in range(3)]
                low = tmp[0:96, 3 * N:4 * N].bitcast(BF16)
                hi, mid = low[:, 0:N], low[:, N:2 * N]
                for c in range(CHUNKS):
                    dve.wait_ge(s["bc_bank"], c + 1)
                    chain(v.tensor_copy(part[0], ps[0:96, c, :]))
                    chain.wait()
                    chain(v.tensor_copy(hi, part[0]))
                    chain.wait()
                    chain(tt(part[1], part[0], hi, ALU.subtract))
                    chain.wait()
                    chain(v.tensor_copy(mid, part[1]))
                    chain.wait()
                    chain(tt(part[2], part[1], mid, ALU.subtract))
                    chain(v.tensor_copy(bc_rows[0:32, cols(c)], hi[0:32]))
                    chain(v.tensor_copy(bc_rows[32:64, cols(c)], mid[32:64]))
                    chain.wait()
                    v.tensor_copy(bc_rows[64:96, cols(c)], part[2][64:96]).then_inc(s["bcp_ready"], 1)
                chain.wait()
                dve.wait_ge(s["bcp_ready"], CHUNKS)
                dve.sem_inc(s["hs_done"], 2)
                carried = carry.rearrange("p (i n) -> p i n", i=2)
                with chain.each(CHUNKS, 32) as c:
                    with chain.each(8, 4) as m:
                        for nb in range(2):
                            step = 16 * c + 2 * m + nb
                            state = g[:, 11, 2 * nb * N:(2 * nb + 2) * N].rearrange("p (i n) -> p i n", i=2)
                            dve.wait_ge(s["da_ready"], 2 * step + 2)
                            dve.wait_ge(s["db_ready"], step + 3)
                            chain.wait()
                            for i in range(2):
                                at = slice((2 * nb + i) * N, (2 * nb + i + 1) * N)
                                ins = v.tensor_tensor_scan(state[:, i, :], g[:, 9, at], g[:, 10, at],
                                                           carry[:, bass.ds(2 * m + (16 * i + nb), 1)],
                                                           ALU.mult, ALU.add)
                                if i == 0:
                                    chain(ins)
                            ins.then_inc(s["hs_done"], 1)
                            hold(dve, s["hs_done"], step + 3)
                            chain(v.tensor_copy(carried[:, :, bass.ds(2 * m + nb, 1)], state[:, :, N - 1:N]))
                            dve.wait_ge(s["cb_bank"], step + 1)
                            dve.wait_ge(s["sum_done"], step + 1)
                            tt(tmp[:, 2 * nb * N:(2 * nb + 2) * N].rearrange("p (i n) -> p i n", i=2), state,
                               ps[:, 4 + nb:5 + nb, :].to_broadcast([P, 2, N])).then_inc(s["hc_ready"], 1)
                boundary(6)

            if LAYERS > 7:
                experts(7, 16, 8, 4, 2, 4, CHUNKS, 33)
                boundary(7)

            for c in range(CHUNKS):
                dve.wait_ge(s["x_ready"], LAYERS * CHUNKS + c + 1)
                tt(G(9, c), R(c), mean0[:, cols(c)], ALU.add).then_inc(s["sum_ready"], 1)


def build(nc, args):
    sandwich(nc, *args)


def kernel(**inputs):
    import ml_dtypes
    import numpy as _np
    import concourse.bacc as _bacc
    from concourse import mybir as _mybir
    from concourse.bass_utils import run_bass_kernel_spmd as _run

    a = {k: _np.asarray(v) for k, v in inputs.items()}

    def L(layer, name):
        return a[f"L{layer // 2}_{'attn' if layer % 2 == 0 else 'ffn'}_{name}"]

    def tiled(m):
        return m.reshape(-1, P, m.shape[1]).transpose(1, 0, 2).reshape(P, -1)

    def col(v):
        return v.reshape(-1, P).T

    def rows(m):
        return _np.concatenate([m, _np.zeros((P - m.shape[0], m.shape[1]), m.dtype)], 0)

    def all_rows(v):
        return _np.broadcast_to(v.reshape(1, -1), (P, v.size))

    def twice(m):
        return _np.concatenate([m, m], 0)

    def halves(m):
        return m.reshape(64, 8, 2).transpose(2, 0, 1).reshape(P, 8)

    ch = _np.arange(P)
    f32 = _np.float32
    head_sum = _np.stack([(ch[:, None] // 8 == ch[None] // 8) & (ch[None] % 8 == e) for e in range(8)], 1)
    head_mean = (ch[:, None] // 8 == ch[None] // 8) / 8.0

    def before(n):
        i = _np.arange(n)
        m = _np.zeros(64)
        m[:n * n] = (i[None] < i[:, None]).reshape(-1)
        return all_rows(m.astype(f32))

    wv2 = L(4 - 2, "wv").reshape(P, 16, 8)
    packed = [
        dict(kw=L(0, "att_kw").T, vw=L(0, "att_vw").T, rw=L(0, "att_rw").T, ow=L(0, "att_ow").T,
             frw=L(0, "f_rw").T, fkw=L(0, "f_kw").T, fvw=tiled(L(0, "f_vw").T),
             vec=_np.stack([L(0, n) for n in ("ln1_w", "ln1_b", "ln2_w", "ln2_b", "tmk", "tmv", "tmr",
                                              "time_first", "f_tmk", "f_tmr", "time_decay")]
                           + [_np.zeros(P, f32)], 1)),
        dict(win=_np.concatenate([L(1, "Win")] * 2, 1), wout=twice(L(1, "Wout")), w1=halves(L(1, "W1")),
             b1=halves(L(1, "b1")), w2=halves(L(1, "W2")), bin=twice(L(1, "bin_")[:, None]),
             b2=twice(L(1, "b2")[:, None]), bout=col(L(1, "bout"))),
        dict(wq=L(2, "wq"), wk=L(2, "wk"),
             wv=_np.stack([_np.repeat(wv2[:, :, e], 8, 1) for e in range(8)], 1).reshape(P, -1),
             wg1=L(2, "wg1"), wg2=rows(L(2, "wg2")), wo=L(2, "wo"), norm_w=col(L(2, "norm_w")),
             head_sum=head_sum.astype(f32).reshape(P, -1), head_mean=head_mean.astype(f32)),
        dict(s=_np.stack([_np.broadcast_to(L(3, n), (P,)) for n in ("s0", "s1", "s2")], 1)),
        dict(wv=L(4, "in_proj_weight")[2048:].reshape(8, P, P).transpose(1, 0, 2).reshape(P, -1),
             wo=tiled(L(4, "out_proj_weight").T), bv=col(L(4, "in_proj_bias")[2048:]),
             bo=col(L(4, "out_proj_bias"))),
        dict(router=L(5, "router_w").T, bias=all_rows(L(5, "e_bias")), before=before(8)),
        dict(wx=L(6, "in_proj_w")[:256].T, conv=all_rows(_np.ascontiguousarray(L(6, "conv_w")[:, 0, :].T)),
             wz=L(6, "in_proj_w")[256:].T,
             wbc=tiled(_np.concatenate([L(6, "x_proj_w").T] * 3, 1)),
             wdt=tiled(L(6, "dt_proj_w").T), wout=tiled(L(6, "out_proj_w").T), conv_b=col(L(6, "conv_b")),
             dt_b=col(L(6, "dt_proj_b")), a_log=tiled(L(6, "A_log")), d=col(L(6, "D_param"))),
        dict(router=L(7, "gate_w").T, bias=all_rows(L(7, "gate_bias")), before=before(4)),
    ]
    blocks = []
    for layer in range(8):
        for name, width in LAYOUT[layer]:
            block = packed[layer][name]
            assert block.shape == (P, width), (layer, name, block.shape)
            blocks.append(block)
    weights = _np.ascontiguousarray(_np.concatenate(blocks, 1))

    def pairs(gate, up, down):
        E, Hn, I = gate.shape
        w = [m.reshape(E // 2, 2, Hn, I).transpose(0, 2, 1, 3).reshape(E // 2, Hn, 2 * I) for m in (gate, up)]
        return _np.concatenate(w + [down.reshape(E // 2, 2 * I, Hn)], 2)

    def wide(m):
        return _np.concatenate([m, _np.zeros((P, P - m.shape[1]), m.dtype)], 1)

    shared5 = _np.concatenate([L(5, "SWg"), L(5, "SWu"), L(5, "SWd")], 1)[None]
    shared7 = _np.concatenate([wide(L(7, "ws1").T), wide(L(7, "ws3").T), rows(L(7, "ws2").T)], 1)[None]
    T_ = (0, 2, 1)
    moe0 = _np.concatenate([shared5, pairs(L(5, "Wg"), L(5, "Wu"), L(5, "Wd"))], 0)
    moe1 = _np.concatenate([shared7, pairs(L(7, "w1").transpose(T_), L(7, "w3").transpose(T_),
                                           L(7, "w2").transpose(T_))], 0)
    bools = _np.concatenate([L(3, "k0")[:P], L(3, "k0")[P:], tiled(L(3, "k1")), tiled(L(3, "k2"))], 1)
    eye = _np.eye(P)
    consts = _np.concatenate([eye, eye - 1.0 / P, _np.full((P, P), 1.0 / P)], 1).astype(f32)

    sel = _np.zeros((96, 48, P), ml_dtypes.bfloat16)
    for part in range(3):
        for n in range(32):
            sel[32 * part + n, n, :] = 1
        for q in range(16):
            sel[32 * part + 2 * q, 32 + q, :64] = 1
            sel[32 * part + 2 * q + 1, 32 + q, 64:] = 1
    theta = (10000.0 ** (-2.0 / P * _np.arange(P))).astype(f32)
    angle = (theta[:, None] * _np.arange(T, dtype=f32)[None]).astype(f32)
    rope = _np.stack([_np.cos(angle), _np.sin(angle)], 1).astype(f32)

    host = dict(x=a["L0_attn_x"].reshape(T, P), weights=weights, bools=_np.ascontiguousarray(bools).view(_np.uint32), moe0=moe0,
                moe1=moe1, consts=consts, selectors=sel, rope=rope)
    nc = _bacc.Bacc("TRN2", target_bir_lowering=False, num_devices=1)
    arrays, aps = {}, {}
    for name, m in host.items():
        m = _np.ascontiguousarray(m)
        arrays[f"in_{name}_dram"] = m
        aps[name] = nc.dram_tensor(f"in_{name}_dram", m.shape, _mybir.dt.from_np(m.dtype),
                                   kind="ExternalInput").ap()
    out = nc.dram_tensor("out_dram", (T, P), _mybir.dt.float32, kind="ExternalOutput").ap()
    sandwich(nc, aps["x"], out, aps["weights"], aps["bools"], aps["moe0"], aps["moe1"], aps["consts"],
             aps["selectors"], aps["rope"])
    r = _run(nc, [arrays], core_ids=[0])
    return r.results[0]["out_dram"].reshape(1, T, P)
```

```python
from contextlib import ExitStack, contextmanager

import concourse.bass as bass
import numpy as np
from concourse import mybir

P = 128
T = 2048
N = 512
CHUNKS = T // N
TILES = N // P
PAD = 4
LEAD = 3
F32 = mybir.dt.float32
F32R = mybir.dt.float32r
BF16 = mybir.dt.bfloat16
U8 = mybir.dt.uint8
ALU = mybir.AluOpType
ACT = mybir.ActivationFunctionType
AX_X = mybir.AxisListType.X
LAYERS = 8

NORMS = ["pre0", "ln1", "ln2", "post0", "pre1", "post1", "pre2", "rms", "post2", "pre3", "post3",
         "pre4", "post4", "pre5", "post5", "pre6", "post6", "pre7", "post7"]
NORM = {name: i for i, name in enumerate(NORMS)}
ACT_SQUARES = [n for n in NORMS if n.startswith("post") or n in ("ln2", "rms")]
POOL_SQUARES = [n for n in NORMS if n not in ACT_SQUARES]
BIG = 1e30
B_BANKS = (2, 3, 6, 7)

LAYOUT = [
    [("kw", 128), ("vw", 128), ("rw", 128), ("ow", 128), ("frw", 128), ("fkw", 512), ("fvw", 512),
     ("vec", 12)],
    [("win", 128), ("wout", 128), ("w1", 8), ("b1", 8), ("w2", 8), ("bin", 1), ("b2", 1), ("bout", 1)],
    [("wq", 128), ("wk", 128), ("wv", 1024), ("wg1", 8), ("wg2", 128), ("wo", 128), ("norm_w", 1),
     ("head_sum", 1024), ("head_mean", 128)],
    [("s", 3)],
    [("wv", 1024), ("wo", 1024), ("bv", 8), ("bo", 1)],
    [("router", 64), ("bias", 64), ("before", 64)],
    [("wx", 256), ("conv", 1024), ("wz", 256), ("wbc", 192), ("wdt", 512), ("wout", 256),
     ("conv_b", 2), ("dt_b", 2), ("a_log", 32), ("d", 2)],
    [("router", 16), ("bias", 16), ("before", 64)],
]
AT = []
for _cols in LAYOUT:
    _at, _o = {}, 0
    for _name, _w in _cols:
        _at[_name] = (_o, _o + _w)
        _o += _w
    AT.append(_at)
WIDTH = [sum(w for _, w in cols) for cols in LAYOUT]
PAIR = 3 * 128
DERIVED = 1024
ARENA = [4 * 1024, 4 * 1024]


def cols(c, off=0, n=N):
    return bass.ds(c * N + off, n) if not isinstance(c, int) else slice(c * N + off, c * N + off + n)


class Chain:

    def __init__(self, eng, sem):
        self.eng, self.sem, self.n, self.reg = eng, sem, 0, 0

    def __call__(self, ins):
        ins.then_inc(self.sem, 1)
        self.n += 1

    def wait(self, but=0):
        self.eng.wait_ge(self.sem, self.reg + (self.n - but))

    @contextmanager
    def each(self, count, per):
        start, reg = self.n, self.reg
        with self.eng.Fori(0, count) as i:
            self.reg = reg + i * per
            yield i
        assert self.n - start == per, (self.n - start, per)
        self.reg = reg
        self.n = start + count * per


def hold(eng, sem, value):
    if not isinstance(value, int) or value > 0:
        eng.wait_ge(sem, value)
        if not isinstance(value, int):
            eng.nop(nofuse=True)


def at_least(eng, sem, value):
    if not isinstance(value, int) or value > 0:
        eng.wait_ge(sem, value)


def sandwich(nc, x, out, weights, bools, moe0, moe1, consts, selectors, rope):
    ctx = ExitStack()
    with ctx:
        def sb(name, shape, dt=F32):
            return ctx.enter_context(nc.sbuf_tensor(name, shape, dt))

        names = """w_loaded bools_loaded sel_loaded consts_loaded x_loaded rope_loaded pair_loaded0 pair_loaded1
            out_stored y_ready x_ready h_ready centred sq_act sq_pool var_ready rstd_ready
            dve_chain act_chain pool_chain zeroed raw_ready
            h1_ready d_ready mix_ready k_bank v_bank r_bank kv_ready sr_ready pp_ready d12_ready
            p_ready d34_ready eb_ready ee_ready den_ready rd_ready rw_ready decay_ready ow_bank x1_ready
            fr_bank fk_bank relu_ready kk_ready fv_bank sr2_ready
            nam_s_bank nam_relu nam_done nam_setup nam_bias_bank nam_bias
            q_bank2 k_bank2 g1_bank g2_bank k2_ready sigq_ready q_used g1_ready gate_ready
            m_ready md_ready me_ready s_ready rs_ready kcs_ready vb_bank vb_used st_ready
            qm_ready qm_used og_ready nrm_ready wo_bank setup2
            f_setup a1_bank a1_relu a2_bank a2_relu a3_bank
            comb_bank comb_ready l2_bank
            lg_bank lg_ready sc_bank parts_ready ct_bank ct_ready
            g_bank u_bank c_bank sg_ready t_ready hid_ready e_done
            conv_setup a_ready xa_bank xa_ready z_bank z_ready dt_bank dt_ready dl_ready du_ready bc_bank bcp_ready
            bb_bank cb_bank bs_ready da_ready db_ready hs_done hc_ready sum_done carried
            x_hi_ready x_split gu_hi_ready gu_split d_hi_ready d_split hh_ready hl_ready
            yt_ready yg_ready mo_bank sum_ready back_ready""".split()
        s = {n: ctx.enter_context(nc.semaphore(n)) for n in names}

        resid = sb("resid", [P, T])
        mean0 = sb("mean0", [P, T])
        normed = sb("normed", [P, LEAD + T + 1])
        y = sb("y", [P, T])
        sq = sb("sq", [P, T])
        rstd = sb("rstd", [P, T])
        tmp = sb("tmp", [P, T])
        with nc.sbuf_tensor("g", [P, 13, T + PAD], F32) as g:
            pass
        parts = sb("parts", [P, 13, T + PAD], F32R)
        arena = [sb(f"arena{i}", [P, ARENA[i]]) for i in range(2)]
        kbool_words = arena[1][:, 3100:3100 + 896].bitcast(mybir.dt.uint32)
        kbool = arena[1][:, 3100:3100 + 896].bitcast(U8)
        const = sb("const", [P, 3 * 128])
        sel = sb("sel", [96, 48, 128], BF16)
        ident_bf = sb("ident_bf", [P, P], BF16)
        small = sb("small", [P, 64])
        carry = sb("carry", [P, 32])
        ps = ctx.enter_context(nc.psum_tensor("ps", [P, 8, N], F32))

        ident, centring, averaging = (const[:, i * 128:(i + 1) * 128] for i in range(3))
        sel_bc, sel_coef = sel[:, 0:32, :], sel[:, 32:48, :]

        def W(layer, name, a=0, b=None):
            lo, hi = AT[layer][name]
            return arena[layer % 2][:, lo + a:(hi if b is None else lo + b)]

        def derived(layer, a, b):
            return arena[layer % 2][:, WIDTH[layer] + a:WIDTH[layer] + b]

        def G(i, c, off=0, n=N):
            return g[:, i, cols(c, off, n)]

        def turned(a, n_experts):
            per_bank = N // n_experts
            at = (a % per_bank) * n_experts
            return ps[:, 4 + a // per_bank, at:at + n_experts]

        def two_of(a, b, k):
            return g[:, a if k % 4 < 2 else b, 2 * (k % 2) * N:2 * (k % 2 + 1) * N].rearrange("p (r n) -> p r n", r=2)

        def H(c):
            return normed[:, cols(c, LEAD)]

        nam_wout = [derived(1, j * 128, (j + 1) * 128) for j in range(8)]
        nam_b1, nam_bout = small[:, 0:8], small[:, 8:9]
        scales = small[:, 9:12]
        comb_bias = small[:, 12:13]
        one = small[:, 13:14]
        eps5, eps6 = small[:, 49:50], small[:, 50:51]
        ffn_w = arena[1][:, 16:16 + 3072]
        comb = derived(4, 0, 128)
        wo_normed = derived(2, 0, 128)
        neg_a = small[:, 16:48]
        diag_d = g[:, 12, 1536:1792].rearrange("p (i n) -> p i n", i=2)
        conv_w = derived(6, 0, 1024).rearrange("p (j n) -> p j n", j=4)
        sc_rows = g[:, 0, 0:T]
        coef_parts = g[:, 3, 0:1536].bitcast(BF16).rearrange("p (a t r) -> p a t r", a=CHUNKS * TILES, t=2)
        coef_rows = g[0:96, 4, 0:T].bitcast(BF16).rearrange("p (t n) -> p t n", t=2)
        bc_rows = g[0:96, 12, 0:1536].bitcast(BF16)
        pair_w = [g[:, 7, i * PAIR:(i + 1) * PAIR] for i in range(2)]
        x_hi, x_lo, hid_hi, hid_lo = (parts[:, k, 0:T] for k in (8, 9, 10, 11))
        w_hi = [parts[:, 12, 2 * i * PAIR:(2 * i + 1) * PAIR] for i in range(2)]
        w_lo = [parts[:, 12, (2 * i + 1) * PAIR:2 * (i + 1) * PAIR] for i in range(2)]

        x_tiles = x.rearrange("(c a p) f -> p c a f", a=TILES, p=P)
        out_tiles = out.rearrange("(c a p) f -> p c a f", a=TILES, p=P)
        x_in = g[:, 11:13, 0:1024]

        block = ctx.enter_context(nc.Block())

        @block.sync
        def _(sp):
            for c in range(CHUNKS):
                sp.dma_start(x_in[:, c // 2, (c % 2) * 512:(c % 2 + 1) * 512]
                             .rearrange("p (a f) -> p a f", a=TILES), x_tiles[:, c]).then_inc(s["x_loaded"], 16)
                if c == 0:
                    sp.dma_start(const[:, :], consts[:, :]).then_inc(s["consts_loaded"], 16)
            lo = 0
            for layer in range(LAYERS):
                if layer >= 2:
                    sp.wait_ge(s["y_ready"], CHUNKS * layer)
                sp.dma_start(arena[layer % 2][:, 0:WIDTH[layer]],
                             weights[:, lo:lo + WIDTH[layer]]).then_inc(s["w_loaded"], 16)
                sp.wait_ge(s["w_loaded"], 16 * (layer + 1))
                lo += WIDTH[layer]
                if layer == 3:
                    sp.dma_start(kbool_words, bools[:, :]).then_inc(s["bools_loaded"], 16)
                if layer == 4:
                    sp.dma_start(sel[:, :, :], selectors[:, :, :]).then_inc(s["sel_loaded"], 16)
                if layer == 2:
                    sp.dma_start(g[:, 10:12, 0:T], rope[:, :, :]).then_inc(s["rope_loaded"], 16)
                for moe_layer, dram, pairs, first in ((5, moe0, 32, 0), (7, moe1, 8, 33)):
                    if layer != moe_layer:
                        continue
                    if moe_layer == 7:
                        sp.wait_ge(s["yg_ready"], CHUNKS)
                    sp.dma_start(pair_w[1], dram[0, :, :]).then_inc(s["pair_loaded1"], 16)
                    sp.dma_start(pair_w[0], dram[1, :, :]).then_inc(s["pair_loaded0"], 16)
                    with sp.Fori(0, pairs // 2 - 1) as i:
                        for k in (0, 1):
                            sp.wait_ge(s["d_split"], 2 * i + (first + 1 + k))
                            sp.dma_start(pair_w[1 - k], dram[bass.ds(2 * i + 2 + k, 1), :, :]
                                         .rearrange("a p n -> p (a n)"))\
                              .then_inc(s["pair_loaded1" if k == 0 else "pair_loaded0"], 16)
                    sp.wait_ge(s["d_split"], first + pairs - 1)
                    sp.dma_start(pair_w[1], dram[pairs, :, :]).then_inc(s["pair_loaded1"], 16)
            for c in range(CHUNKS):
                sp.wait_ge(s["back_ready"], c + 1)
                sp.dma_start(out_tiles[:, c], g[:, 10, cols(c)].rearrange("p (a f) -> p a f", a=TILES))\
                  .then_inc(s["out_stored"], 16)
            sp.wait_ge(s["out_stored"], 16 * CHUNKS)

        @block.tensor
        def _(pe):
            def mm(o, lhsT, rhs, start=True, stop=True, **kw):
                return nc.tensor.matmul(o, lhsT, rhs, start=start, stop=stop, **kw)

            def centre(boundary, src, bank, ready="y_ready"):
                for c in range(CHUNKS):
                    pe.wait_ge(s[ready], boundary * CHUNKS + c + 1)
                    mm(ps[:, bank + c, :], centring, src(c)).then_inc(s["centred"], 1)

            def variance(name, bank=4, matrix=averaging):
                by = "sq_act" if name in ACT_SQUARES else "sq_pool"
                k = (ACT_SQUARES if name in ACT_SQUARES else POOL_SQUARES).index(name)
                for c in range(CHUNKS):
                    pe.wait_ge(s[by], k * CHUNKS + c + 1)
                    mm(ps[:, bank + c, :], matrix, sq[:, cols(c)]).then_inc(s["var_ready"], 1)

            def boundary(layer):
                centre(layer + 1, lambda c: y[:, cols(c)], 0)
                variance(f"post{layer}")
                if layer + 1 < LAYERS:
                    variance(f"pre{layer + 1}")

            def h(layer, c):
                pe.wait_ge(s["h_ready"], layer * CHUNKS + c + 1)

            pe.wait_ge(s["consts_loaded"], 16)
            for c in range(CHUNKS):
                pe.wait_ge(s["x_loaded"], 16 * CHUNKS)
                for a in range(TILES):
                    last = nc.tensor.transpose(ps[:, c, a * P:(a + 1) * P],
                                               x_in[:, c // 2, (c % 2) * 512 + a * P:(c % 2) * 512 + (a + 1) * P],
                                               ident)
                last.then_inc(s["raw_ready"], 1)
            centre(0, lambda c: y[:, cols(c)], 4)
            variance("pre0", 0)
            variance("ln1", 0)

            pe.wait_ge(s["w_loaded"], 16)
            for c in range(CHUNKS):
                pe.wait_ge(s["mix_ready"], c + 1)
                mm(ps[:, c, :], W(0, "kw"), G(2, c)).then_inc(s["k_bank"], 1)
                mm(ps[:, 4 + c, :], W(0, "vw"), G(3, c)).then_inc(s["v_bank"], 1)
            for c in range(CHUNKS):
                pe.wait_ge(s["kv_ready"], c + 1)
                mm(ps[:, c, :], W(0, "rw"), G(4, c)).then_inc(s["r_bank"], 1)
            for c in range(CHUNKS):
                pe.wait_ge(s["rw_ready"], c + 1)
                mm(ps[:, c, :], W(0, "ow"), G(4, c)).then_inc(s["ow_bank"], 1)
            for c in range(CHUNKS):
                pe.wait_ge(s["x1_ready"], c + 1)
                mm(ps[:, 4 + c, :], centring, G(5, c)).then_inc(s["centred"], 1)
            variance("ln2", 0)
            for c in range(CHUNKS):
                pe.wait_ge(s["mix_ready"], CHUNKS + c + 1)
                mm(ps[:, c, :], W(0, "frw"), G(4, c)).then_inc(s["fr_bank"], 1)
            pe.wait_ge(s["sr2_ready"], CHUNKS)
            for c in range(CHUNKS):
                pe.wait_ge(s["relu_ready"], 4 * c)
                for m in range(4):
                    mm(ps[:, m, :], W(0, "fkw", m * 128, m * 128 + 128), G(2, c)).then_inc(s["fk_bank"], 1)
                for m in range(4):
                    pe.wait_ge(s["kk_ready"], 4 * c + m + 1)
                    last = mm(ps[:, 4 + c, :], W(0, "fvw", m * 128, m * 128 + 128),
                              g[:, 7, m * N:(m + 1) * N], m == 0, m == 3)
                last.then_inc(s["fv_bank"], 1)
            boundary(0)

            if LAYERS > 1:
                pe.wait_ge(s["w_loaded"], 32)
                pe.wait_ge(s["nam_setup"], 1)
                h(1, 3)
                mm(ps[:, 7, 0:1], W(1, "wout")[0:64], W(1, "b2")[0:64]).then_inc(s["nam_bias_bank"], 1)
                for c in range(CHUNKS):
                    h(1, c)
                    mm(ps[:, c, :], W(1, "win"), H(c)).then_inc(s["nam_s_bank"], 1)
                pe.wait_ge(s["nam_bias"], 1)
                for c in range(CHUNKS):
                    for j in range(8):
                        pe.wait_ge(s["nam_relu"], 8 * c + j + 1)
                        last = mm(ps[:, 4 + c, :], nam_wout[j], g[:, j // 4, (j % 4) * N:(j % 4 + 1) * N],
                                  j == 0, j == 7)
                    last.then_inc(s["nam_done"], 1)
                boundary(1)

            if LAYERS > 2:
                pe.wait_ge(s["w_loaded"], 48)
                for c in range(CHUNKS):
                    h(2, c)
                    mm(ps[:, c, :], W(2, "wk"), H(c)).then_inc(s["k_bank2"], 1)
                    mm(ps[:, 4 + c, :], W(2, "wq"), H(c)).then_inc(s["q_bank2"], 1)
                for c in range(CHUNKS):
                    pe.wait_ge(s["k2_ready"], c + 1)
                    mm(ps[0:8, c, :], W(2, "wg1"), H(c)).then_inc(s["g1_bank"], 1)
                for c in range(CHUNKS):
                    pe.wait_ge(s["q_used"], c + 1)
                    pe.wait_ge(s["g1_ready"], c + 1)
                    mm(ps[:, 4 + c, :], W(2, "wg2")[0:8], tmp[0:8, cols(c)]).then_inc(s["g2_bank"], 1)
                pe.wait_ge(s["gate_ready"], CHUNKS)

                def spread_v(e, c):
                    pe.wait_ge(s["vb_used"], 8 * c + e + 1)
                    mm(ps[:, e % 4, :], W(2, "wv", e * 128, e * 128 + 128), H(c)).then_inc(s["vb_bank"], 1)

                def features(c, more):
                    for e in range(8):
                        if e < 5 or more:
                            spread_v((e + 3) % 8, c + (e + 3) // 8)
                        pe.wait_ge(s["qm_ready"], 8 * c + e + 5)
                        for r in range(2):
                            last = mm(ps[:, 4 + c, :] if isinstance(c, int) else
                                      ps[:, bass.ds(c + 4, 1), :].rearrange("p a n -> p (a n)"),
                                      W(2, "head_sum", e * 128, e * 128 + 128),
                                      g[:, 2, (2 * (e % 2) + r) * N:(2 * (e % 2) + r + 1) * N],
                                      e == 0 and r == 0, e == 7 and r == 1)
                        last.then_inc(s["qm_used"], 1)

                pe.sem_inc(s["qm_used"], 2)
                for e in range(3):
                    spread_v(e, 0)
                with pe.Fori(0, CHUNKS - 1) as c:
                    features(c, True)
                features(CHUNKS - 1, False)
                variance("rms", 0, W(2, "head_mean"))
                pe.wait_ge(s["setup2"], 1)
                for c in range(CHUNKS):
                    pe.wait_ge(s["nrm_ready"], c + 1)
                    mm(ps[:, 4 + c, :], wo_normed, G(5, c)).then_inc(s["wo_bank"], 1)
                boundary(2)

            if LAYERS > 3:
                pe.wait_ge(s["f_setup"], 1)
                h(3, 3)
                for c in range(CHUNKS):
                    pe.wait_ge(s["a1_relu"], 4 * c)
                    pe.wait_ge(s["y_ready"], 4 * CHUNKS + c)
                    for m in range(4):
                        mm(ps[:, m, :], ffn_w[:, m * 128:m * 128 + 128], H(c)).then_inc(s["a1_bank"], 1)
                    pe.wait_ge(s["a2_relu"], 4 * c)
                    for m in range(4):
                        for k in range(4):
                            if m == 0:
                                pe.wait_ge(s["a1_relu"], 4 * c + k + 1)
                            last = mm(ps[:, 4 + m, :],
                                      ffn_w[:, 512 + k * 512 + m * 128:512 + k * 512 + m * 128 + 128],
                                      g[:, 0, k * N:(k + 1) * N], k == 0, k == 3)
                        last.then_inc(s["a2_bank"], 1)
                    for k in range(4):
                        pe.wait_ge(s["a2_relu"], 4 * c + k + 1)
                        last = mm(ps[:, c, :], ffn_w[:, 2560 + k * 128:2560 + k * 128 + 128],
                                  g[:, 1, k * N:(k + 1) * N], k == 0, k == 3)
                    last.then_inc(s["a3_bank"], 1)
                if LAYERS > 4:
                    pe.wait_ge(s["w_loaded"], 80)
                    for k in range(8):
                        mm(ps[:, 7, 0:128], W(4, "wv", k * 128, k * 128 + 128),
                           W(4, "wo", k * 128, k * 128 + 128), k == 0, k == 7)
                    for k in range(8):
                        last = mm(ps[:, 6, 0:1], W(4, "wo", k * 128, k * 128 + 128),
                                  W(4, "bv", k, k + 1), k == 0, k == 7)
                    last.then_inc(s["comb_bank"], 1)
                    pe.wait_ge(s["comb_ready"], 1)
                boundary(3)

            if LAYERS > 4:
                for c in range(CHUNKS):
                    h(4, c)
                    mm(ps[:, c, :], comb, H(c)).then_inc(s["l2_bank"], 1)
                boundary(4)

            def experts(layer, n_experts, pairs, order, r0):
                pe.wait_ge(s["w_loaded"], 16 * (layer + 1))
                pe.wait_ge(s["sel_loaded"], 16)
                for c in range(CHUNKS):
                    h(layer, c)
                    mm(ps[0:n_experts, c, :], W(layer, "router"), H(c)).then_inc(s["lg_bank"], 1)
                pe.wait_ge(s["x_ready"], CHUNKS * (layer + 1))
                for c in range(CHUNKS):
                    pe.wait_ge(s["lg_ready"], CHUNKS * order + c + 1)
                    for a in range(c * TILES, (c + 1) * TILES):
                        last = nc.tensor.transpose(turned(a, n_experts), sc_rows[0:n_experts, a * P:(a + 1) * P],
                                                   ident[0:n_experts, 0:n_experts])
                last.then_inc(s["sc_bank"], 1)
                pe.wait_ge(s["parts_ready"], order + 1)
                for c in range(CHUNKS):
                    for t in range(2):
                        for a in range(TILES):
                            last = nc.tensor.transpose(
                                ps[0:96, 4 + c, :].bitcast(BF16)[:, t * N + a * P:t * N + (a + 1) * P],
                                coef_parts[:, c * TILES + a, t, :], ident_bf[:, :])
                    last.then_inc(s["ct_bank"], 1)
                pe.wait_ge(s["ct_ready"], CHUNKS * (order + 1))
                pe.wait_ge(s["x_split"], CHUNKS * (order + 1))

                def product(o, slot, at, hi, lo, start=True, stop=True):
                    hi_w, lo_w = w_hi[slot][:, at:at + 128], w_lo[slot][:, at:at + 128]
                    mm(o, hi_w, hi, start, False, skip_group_check=True)
                    mm(o, hi_w, lo, False, False, skip_group_check=True)
                    return mm(o, lo_w, hi, False, stop, skip_group_check=True)

                def turn(n, slot, c, coef=None, down=None):
                    gb = 4 if c % 2 == 0 else 7
                    at_least(pe, s["sg_ready"], n - 1)
                    product(ps[:, gb, :], slot, 0, x_hi[:, cols(c)], x_lo[:, cols(c)]).then_inc(s["g_bank"], 1)
                    at_least(pe, s["t_ready"], n)
                    product(ps[:, 5, :], slot, 128, x_hi[:, cols(c)], x_lo[:, cols(c)]).then_inc(s["u_bank"], 1)
                    if down is not None:
                        down_product(n - 3, (c + 1) % 4, *down)
                    if coef is not None:
                        t, q = coef
                        pe.wait_ge(s["hid_ready"], n)
                        mm(ps[:, 6, :], sel_coef[:, q, :].rearrange("p a n -> p (a n)"),
                           coef_rows[:, t, cols(c)]).then_inc(s["c_bank"], 1)

                def down_product(n, c, slot, start=False, stop=False):
                    if c == 0:
                        pe.wait_ge(s["d_split"], n // 4 + 1 if isinstance(n, int) else down_round[0])
                    pe.wait_ge(s["hl_ready"], n + 1)
                    product(ps[:, c, :], slot, 256, hid_hi[:, cols(c)], hid_lo[:, cols(c)], start, stop)\
                        .then_inc(s["e_done"], 1)

                down_round = [None]

                def round_of(r, slot, coef, before, stop=False):
                    pe.wait_ge(s["gu_split"], r + 1)
                    down_round[0] = r + 1
                    for c in range(CHUNKS):
                        down = (slot, before is None, stop) if c == 3 else before
                        turn(4 * r + c, slot, c, coef, down)

                round_of(r0, 1, None, None)
                round_of(r0 + 1, 0, (0, bass.ds(0, 1)), (1, True))
                with pe.Fori(0, pairs // 2 - 1) as i:
                    for k in (0, 1):
                        round_of(2 * i + (r0 + 2 + k), 1 - k, (1 - k, bass.ds(i + k, 1)), (k,))
                round_of(r0 + pairs, 1, (1, bass.ds(pairs // 2 - 1, 1)), (0,), True)
                for c in range(1, CHUNKS):
                    down_product(4 * (r0 + pairs) + c, c, 1, False, True)

            if LAYERS > 5:
                experts(5, 64, 32, 0, 0)
                boundary(5)

            if LAYERS > 6:
                pe.wait_ge(s["conv_setup"], 1)
                for c in range(CHUNKS):
                    h(6, c)
                    for i in range(2):
                        for j in range(4):
                            last = mm(ps[:, 4 * i + c, :], conv_w[:, j, i * 128:i * 128 + 128],
                                      normed[:, cols(c, j)], j == 0, j == 3)
                        last.then_inc(s["xa_bank"], 1)
                for c in range(CHUNKS):
                    pe.wait_ge(s["xa_ready"], 2 * c + 2)
                    for i in range(2):
                        mm(ps[:, 4 * i + c, :], W(6, "wz", i * 128, i * 128 + 128), H(c)).then_inc(s["z_bank"], 1)
                for c in range(CHUNKS):
                    pe.wait_ge(s["z_ready"], 2 * c + 2)
                    for i in range(2):
                        for k in range(2):
                            last = mm(ps[:, 4 * i + c, :],
                                      W(6, "wdt", k * 256 + i * 128, k * 256 + i * 128 + 128), G(k, c),
                                      k == 0, k == 1)
                        last.then_inc(s["dt_bank"], 1)
                for c in range(CHUNKS):
                    pe.wait_ge(s["dt_ready"], 2 * c + 2)
                    for k in range(2):
                        last = mm(ps[0:96, c, :], W(6, "wbc", k * 96, k * 96 + 96), G(k, c), k == 0, k == 1)
                    last.then_inc(s["bc_bank"], 1)
                pe.wait_ge(s["bcp_ready"], CHUNKS)

                def row(n):
                    return sel_bc[:, bass.ds(n, 1), :].rearrange("p a n -> p (a n)")

                def spread_b(k, n, c, step):
                    at_least(pe, s["bs_ready"], step - 3)
                    mm(ps[:, B_BANKS[k], :], row(n), bc_rows[:, cols(c)]).then_inc(s["bb_bank"], 1)

                def spread_c(nb, n, c, step):
                    at_least(pe, s["hc_ready"], step - 1)
                    mm(ps[:, 4 + nb, :], row(n + 16), bc_rows[:, cols(c)]).then_inc(s["cb_bank"], 1)

                def sum_n(nb, step, stop=False):
                    pe.wait_ge(s["hc_ready"], step + 1)
                    for i in range(2):
                        last = mm(ps[:, i, :], ident, tmp[:, (2 * nb + i) * N:(2 * nb + i + 1) * N], False, stop,
                                  skip_group_check=True)
                    last.then_inc(s["sum_done"], 1)

                for k in range(4):
                    spread_b(k, k, 0, k)
                spread_c(0, 0, 0, 0)
                pe.sem_inc(s["sum_done"], 2)
                with pe.Fori(0, CHUNKS) as c:
                    def spread_ahead(k, n):
                        spread_b(k, n + 4, c, 16 * c + n + 4)
                        spread_c((k + 1) % 2, n + 1, c, 16 * c + n + 1)

                    spread_ahead(0, 0)
                    pe.wait_ge(s["yt_ready"], 2 * c + 1)
                    for i in range(2):
                        mm(ps[:, i, :], diag_d[:, i, :], G(i, c), True, False, skip_group_check=True)
                    sum_n(0, 16 * c)
                    for k in range(1, 4):
                        spread_ahead(k, k)
                        sum_n(k % 2, 16 * c + k)
                    with pe.Fori(1, 3) as m:
                        for k in range(4):
                            spread_ahead(k, 4 * m + k)
                            sum_n(k % 2, 16 * c + 4 * m + k)
                    for k in range(4):
                        spread_b(k, k, c + 1, 16 * c + 16 + k)
                        spread_c((k + 1) % 2, 13 + k if k < 3 else 0, c + k // 3, 16 * c + 13 + k)
                        sum_n(k % 2, 16 * c + 12 + k, True)
                pe.wait_ge(s["yt_ready"], 2 * CHUNKS + 1)
                for c in range(CHUNKS):
                    pe.wait_ge(s["yg_ready"], c + 1)
                    for k in range(2):
                        last = mm(ps[:, c, :], W(6, "wout", k * 128, k * 128 + 128), G(2 + k, c), k == 0, k == 1)
                    last.then_inc(s["mo_bank"], 1)
                boundary(6)

            if LAYERS > 7:
                experts(7, 16, 8, 1, 33)
                boundary(7)

            for c in range(CHUNKS):
                pe.wait_ge(s["sum_ready"], c + 1)
                for a in range(TILES):
                    last = nc.tensor.transpose(ps[:, 4 + c, a * P:(a + 1) * P],
                                               g[:, 9, c * N + a * P:c * N + (a + 1) * P], ident)
                last.then_inc(s["raw_ready"], 1)

        @block.scalar
        def _(act):
            chain = Chain(act, s["act_chain"])

            def f(o, i, func, **kw):
                return nc.scalar.activation(o, i, func, **kw)

            def use_log_exp():
                act.preload_act_table_set("natural_log_exp_and_others")

            def square(name, src, sem, base):
                k = ACT_SQUARES.index(name)
                for c in range(CHUNKS):
                    act.wait_ge(s[sem], base + c + 1)
                    f(sq[:, cols(c)], src(c), ACT.Square).then_inc(s["sq_act"], 1)

            def rstd_of(name, eps, bank=4):
                k = NORM[name]
                for c in range(CHUNKS):
                    act.wait_ge(s["var_ready"], k * CHUNKS + c + 1)
                    chain(f(rstd[:, cols(c)], ps[:, bank + c, :], ACT.Ln, bias=eps))
                    chain.wait()
                    f(rstd[:, cols(c)], rstd[:, cols(c)], ACT.Exp, scale=-0.5).then_inc(s["rstd_ready"], 1)

            def boundary(layer):
                square(f"post{layer}", lambda c: ps[:, c, :], "centred", CHUNKS * (layer + 2))
                rstd_of(f"post{layer}", eps5)
                if layer + 1 < LAYERS:
                    rstd_of(f"pre{layer + 1}", eps5)

            def evacuate(sem, bank, **kw):
                for c in range(CHUNKS):
                    act.wait_ge(s[sem], c + 1)
                    f(y[:, cols(c)], ps[:, bank + c, :], ACT.Identity, **kw).then_inc(s["y_ready"], 1)

            use_log_exp()
            act.wait_ge(s["zeroed"], 1)
            for c in range(CHUNKS):
                act.wait_ge(s["raw_ready"], c + 1)
                f(y[:, cols(c)], ps[:, c, :], ACT.Copy).then_inc(s["y_ready"], 1)
            rstd_of("pre0", eps5, 0)
            rstd_of("ln1", eps5, 0)

            act.wait_ge(s["w_loaded"], 16)
            f(small[:, 15:16], W(0, "vec", 10, 11), ACT.Exp).then_inc(s["decay_ready"], 1)
            for c in range(CHUNKS):
                act.wait_ge(s["k_bank"], c + 1)
                f(G(5, c), ps[:, c, :], ACT.Copy)
                act.wait_ge(s["v_bank"], c + 1)
                f(G(6, c), ps[:, 4 + c, :], ACT.Copy).then_inc(s["kv_ready"], 1)
            for c in range(CHUNKS):
                act.wait_ge(s["r_bank"], c + 1)
                f(G(7, c), ps[:, c, :], ACT.Sigmoid).then_inc(s["sr_ready"], 1)
            use_log_exp()
            for c in range(CHUNKS):
                act.wait_ge(s["d12_ready"], c + 1)
                f(G(11, c), G(11, c), ACT.Exp, bias=small[:, 14:15])
                f(G(12, c), G(12, c), ACT.Exp).then_inc(s["eb_ready"], 1)
                act.wait_ge(s["d34_ready"], c + 1)
                f(G(1, c), G(1, c), ACT.Exp)
                f(G(2, c), G(2, c), ACT.Exp, bias=W(0, "vec", 7, 8)).then_inc(s["ee_ready"], 1)
            for c in range(CHUNKS):
                act.wait_ge(s["den_ready"], c + 1)
                chain(f(y[:, cols(c)], y[:, cols(c)], ACT.Ln))
                chain.wait()
                f(y[:, cols(c)], y[:, cols(c)], ACT.Exp, scale=-1.0).then_inc(s["rd_ready"], 1)
            square("ln2", lambda c: ps[:, 4 + c, :], "centred", CHUNKS)
            rstd_of("ln2", eps5, 0)
            for c in range(CHUNKS):
                act.wait_ge(s["fr_bank"], c + 1)
                f(G(8, c), ps[:, c, :], ACT.Sigmoid).then_inc(s["sr2_ready"], 1)
            use_log_exp()
            for c in range(CHUNKS):
                act.wait_ge(s["kk_ready"], 4 * c)
                for m in range(4):
                    act.wait_ge(s["fk_bank"], 4 * c + m + 1)
                    f(g[:, 6, m * N:(m + 1) * N], ps[:, m, :], ACT.Relu).then_inc(s["relu_ready"], 1)
            boundary(0)

            if LAYERS > 1:
                act.wait_ge(s["nam_bias_bank"], 1)
                f(nam_bout, ps[:, 7, 0:1], ACT.Identity, bias=W(1, "bout")).then_inc(s["nam_bias"], 1)
                for c in range(CHUNKS):
                    act.wait_ge(s["nam_s_bank"], c + 1)
                    act.wait_ge(s["nam_done"], c)
                    for j in range(8):
                        f(g[:, j // 4, (j % 4) * N:(j % 4 + 1) * N], ps[:, c, :], ACT.Relu,
                          scale=W(1, "w1", j, j + 1), bias=nam_b1[:, j:j + 1]).then_inc(s["nam_relu"], 1)
                act.wait_ge(s["nam_bias"], 1)
                evacuate("nam_done", 4, bias=nam_bout)
                boundary(1)

            if LAYERS > 2:
                for c in range(CHUNKS):
                    act.wait_ge(s["k_bank2"], c + 1)
                    f(G(0, c), ps[:, c, :], ACT.Copy).then_inc(s["k2_ready"], 1)
                    act.wait_ge(s["q_bank2"], c + 1)
                    f(G(5, c), ps[:, 4 + c, :], ACT.Sigmoid).then_inc(s["sigq_ready"], 1)
                for c in range(CHUNKS):
                    act.wait_ge(s["g1_bank"], c + 1)
                    f(tmp[0:8, cols(c)], ps[0:8, c, :], ACT.Copy).then_inc(s["g1_ready"], 1)
                for c in range(CHUNKS):
                    act.wait_ge(s["g2_bank"], c + 1)
                    f(G(12, c), ps[:, 4 + c, :], ACT.Sigmoid).then_inc(s["gate_ready"], 1)
                use_log_exp()
                for c in range(CHUNKS):
                    act.wait_ge(s["md_ready"], c + 1)
                    f(G(3, c), G(3, c), ACT.Exp)
                    f(G(4, c), G(4, c), ACT.Exp).then_inc(s["me_ready"], 1)
                for c in range(CHUNKS):
                    act.wait_ge(s["s_ready"], c + 1)
                    chain(f(rstd[:, cols(c)], G(2, c, 1), ACT.Ln))
                    chain.wait()
                    f(rstd[:, cols(c)], rstd[:, cols(c)], ACT.Exp, scale=-1.0).then_inc(s["rs_ready"], 1)
                square("rms", lambda c: G(4, c), "og_ready", 0)
                rstd_of("rms", eps6, 0)
                evacuate("wo_bank", 4)
                boundary(2)

            if LAYERS > 3:
                act.wait_ge(s["f_setup"], 1)
                for c in range(CHUNKS):
                    for m in range(4):
                        act.wait_ge(s["a1_bank"], 4 * c + m + 1)
                        f(g[:, 0, m * N:(m + 1) * N], ps[:, m, :], ACT.Relu, scale=scales[:, 0:1])\
                            .then_inc(s["a1_relu"], 1)
                    for m in range(4):
                        act.wait_ge(s["a2_bank"], 4 * c + m + 1)
                        f(g[:, 1, m * N:(m + 1) * N], ps[:, 4 + m, :], ACT.Relu, scale=scales[:, 1:2])\
                            .then_inc(s["a2_relu"], 1)
                    act.wait_ge(s["a3_bank"], c + 1)
                    f(y[:, cols(c)], ps[:, c, :], ACT.Copy, scale=scales[:, 2:3]).then_inc(s["y_ready"], 1)
                if LAYERS > 4:
                    act.wait_ge(s["comb_bank"], 1)
                    f(comb, ps[:, 7, 0:128], ACT.Copy)
                    f(comb_bias, ps[:, 6, 0:1], ACT.Identity, bias=W(4, "bo")).then_inc(s["comb_ready"], 1)
                boundary(3)

            if LAYERS > 4:
                act.wait_ge(s["comb_ready"], 1)
                evacuate("l2_bank", 0, bias=comb_bias)
                boundary(4)

            def experts(layer, n_experts, pairs, order, r0):
                base1, base0 = (0, 0) if layer == 5 else (17, 16)
                for c in range(CHUNKS):
                    act.wait_ge(s["h_ready"], CHUNKS * layer + c + 1)
                    f(x_hi[:, cols(c)], H(c), ACT.Copy).then_inc(s["x_hi_ready"], 1)
                    act.wait_ge(s["lg_bank"], CHUNKS * order + c + 1)
                    f(sc_rows[0:n_experts, cols(c)], ps[0:n_experts, c, :], ACT.Sigmoid).then_inc(s["lg_ready"], 1)

                def gate_up_hi(r, slot, loaded):
                    act.wait_ge(s[f"pair_loaded{slot}"], loaded)
                    at_least(act, s["u_bank"], 4 * r - 4)
                    f(w_hi[slot][:, 0:256], pair_w[slot][:, 0:256], ACT.Copy).then_inc(s["gu_hi_ready"], 1)

                def down_hi(r, slot):
                    at_least(act, s["e_done"], 4 * r - 4)
                    f(w_hi[slot][:, 256:384], pair_w[slot][:, 256:384], ACT.Copy).then_inc(s["d_hi_ready"], 1)

                def silu(n, par):
                    act.wait_ge(s["g_bank"], n + 1)
                    at_least(act, s["t_ready"], n - 1)
                    f(g[:, 5, par * N:(par + 1) * N], ps[:, 4 if par == 0 else 7, :], ACT.Silu)\
                        .then_inc(s["sg_ready"], 1)

                def hidden_hi(n, c):
                    act.wait_ge(s["hid_ready"], n + 1)
                    at_least(act, s["e_done"], n - 3)
                    f(hid_hi[:, cols(c)], g[:, 6, (c % 2) * N:(c % 2 + 1) * N], ACT.Copy).then_inc(s["hh_ready"], 1)

                def round_of(r, slot, following=None):
                    for c in range(CHUNKS):
                        silu(4 * r + c, c % 2)
                        if c or not isinstance(r, int) or r > r0:
                            hidden_hi(4 * r + (c - 1), (c - 1) % 4)
                        if following is not None and c == 0:
                            gate_up_hi(r + 1, 1 - slot, following)
                        if following is not None and c == 3:
                            down_hi(r + 1, 1 - slot)

                gate_up_hi(r0, 1, 16 * (base1 + 1))
                down_hi(r0, 1)
                for c in range(CHUNKS):
                    act.wait_ge(s["ct_bank"], CHUNKS * order + c + 1)
                    f(coef_rows[:, :, cols(c)], ps[0:96, 4 + c, :].bitcast(BF16).rearrange("p (t n) -> p t n", t=2),
                      ACT.Copy).then_inc(s["ct_ready"], 1)
                round_of(r0, 1, 16 * (base0 + 1))
                round_of(r0 + 1, 0, 16 * (base1 + 2))
                with act.Fori(0, pairs // 2 - 1) as i:
                    round_of(2 * i + (r0 + 2), 1, 16 * i + 16 * (base0 + 2))
                    round_of(2 * i + (r0 + 3), 0, 16 * i + 16 * (base1 + 3))
                round_of(r0 + pairs, 1)
                hidden_hi(4 * (r0 + pairs) + 3, 3)
                use_log_exp()
                for c in range(CHUNKS):
                    act.wait_ge(s["e_done"], CHUNKS * (r0 + pairs) + c + 1)
                    f(y[:, cols(c)], ps[:, c, :], ACT.Copy).then_inc(s["y_ready"], 1)

            if LAYERS > 5:
                experts(5, 64, 32, 0, 0)
                boundary(5)

            if LAYERS > 6:
                act.wait_ge(s["w_loaded"], 7 * 16)
                act.wait_ge(s["a_ready"], 1)
                f(neg_a, W(6, "a_log"), ACT.Exp).then_inc(s["a_ready"], 1)
                for c in range(CHUNKS):
                    for i in range(2):
                        act.wait_ge(s["xa_bank"], 2 * c + i + 1)
                        f(G(i, c), ps[:, 4 * i + c, :], ACT.Silu, bias=W(6, "conv_b", i, i + 1))\
                            .then_inc(s["xa_ready"], 1)
                for c in range(CHUNKS):
                    for i in range(2):
                        act.wait_ge(s["z_bank"], 2 * c + i + 1)
                        f(G(2 + i, c), ps[:, 4 * i + c, :], ACT.Silu).then_inc(s["z_ready"], 1)
                use_log_exp()
                for c in range(CHUNKS):
                    for i in range(2):
                        act.wait_ge(s["dt_bank"], 2 * c + i + 1)
                        f(G(10 + i, c), ps[:, 4 * i + c, :], ACT.Relu, bias=W(6, "dt_b", i, i + 1))
                        chain(f(G(8 + i, c), ps[:, 4 * i + c, :], ACT.Abs, bias=W(6, "dt_b", i, i + 1)))
                        chain.wait()
                        chain(f(G(8 + i, c), G(8 + i, c), ACT.Exp, scale=-1.0))
                        chain.wait()
                        f(G(8 + i, c), G(8 + i, c), ACT.Ln, bias=one).then_inc(s["dt_ready"], 1)
                act.wait_ge(s["dl_ready"], CHUNKS)
                act.wait_ge(s["a_ready"], 3)

                def state_step(c, k, n):
                    nb = k % 2
                    step = 16 * c + n
                    act.wait_ge(s["bb_bank"], step + 1)
                    act.wait_ge(s["db_ready"], step + 1)
                    f(g[:, 8, k * N:(k + 1) * N], ps[:, B_BANKS[k], :], ACT.Copy).then_inc(s["bs_ready"], 1)
                    hold(act, s["hs_done"], step + 1)
                    for i in range(2):
                        f(g[:, 9, (2 * nb + i) * N:(2 * nb + i + 1) * N], G(4 + i, c), ACT.Exp,
                          scale=neg_a[:, bass.ds(n + 16 * i, 1)]).then_inc(s["da_ready"], 1)

                def states_2_to_15(c):
                    for n in (2, 3):
                        state_step(c, n, n)
                    with act.Fori(1, 4) as m:
                        for k in range(4):
                            state_step(c, k, 4 * m + k)

                def sums_out(c):
                    hold(act, s["sum_done"], 16 * c + 18)
                    for i in range(2):
                        f(G(i, c), ps[:, i, :], ACT.Copy).then_inc(s["yt_ready"], 1)

                act.sem_inc(s["yt_ready"], 1)
                for n in (0, 1):
                    state_step(0, n, n)
                with act.Fori(0, CHUNKS - 1) as c:
                    states_2_to_15(c)
                    for n in (0, 1):
                        state_step(c + 1, n, n)
                    sums_out(c)
                states_2_to_15(CHUNKS - 1)
                sums_out(CHUNKS - 1)
                act.wait_ge(s["carried"], 1)
                evacuate("mo_bank", 0)
                boundary(6)

            if LAYERS > 7:
                experts(7, 16, 8, 1, 33)
                boundary(7)

            for c in range(CHUNKS):
                act.wait_ge(s["raw_ready"], CHUNKS + c + 1)
                f(G(10, c), ps[:, 4 + c, :], ACT.Copy).then_inc(s["back_ready"], 1)

        @block.gpsimd
        def _(pool):
            pv = nc.gpsimd

            def square(name, src, sem, base):
                for c in range(CHUNKS):
                    pool.wait_ge(s[sem], base + c + 1)
                    pv.tensor_tensor(sq[:, cols(c)], src(c), src(c), ALU.mult).then_inc(s["sq_pool"], 1)

            def R(c):
                return resid[:, cols(c)]

            square("pre0", R, "x_ready", 0)
            square("ln1", H, "h_ready", 0)

            def token_shift(base):
                for c in range(CHUNKS):
                    pool.wait_ge(s["h1_ready"], base + c + 1)
                    pv.tensor_tensor(G(1, c), G(0, c, 1), G(0, c, 0), ALU.subtract).then_inc(s["d_ready"], 1)

            token_shift(0)
            for c in range(CHUNKS):
                pool.wait_ge(s["pp_ready"], c + 1)
                pv.tensor_tensor(G(11, c), G(8, c, 0), G(8, c, 1), ALU.subtract)
                pv.tensor_tensor(G(12, c), G(5, c), G(8, c, 1), ALU.subtract).then_inc(s["d12_ready"], 1)
                pool.wait_ge(s["p_ready"], c + 1)
                pv.tensor_tensor(G(1, c), G(8, c, 0), G(3, c), ALU.subtract)
                pv.tensor_tensor(G(2, c), G(5, c), G(3, c), ALU.subtract).then_inc(s["d34_ready"], 1)
            token_shift(CHUNKS)

            def experts(layer, pairs, order, r0):
                for c in range(CHUNKS):
                    pool.wait_ge(s["x_hi_ready"], CHUNKS * order + c + 1)
                    pv.tensor_tensor(x_lo[:, cols(c)], H(c), x_hi[:, cols(c)].bitcast(F32), ALU.subtract)\
                        .then_inc(s["x_split"], 1)

                def weights_lo(r, slot, a, b, ready, done):
                    pool.wait_ge(s[ready], r + 1)
                    pv.tensor_tensor(w_lo[slot][:, a:b], pair_w[slot][:, a:b], w_hi[slot][:, a:b].bitcast(F32),
                                     ALU.subtract).then_inc(s[done], 1)

                def gate_up_lo(r, slot):
                    weights_lo(r, slot, 0, 256, "gu_hi_ready", "gu_split")

                def down_lo(r, slot):
                    weights_lo(r, slot, 256, 384, "d_hi_ready", "d_split")

                def round_of(r, slot, following=True):
                    for c in range(CHUNKS):
                        if following and c == 1:
                            gate_up_lo(r + 1, 1 - slot)
                        pool.wait_ge(s["hh_ready"], 4 * r + (c + 1))
                        pv.tensor_tensor(hid_lo[:, cols(c)], g[:, 6, (c % 2) * N:(c % 2 + 1) * N],
                                         hid_hi[:, cols(c)].bitcast(F32), ALU.subtract).then_inc(s["hl_ready"], 1)
                    if following:
                        down_lo(r + 1, 1 - slot)

                gate_up_lo(r0, 1)
                down_lo(r0, 1)
                round_of(r0, 1)
                round_of(r0 + 1, 0)
                with pool.Fori(0, pairs // 2 - 1) as i:
                    round_of(2 * i + (r0 + 2), 1)
                    round_of(2 * i + (r0 + 3), 0)
                round_of(r0 + pairs, 1, False)

            for layer in range(1, LAYERS):
                square(f"pre{layer}", R, "x_ready", CHUNKS * layer)
                if layer == 5:
                    experts(5, 32, 0, 0)
                if layer == 7:
                    experts(7, 8, 1, 33)
                if layer == 2:
                    for c in range(CHUNKS):
                        pool.wait_ge(s["m_ready"], c + 1)
                        pv.tensor_tensor(G(3, c), G(1, c, 0), G(1, c, 1), ALU.subtract)
                        pv.tensor_tensor(G(4, c), G(0, c), G(1, c, 1), ALU.subtract).then_inc(s["md_ready"], 1)
                    pool.sem_inc(s["qm_ready"], 4)
                    with pool.Fori(0, CHUNKS) as c:
                        for e in range(8):
                            par = e % 2
                            pool.wait_ge(s["st_ready"], 8 * c + e + 1)
                            hold(pool, s["qm_used"], 8 * c + e + 1)
                            pv.tensor_tensor(
                                g[:, 2, 2 * par * N:(2 * par + 2) * N].rearrange("p (r n) -> p r n", r=2),
                                two_of(1, 10, e), g[:, 8:10, cols(c)], ALU.mult).then_inc(s["qm_ready"], 1)
                if layer == 6:
                    pool.wait_ge(s["du_ready"], CHUNKS)
                    pool.sem_inc(s["db_ready"], 4)
                    with pool.Fori(0, CHUNKS) as c:
                        with pool.Fori(0, 4) as m:
                            for k in range(4):
                                nb = k % 2
                                step = 16 * c + 4 * m + k
                                pool.wait_ge(s["bs_ready"], step + 1)
                                hold(pool, s["hs_done"], step + 1)
                                pv.tensor_tensor(
                                    g[:, 10, 2 * nb * N:(2 * nb + 2) * N].rearrange("p (i n) -> p i n", i=2),
                                    g[:, 6:8, cols(c)],
                                    g[:, 8:9, k * N:(k + 1) * N].to_broadcast([P, 2, N]),
                                    ALU.mult).then_inc(s["db_ready"], 1)

        @block.vector
        def _(dve):
            v = nc.vector
            chain = Chain(dve, s["dve_chain"])

            def tt(o, a, b, op=ALU.mult):
                return v.tensor_tensor(o, a, b, op)

            def scale_by_rstd(name, o, src, done):
                for c in range(CHUNKS):
                    dve.wait_ge(s["rstd_ready"], NORM[name] * CHUNKS + c + 1)
                    tt(o(c), src(c), rstd[:, cols(c)]).then_inc(s[done], 1)

            def R(c):
                return resid[:, cols(c)]

            def boundary(layer):
                for c in range(CHUNKS):
                    dve.wait_ge(s["rstd_ready"], NORM[f"post{layer}"] * CHUNKS + c + 1)
                    chain(tt(tmp[:, cols(c)], ps[:, c, :], rstd[:, cols(c)]))
                    chain.wait()
                    tt(R(c), R(c), tmp[:, cols(c)], ALU.add).then_inc(s["x_ready"], 1)
                if layer + 1 < LAYERS:
                    scale_by_rstd(f"pre{layer + 1}", H, R, "h_ready")

            for k, value in ((13, 1.0), (49, 1e-5), (50, 1e-6)):
                v.memset(small[:, k:k + 1], value)
            v.memset(normed[:, 0:LEAD], 0.0)
            v.memset(g[:, 0, 0:1], 0.0)
            v.memset(g[:, 8, 0:1], -1e38)
            v.memset(g[:, 9:11, 0:1], 0.0)
            chain(v.memset(carry[:, :], 0.0))
            v.memset(small[:, 51:52], 0.0).then_inc(s["zeroed"], 1)
            dve.wait_ge(s["consts_loaded"], 16)
            chain(v.tensor_copy(ident_bf[:, :], ident))

            for c in range(CHUNKS):
                dve.wait_ge(s["centred"], c + 1)
                tt(mean0[:, cols(c)], y[:, cols(c)], ps[:, 4 + c, :], ALU.subtract)
                v.tensor_copy(R(c), ps[:, 4 + c, :]).then_inc(s["x_ready"], 1)
            scale_by_rstd("pre0", H, R, "h_ready")

            vec = [W(0, "vec", k, k + 1) for k in range(12)]
            ln1_w, ln1_b, ln2_w, ln2_b, tmk, tmv, tmr, bonus, f_tmk, f_tmr = vec[:10]
            w_decay = small[:, 14:15]
            dve.wait_ge(s["decay_ready"], 1)
            chain(v.tensor_scalar(w_decay, small[:, 15:16], -1.0, None, ALU.mult))

            for c in range(CHUNKS):
                dve.wait_ge(s["rstd_ready"], NORM["ln1"] * CHUNKS + c + 1)
                chain(tt(tmp[:, cols(c)], H(c), rstd[:, cols(c)]))
                chain.wait()
                v.tensor_scalar(G(0, c, 1), tmp[:, cols(c)], ln1_w, ln1_b, ALU.mult, ALU.add)\
                    .then_inc(s["h1_ready"], 1)

            def mix(o, amount, c):
                return v.scalar_tensor_tensor(o, G(1, c), amount, G(0, c, 0), ALU.mult, ALU.add)

            for c in range(CHUNKS):
                dve.wait_ge(s["d_ready"], c + 1)
                mix(G(2, c), tmk, c)
                mix(G(3, c), tmv, c)
                mix(G(4, c), tmr, c).then_inc(s["mix_ready"], 1)
            for c in range(CHUNKS):
                dve.wait_ge(s["kv_ready"], c + 1)
                v.tensor_tensor_scan(G(8, c, 1), w_decay.to_broadcast([P, N]), G(5, c),
                                     g[:, 8, cols(c, 0, 1)], ALU.add, ALU.max).then_inc(s["pp_ready"], 1)
                dve.wait_ge(s["pp_ready"], c + 1)
                v.scalar_tensor_tensor(G(3, c), G(5, c), bonus, G(8, c, 0), ALU.add, ALU.max)\
                    .then_inc(s["p_ready"], 1)
            for c in range(CHUNKS):
                dve.wait_ge(s["eb_ready"], c + 1)
                dve.wait_ge(s["ee_ready"], c + 1)
                dve.wait_ge(s["sr_ready"], c + 1)
                chain(tt(G(3, c), G(12, c), G(6, c)))
                chain(v.tensor_tensor_scan(G(10, c, 1), G(11, c), G(12, c), g[:, 10, cols(c, 0, 1)],
                                           ALU.mult, ALU.add))
                chain.wait()
                chain(v.tensor_tensor_scan(G(9, c, 1), G(11, c), G(3, c), g[:, 9, cols(c, 0, 1)],
                                           ALU.mult, ALU.add))
                chain(tt(y[:, cols(c)], G(1, c), G(10, c, 0)))
                chain.wait()
                tt(y[:, cols(c)], y[:, cols(c)], G(2, c), ALU.add).then_inc(s["den_ready"], 1)
                chain(tt(G(4, c), G(1, c), G(9, c, 0)))
                chain(tt(tmp[:, cols(c)], G(2, c), G(6, c)))
                chain.wait()
                chain(tt(G(4, c), G(4, c), tmp[:, cols(c)], ALU.add))
            for c in range(CHUNKS):
                chain.wait()
                dve.wait_ge(s["rd_ready"], c + 1)
                chain(tt(G(4, c), G(4, c), y[:, cols(c)]))
                chain.wait()
                tt(G(4, c), G(4, c), G(7, c)).then_inc(s["rw_ready"], 1)
            for c in range(CHUNKS):
                dve.wait_ge(s["ow_bank"], c + 1)
                tt(G(5, c), H(c), ps[:, c, :], ALU.add).then_inc(s["x1_ready"], 1)
            for c in range(CHUNKS):
                dve.wait_ge(s["rstd_ready"], NORM["ln2"] * CHUNKS + c + 1)
                chain(tt(tmp[:, cols(c)], ps[:, 4 + c, :], rstd[:, cols(c)]))
                chain.wait()
                v.tensor_scalar(G(0, c, 1), tmp[:, cols(c)], ln2_w, ln2_b, ALU.mult, ALU.add)\
                    .then_inc(s["h1_ready"], 1)
            for c in range(CHUNKS):
                dve.wait_ge(s["d_ready"], CHUNKS + c + 1)
                mix(G(2, c), f_tmk, c)
                mix(G(4, c), f_tmr, c).then_inc(s["mix_ready"], 1)
            for c in range(CHUNKS):
                dve.wait_ge(s["fv_bank"], c)
                for m in range(4):
                    dve.wait_ge(s["relu_ready"], 4 * c + m + 1)
                    tt(g[:, 7, m * N:(m + 1) * N], g[:, 6, m * N:(m + 1) * N], g[:, 6, m * N:(m + 1) * N])\
                        .then_inc(s["kk_ready"], 1)
            for c in range(CHUNKS):
                dve.wait_ge(s["sr2_ready"], c + 1)
                dve.wait_ge(s["fv_bank"], c + 1)
                chain(tt(tmp[:, cols(c)], G(8, c), ps[:, 4 + c, :]))
                chain.wait()
                tt(y[:, cols(c)], G(5, c), tmp[:, cols(c)], ALU.add).then_inc(s["y_ready"], 1)

            if LAYERS > 1:
                dve.wait_ge(s["w_loaded"], 32)
                v.scalar_tensor_tensor(nam_b1, W(1, "w1"), W(1, "bin"), W(1, "b1"), ALU.mult, ALU.add)
                for j in range(8):
                    last = v.tensor_scalar(nam_wout[j], W(1, "wout"), W(1, "w2", j, j + 1), None, ALU.mult)
                last.then_inc(s["nam_setup"], 1)
            boundary(0)
            if LAYERS > 1:
                boundary(1)

            if LAYERS > 2:
                dve.wait_ge(s["w_loaded"], 48)
                v.tensor_scalar(wo_normed, W(2, "wo"), W(2, "norm_w"), None, ALU.mult).then_inc(s["setup2"], 1)
                v.memset(g[:, 1, 0:1], 0.0)
                chain(v.memset(g[:, 2, 0:1], 1.0))
                chain.wait()
                for c in range(CHUNKS):
                    dve.wait_ge(s["k2_ready"], c + 1)
                    v.tensor_tensor_scan(G(1, c, 1), G(0, c), G(0, c), g[:, 1, cols(c, 0, 1)],
                                         ALU.max, ALU.max).then_inc(s["m_ready"], 1)
                    dve.wait_ge(s["m_ready"], c + 1)
                for c in range(CHUNKS):
                    dve.wait_ge(s["sigq_ready"], c + 1)
                    tt(G(5, c), G(5, c), ps[:, 4 + c, :]).then_inc(s["q_used"], 1)
                for c in range(CHUNKS):
                    dve.wait_ge(s["me_ready"], c + 1)
                    v.tensor_tensor_scan(G(2, c, 1), G(3, c), G(4, c), g[:, 2, cols(c, 0, 1)],
                                         ALU.mult, ALU.add).then_inc(s["s_ready"], 1)
                    dve.wait_ge(s["s_ready"], c + 1)
                dve.wait_ge(s["rope_loaded"], 16)
                for c in range(CHUNKS):
                    dve.wait_ge(s["rs_ready"], c + 1)
                    dve.wait_ge(s["q_used"], c + 1)
                    chain(tt(G(4, c), G(4, c), rstd[:, cols(c)]))
                    tt(G(8, c), G(5, c), G(10, c))
                    tt(G(9, c), G(5, c), G(11, c))
                    chain.wait()
                    chain(v.tensor_scalar(G(3, c), G(4, c), -1.0, 1.0, ALU.mult, ALU.add))
                    tt(G(6, c), G(4, c), G(10, c))
                    chain(tt(G(7, c), G(4, c), G(11, c)))
                chain.wait()
                dve.sem_inc(s["vb_used"], 4)

                def inputs(e, c):
                    hold(dve, s["vb_bank"], 8 * c + e + 1)
                    tt(two_of(0, 11, e), g[:, 6:8, cols(c)],
                       ps[:, e % 4:e % 4 + 1, :].to_broadcast([P, 2, N])).then_inc(s["vb_used"], 1)

                def carry_on(e, c):
                    dve.wait_ge(s["st_ready"], 8 * c + e + 1)
                    chain(v.tensor_copy(carry[:, 2 * e:2 * e + 2], two_of(1, 10, e)[:, :, N - 1]))

                with chain.each(CHUNKS, 8) as c:
                    inputs(0, c)
                    for e in range(8):
                        if e < 7:
                            inputs(e + 1, c)
                        chain.wait(but=1)
                        dve.wait_ge(s["vb_used"], 8 * c + e + 5)
                        hold(dve, s["qm_ready"], 8 * c + e + 1)
                        for r in range(2):
                            last = v.tensor_tensor_scan(two_of(1, 10, e)[:, r, :], G(3, c), two_of(0, 11, e)[:, r, :],
                                                        carry[:, 2 * e + r:2 * e + r + 1], ALU.mult, ALU.add)
                        last.then_inc(s["st_ready"], 1)
                        if e:
                            carry_on(e - 1, c)
                    carry_on(7, c)
                for c in range(CHUNKS):
                    dve.wait_ge(s["qm_used"], 8 * c + 10)
                    tt(G(4, c), G(12, c), ps[:, 4 + c, :]).then_inc(s["og_ready"], 1)
                scale_by_rstd("rms", lambda c: G(5, c), lambda c: G(4, c), "nrm_ready")
            if LAYERS > 3:
                dve.wait_ge(s["w_loaded"], 64)
                dve.wait_ge(s["bools_loaded"], 16)
                tt(ffn_w[:, 0:512], kbool[:, 0:512], kbool[:, 512:1024], ALU.subtract)
                v.tensor_scalar(ffn_w[:, 512:3072], kbool[:, 1024:3584], 2.0, -1.0, ALU.mult, ALU.add)
                v.tensor_scalar(scales[:, 0:1], W(3, "s", 0, 1), 4.0, None, ALU.mult)
                v.tensor_scalar(scales[:, 1:2], W(3, "s", 1, 2), 2.0, None, ALU.mult)
                v.tensor_copy(scales[:, 2:3], W(3, "s", 2, 3)).then_inc(s["f_setup"], 1)
            for layer in (2, 3, 4):
                if LAYERS > layer:
                    boundary(layer)

            def experts(layer, E, pairs, groups, keep_groups, top, order, r0):
                size = E // groups
                tiles = CHUNKS * TILES
                w = tiles * E
                whole = [home[:, k * 1024:(k + 1) * 1024]
                         for home in (g[:, 1, :], g[:, 2, :], tmp, y, sq, rstd) for k in range(2)]
                score, biased, equal, others, kept, replaced, coef = (b[:, 0:w] for b in whole[:7])
                better, ahead = whole[7][:, 0:tiles * groups * groups], whole[8][:, 0:tiles * groups * groups]
                G1 = tiles * groups
                best, count, second, group, two, keep = (whole[9][:, 128 * k:128 * k + G1] for k in range(6))
                top8 = whole[9][:, 768:768 + 8 * tiles].rearrange("p (a n) -> p a n", a=tiles)
                total, share = whole[9][:, 896:896 + tiles], whole[9][:, 912:912 + tiles]
                wide = 16 * (E + 4)
                if layer == 7:
                    padded = whole[10][:, 0:wide].rearrange("p (a n) -> p a n", a=tiles)
                    out_padded = whole[11][:, 0:wide].rearrange("p (a n) -> p a n", a=tiles)
                before = W(layer, "before", 0, groups * groups)
                bias = W(layer, "bias", 0, E)

                def by(ap, k):
                    return ap.rearrange("p (a e) -> p a e", e=k)

                def over(ap, n):
                    return by(ap, 1).to_broadcast([P, ap.shape[1], n])

                def square_of(ap, axis):
                    q = by(ap, groups)
                    q = q.unsqueeze(3) if axis == 2 else q.unsqueeze(2)
                    return q.to_broadcast([P, tiles, groups, groups])

                def step(ins):
                    chain(ins)
                    chain.wait()

                dve.wait_ge(s["w_loaded"], 16 * (layer + 1))
                step(v.memset(g[:, 3, 0:1536], 0.0))
                dve.wait_ge(s["sc_bank"], order + 1)
                step(v.tensor_copy(score, ps[:, 4:6, :].rearrange("p b n -> p (b n)")[:, 0:w]))
                step(tt(by(biased, E), by(score, E), bias.unsqueeze(1).to_broadcast([P, tiles, E]), ALU.add))
                step(v.tensor_reduce(best, by(biased, size), AX_X, ALU.max))
                if layer == 5:
                    step(tt(by(equal, size), by(biased, size), over(best, size), ALU.is_equal))
                    step(v.tensor_reduce(count, by(equal, size), AX_X, ALU.add))
                    step(v.scalar_tensor_tensor(others, equal, -BIG, biased, ALU.mult, ALU.add))
                    step(v.tensor_reduce(second, by(others, size), AX_X, ALU.max))
                    step(v.tensor_scalar(two, count, 2.0, None, ALU.is_ge))
                    step(tt(group, two, best))
                    step(v.tensor_scalar(two, two, -1.0, BIG, ALU.add, ALU.mult))
                    step(tt(group, group, two, ALU.add))
                    step(tt(second, second, group, ALU.max))
                    step(tt(group, best, second, ALU.add))
                else:
                    group = best
                b4 = better.rearrange("p (a i j) -> p a i j", i=groups, j=groups)
                a4 = ahead.rearrange("p (a i j) -> p a i j", i=groups, j=groups)
                chain(tt(b4, square_of(group, 3), square_of(group, 2), ALU.is_gt))
                step(tt(a4, square_of(group, 3), square_of(group, 2), ALU.is_equal))
                step(tt(by(ahead, groups * groups), by(ahead, groups * groups),
                        before.unsqueeze(1).to_broadcast([P, tiles, groups * groups])))
                step(tt(better, better, ahead, ALU.add))
                step(v.tensor_reduce(keep, by(better, groups), AX_X, ALU.add))
                step(v.tensor_scalar(keep, keep, float(keep_groups), None, ALU.is_lt))
                step(tt(by(kept, size), by(biased, size), over(keep, size)))
                if layer == 5:
                    for a in range(tiles):
                        last = v.max(top8[:, a, :], kept[:, a * E:(a + 1) * E])
                    step(last)
                    for a in range(tiles):
                        last = v.match_replace(replaced[:, a * E:(a + 1) * E], top8[:, a, :],
                                               kept[:, a * E:(a + 1) * E], BIG)
                    step(last)
                    chosen = replaced
                else:
                    step(v.tensor_scalar(keep, keep, -1.0, BIG, ALU.add, ALU.mult))
                    step(tt(by(kept, size), by(kept, size), over(keep, size), ALU.add))
                    chain(v.memset(padded[:, :, E:E + 4], -2 * BIG))
                    step(v.tensor_copy(padded[:, :, 0:E], by(kept, E)))
                    for a in range(tiles):
                        last = v.max(top8[:, a, :], kept[:, a * E:(a + 1) * E])
                    step(last)
                    step(v.memset(top8[:, :, 4:8], -2 * BIG))
                    for a in range(tiles):
                        last = v.match_replace(out_padded[:, a, :], top8[:, a, :], padded[:, a, :], BIG)
                    step(last)
                    step(v.tensor_copy(by(replaced, E), out_padded[:, :, 0:E]))
                step(v.scalar_tensor_tensor(coef, replaced, BIG, score, ALU.is_equal, ALU.mult))
                if layer == 5:
                    step(v.tensor_reduce(total, by(coef, E), AX_X, ALU.add))
                    step(v.tensor_scalar(total, total, 1e-20, None, ALU.add))
                    step(v.reciprocal(share, total))
                    step(v.tensor_scalar(share, share, 2.5, None, ALU.mult))
                    step(tt(by(coef, E), by(coef, E), over(share, E)))
                for part in range(3):
                    for t in range(2):
                        view = coef.rearrange("p (a q t r) -> p a q t r", a=tiles, t=2, r=2)[:, :, :, t, :]
                        dst = coef_parts[:, :, t, 32 * part:32 * part + E // 2]\
                            .rearrange("p a (q r) -> p a q r", r=2)
                        if part < 2:
                            chain(v.tensor_copy(dst, view))
                        else:
                            last = v.tensor_copy(dst, view)
                    if part < 2:
                        chain.wait()
                        for t in range(2):
                            view = coef.rearrange("p (a q t r) -> p a q t r", a=tiles, t=2, r=2)[:, :, :, t, :]
                            dst = coef_parts[:, :, t, 32 * part:32 * part + E // 2]\
                                .rearrange("p a (q r) -> p a q r", r=2)
                            chain(tt(view, view, dst, ALU.subtract))
                        chain.wait()
                last.then_inc(s["parts_ready"], 1)

                def glu(n, c, coef_no=None):
                    par = c % 2
                    silu_n = g[:, 5, par * N:(par + 1) * N]
                    prod = g[:, 5, (2 + par) * N:(3 + par) * N]
                    hidden = g[:, 6, par * N:(par + 1) * N]
                    dve.wait_ge(s["sg_ready"], n + 1)
                    dve.wait_ge(s["u_bank"], n + 1)
                    at_least(dve, s["hl_ready"], n - 1)
                    tt(prod, silu_n, ps[:, 5, :]).then_inc(s["t_ready"], 1)
                    dve.wait_ge(s["t_ready"], n + 1)
                    if coef_no is None:
                        v.tensor_copy(hidden, prod).then_inc(s["hid_ready"], 1)
                    else:
                        dve.wait_ge(s["c_bank"], coef_no)
                        tt(hidden, prod, ps[:, 6, :]).then_inc(s["hid_ready"], 1)

                n0 = r0 * CHUNKS
                c0 = 0 if layer == 5 else 32 * CHUNKS
                for c in range(CHUNKS):
                    glu(n0 + c, c)
                with dve.Fori(0, pairs) as p:
                    for c in range(CHUNKS):
                        glu(p * CHUNKS + (n0 + CHUNKS + c), c, p * CHUNKS + (c0 + c + 1))

            if LAYERS > 5:
                experts(5, 64, 32, 8, 4, 8, 0, 0)
                if LAYERS > 6:
                    dve.wait_ge(s["w_loaded"], 7 * 16)
                    conv = W(6, "conv").rearrange("p (j n) -> p j n", j=4)
                    for j in range(4):
                        last = tt(conv_w[:, j, :], W(6, "wx"), conv[:, j, :])
                    last.then_inc(s["conv_setup"], 1)
                boundary(5)

            if LAYERS > 6:
                v.tensor_scalar(W(6, "a_log"), W(6, "a_log"), 80.0, None, ALU.min).then_inc(s["a_ready"], 1)
                dve.wait_ge(s["a_ready"], 2)
                v.tensor_scalar(neg_a, neg_a, -1.0, None, ALU.mult).then_inc(s["a_ready"], 1)
                for i in range(2):
                    v.tensor_scalar(diag_d[:, i, :], ident, W(6, "d", i, i + 1), None, ALU.mult)
                v.memset(g[0:96, 12, T // 2:T // 2 + N // 2], 0.0)
                chain(v.memset(carry[:, :], 0.0))
                for c in range(CHUNKS):
                    dve.wait_ge(s["dt_ready"], 2 * c + 2)
                    tt(g[:, 4:6, cols(c)], g[:, 8:10, cols(c)], g[:, 10:12, cols(c)], ALU.add)\
                        .then_inc(s["dl_ready"], 1)
                    dve.wait_ge(s["dl_ready"], c + 1)
                    tt(g[:, 6:8, cols(c)], g[:, 4:6, cols(c)], g[:, 0:2, cols(c)]).then_inc(s["du_ready"], 1)
                part = [tmp[0:96, k * N:(k + 1) * N] for k in range(3)]
                low = tmp[0:96, 3 * N:4 * N].bitcast(BF16)
                hi, mid = low[:, 0:N], low[:, N:2 * N]
                for c in range(CHUNKS):
                    dve.wait_ge(s["bc_bank"], c + 1)
                    chain(v.tensor_copy(part[0], ps[0:96, c, :]))
                    chain.wait()
                    chain(v.tensor_copy(hi, part[0]))
                    chain.wait()
                    chain(tt(part[1], part[0], hi, ALU.subtract))
                    chain.wait()
                    chain(v.tensor_copy(mid, part[1]))
                    chain.wait()
                    chain(tt(part[2], part[1], mid, ALU.subtract))
                    chain(v.tensor_copy(bc_rows[0:32, cols(c)], hi[0:32]))
                    chain(v.tensor_copy(bc_rows[32:64, cols(c)], mid[32:64]))
                    chain.wait()
                    v.tensor_copy(bc_rows[64:96, cols(c)], part[2][64:96]).then_inc(s["bcp_ready"], 1)
                chain.wait()
                dve.wait_ge(s["bcp_ready"], CHUNKS)
                dve.sem_inc(s["hs_done"], 2)
                carried = carry.rearrange("p (i n) -> p i n", i=2)

                def buffer_of(k):
                    home = g[:, 11, :] if k < 2 else y
                    return home[:, 2 * (k % 2) * N:2 * (k % 2 + 1) * N].rearrange("p (i n) -> p i n", i=2)

                def scan(k, n, step):
                    dve.wait_ge(s["da_ready"], 2 * step + 2)
                    dve.wait_ge(s["db_ready"], step + 5)
                    chain.wait(but=1)
                    dve.nop(nofuse=True)
                    for i in range(2):
                        at = slice((2 * (k % 2) + i) * N, (2 * (k % 2) + i + 1) * N)
                        ins = v.tensor_tensor_scan(buffer_of(k)[:, i, :], g[:, 9, at], g[:, 10, at],
                                                   carry[:, bass.ds(n + 16 * i, 1)], ALU.mult, ALU.add)
                    ins.then_inc(s["hs_done"], 1)

                def times_c(k, n, step):
                    nb = k % 2
                    dve.wait_ge(s["cb_bank"], step + 1)
                    dve.wait_ge(s["sum_done"], step + 1)
                    hold(dve, s["hs_done"], step + 3)
                    tt(tmp[:, 2 * nb * N:(2 * nb + 2) * N].rearrange("p (i n) -> p i n", i=2), buffer_of(k),
                       ps[:, 4 + nb:5 + nb, :].to_broadcast([P, 2, N])).then_inc(s["hc_ready"], 1)
                    chain(v.tensor_copy(carried[:, :, bass.ds(n, 1)], buffer_of(k)[:, :, N - 1:N]))

                with chain.each(CHUNKS, 16) as c:
                    scan(0, 0, 16 * c)
                    with chain.each(3, 4) as m:
                        for k in range(4):
                            n = 4 * m + k
                            scan((k + 1) % 4, n + 1, 16 * c + n + 1)
                            times_c(k, n, 16 * c + n)
                    for n in range(12, 15):
                        scan((n + 1) % 4, n + 1, 16 * c + n + 1)
                        times_c(n % 4, n, 16 * c + n)
                    times_c(3, 15, 16 * c + 15)
                chain.wait()
                dve.sem_inc(s["carried"], 1)
                for c in range(CHUNKS):
                    dve.wait_ge(s["yt_ready"], 2 * c + 3)
                    tt(g[:, 2:4, cols(c)], g[:, 0:2, cols(c)], g[:, 2:4, cols(c)]).then_inc(s["yg_ready"], 1)
                boundary(6)

            if LAYERS > 7:
                experts(7, 16, 8, 4, 2, 4, 1, 33)
                boundary(7)

            for c in range(CHUNKS):
                dve.wait_ge(s["x_ready"], LAYERS * CHUNKS + c + 1)
                tt(G(9, c), R(c), mean0[:, cols(c)], ALU.add).then_inc(s["sum_ready"], 1)


def build(nc, args):
    sandwich(nc, *args)


def kernel(**inputs):
    import ml_dtypes
    import numpy as _np
    import concourse.bacc as _bacc
    from concourse import mybir as _mybir
    from concourse.bass_utils import run_bass_kernel_spmd as _run

    a = {k: _np.asarray(v) for k, v in inputs.items()}

    def L(layer, name):
        return a[f"L{layer // 2}_{'attn' if layer % 2 == 0 else 'ffn'}_{name}"]

    def tiled(m):
        return m.reshape(-1, P, m.shape[1]).transpose(1, 0, 2).reshape(P, -1)

    def col(v):
        return v.reshape(-1, P).T

    def rows(m):
        return _np.concatenate([m, _np.zeros((P - m.shape[0], m.shape[1]), m.dtype)], 0)

    def all_rows(v):
        return _np.broadcast_to(v.reshape(1, -1), (P, v.size))

    def twice(m):
        return _np.concatenate([m, m], 0)

    def halves(m):
        return m.reshape(64, 8, 2).transpose(2, 0, 1).reshape(P, 8)

    ch = _np.arange(P)
    f32 = _np.float32
    head_sum = _np.stack([(ch[:, None] // 8 == ch[None] // 8) & (ch[None] % 8 == e) for e in range(8)], 1)
    head_mean = (ch[:, None] // 8 == ch[None] // 8) / 8.0

    def before(n):
        i = _np.arange(n)
        m = _np.zeros(64)
        m[:n * n] = (i[None] < i[:, None]).reshape(-1)
        return all_rows(m.astype(f32))

    wv2 = L(4 - 2, "wv").reshape(P, 16, 8)
    packed = [
        dict(kw=L(0, "att_kw").T, vw=L(0, "att_vw").T, rw=L(0, "att_rw").T, ow=L(0, "att_ow").T,
             frw=L(0, "f_rw").T, fkw=L(0, "f_kw").T, fvw=tiled(L(0, "f_vw").T),
             vec=_np.stack([L(0, n) for n in ("ln1_w", "ln1_b", "ln2_w", "ln2_b", "tmk", "tmv", "tmr",
                                              "time_first", "f_tmk", "f_tmr", "time_decay")]
                           + [_np.zeros(P, f32)], 1)),
        dict(win=_np.concatenate([L(1, "Win")] * 2, 1), wout=twice(L(1, "Wout")), w1=halves(L(1, "W1")),
             b1=halves(L(1, "b1")), w2=halves(L(1, "W2")), bin=twice(L(1, "bin_")[:, None]),
             b2=twice(L(1, "b2")[:, None]), bout=col(L(1, "bout"))),
        dict(wq=L(2, "wq"), wk=L(2, "wk"),
             wv=_np.stack([_np.repeat(wv2[:, :, e], 8, 1) for e in range(8)], 1).reshape(P, -1),
             wg1=L(2, "wg1"), wg2=rows(L(2, "wg2")), wo=L(2, "wo"), norm_w=col(L(2, "norm_w")),
             head_sum=head_sum.astype(f32).reshape(P, -1), head_mean=head_mean.astype(f32)),
        dict(s=_np.stack([_np.broadcast_to(L(3, n), (P,)) for n in ("s0", "s1", "s2")], 1)),
        dict(wv=L(4, "in_proj_weight")[2048:].reshape(8, P, P).transpose(1, 0, 2).reshape(P, -1),
             wo=tiled(L(4, "out_proj_weight").T), bv=col(L(4, "in_proj_bias")[2048:]),
             bo=col(L(4, "out_proj_bias"))),
        dict(router=L(5, "router_w").T, bias=all_rows(L(5, "e_bias")), before=before(8)),
        dict(wx=L(6, "in_proj_w")[:256].T, conv=all_rows(_np.ascontiguousarray(L(6, "conv_w")[:, 0, :].T)),
             wz=L(6, "in_proj_w")[256:].T,
             wbc=tiled(_np.concatenate([L(6, "x_proj_w").T] * 3, 1)),
             wdt=tiled(L(6, "dt_proj_w").T), wout=tiled(L(6, "out_proj_w").T), conv_b=col(L(6, "conv_b")),
             dt_b=col(L(6, "dt_proj_b")), a_log=tiled(L(6, "A_log")), d=col(L(6, "D_param"))),
        dict(router=L(7, "gate_w").T, bias=all_rows(L(7, "gate_bias")), before=before(4)),
    ]
    blocks = []
    for layer in range(8):
        for name, width in LAYOUT[layer]:
            block = packed[layer][name]
            assert block.shape == (P, width), (layer, name, block.shape)
            blocks.append(block)
    weights = _np.ascontiguousarray(_np.concatenate(blocks, 1))

    def pairs(gate, up, down):
        E, Hn, I = gate.shape
        w = [m.reshape(E // 2, 2, Hn, I).transpose(0, 2, 1, 3).reshape(E // 2, Hn, 2 * I) for m in (gate, up)]
        return _np.concatenate(w + [down.reshape(E // 2, 2 * I, Hn)], 2)

    def wide(m):
        return _np.concatenate([m, _np.zeros((P, P - m.shape[1]), m.dtype)], 1)

    shared5 = _np.concatenate([L(5, "SWg"), L(5, "SWu"), L(5, "SWd")], 1)[None]
    shared7 = _np.concatenate([wide(L(7, "ws1").T), wide(L(7, "ws3").T), rows(L(7, "ws2").T)], 1)[None]
    T_ = (0, 2, 1)
    moe0 = _np.concatenate([shared5, pairs(L(5, "Wg"), L(5, "Wu"), L(5, "Wd"))], 0)
    moe1 = _np.concatenate([shared7, pairs(L(7, "w1").transpose(T_), L(7, "w3").transpose(T_),
                                           L(7, "w2").transpose(T_))], 0)
    bools = _np.concatenate([L(3, "k0")[:P], L(3, "k0")[P:], tiled(L(3, "k1")), tiled(L(3, "k2"))], 1)
    eye = _np.eye(P)
    consts = _np.concatenate([eye, eye - 1.0 / P, _np.full((P, P), 1.0 / P)], 1).astype(f32)

    sel = _np.zeros((96, 48, P), ml_dtypes.bfloat16)
    for part in range(3):
        for n in range(32):
            sel[32 * part + n, n, :] = 1
        for q in range(16):
            sel[32 * part + 2 * q, 32 + q, :64] = 1
            sel[32 * part + 2 * q + 1, 32 + q, 64:] = 1
    theta = (10000.0 ** (-2.0 / P * _np.arange(P))).astype(f32)
    angle = (theta[:, None] * _np.arange(T, dtype=f32)[None]).astype(f32)
    rope = _np.stack([_np.cos(angle), _np.sin(angle)], 1).astype(f32)

    host = dict(x=a["L0_attn_x"].reshape(T, P), weights=weights, bools=_np.ascontiguousarray(bools).view(_np.uint32), moe0=moe0,
                moe1=moe1, consts=consts, selectors=sel, rope=rope)
    nc = _bacc.Bacc("TRN2", target_bir_lowering=False, num_devices=1)
    arrays, aps = {}, {}
    for name, m in host.items():
        m = _np.ascontiguousarray(m)
        arrays[f"in_{name}_dram"] = m
        aps[name] = nc.dram_tensor(f"in_{name}_dram", m.shape, _mybir.dt.from_np(m.dtype),
                                   kind="ExternalInput").ap()
    out = nc.dram_tensor("out_dram", (T, P), _mybir.dt.float32, kind="ExternalOutput").ap()
    sandwich(nc, aps["x"], out, aps["weights"], aps["bools"], aps["moe0"], aps["moe1"], aps["consts"],
             aps["selectors"], aps["rope"])
    r = _run(nc, [arrays], core_ids=[0])
    return r.results[0]["out_dram"].reshape(1, T, P)
```

```python
from contextlib import ExitStack, contextmanager

import concourse.bass as bass
import numpy as np
from concourse import mybir

P = 128
T = 2048
N = 512
CHUNKS = T // N
TILES = N // P
PAD = 4
LEAD = 3
F32 = mybir.dt.float32
F32R = mybir.dt.float32r
BF16 = mybir.dt.bfloat16
U8 = mybir.dt.uint8
ALU = mybir.AluOpType
ACT = mybir.ActivationFunctionType
AX_X = mybir.AxisListType.X
LAYERS = 8

NORMS = ["pre0", "ln1", "ln2", "post0", "pre1", "post1", "pre2", "rms", "post2", "pre3", "post3",
         "pre4", "post4", "pre5", "post5", "pre6", "post6", "pre7", "post7"]
NORM = {name: i for i, name in enumerate(NORMS)}
ACT_SQUARES = [n for n in NORMS if n.startswith("post") or n in ("ln2", "rms")]
POOL_SQUARES = [n for n in NORMS if n not in ACT_SQUARES]
CENTRED = (2, 4, 6)
BIG = 1e30
B_BANKS = (2, 3, 6, 7)

LAYOUT = [
    [("kw", 128), ("vw", 128), ("rw", 128), ("ow", 128), ("frw", 128), ("fkw", 512), ("fvw", 512),
     ("vec", 12)],
    [("win", 128), ("wout", 128), ("w1", 8), ("b1", 8), ("w2", 8), ("bin", 1), ("b2", 1), ("bout", 1)],
    [("wq", 128), ("wk", 128), ("wv", 1024), ("wg1", 8), ("wg2", 128), ("wo", 128), ("norm_w", 1),
     ("head_sum", 1024), ("head_mean", 128)],
    [("s", 3)],
    [("wv", 1024), ("wo", 1024), ("bv", 8), ("bo", 1)],
    [("router", 64), ("bias", 64), ("before", 64)],
    [("wx", 256), ("conv", 8), ("wz", 256), ("wbc", 192), ("wdt", 512), ("wout", 256),
     ("conv_b", 2), ("dt_b", 2), ("a_log", 32), ("d", 2)],
    [("router", 16), ("bias", 16), ("before", 64)],
]
AT = []
for _cols in LAYOUT:
    _at, _o = {}, 0
    for _name, _w in _cols:
        _at[_name] = (_o, _o + _w)
        _o += _w
    AT.append(_at)
WIDTH = [sum(w for _, w in cols) for cols in LAYOUT]
PAIR = 3 * 128
DERIVED = 1024
ARENA = [4 * 1024, 4 * 1024]


def cols(c, off=0, n=N):
    return bass.ds(c * N + off, n) if not isinstance(c, int) else slice(c * N + off, c * N + off + n)


class Chain:

    def __init__(self, eng, sem):
        self.eng, self.sem, self.n, self.reg = eng, sem, 0, 0

    def __call__(self, ins):
        ins.then_inc(self.sem, 1)
        self.n += 1

    def wait(self, but=0):
        self.eng.wait_ge(self.sem, self.reg + (self.n - but))

    @contextmanager
    def each(self, count, per):
        start, reg = self.n, self.reg
        with self.eng.Fori(0, count) as i:
            self.reg = reg + i * per
            yield i
        assert self.n - start == per, (self.n - start, per)
        self.reg = reg
        self.n = start + count * per


def y_before(layer):
    return CHUNKS * (1 + sum(k not in CENTRED for k in range(layer)))


def hold(eng, sem, value):
    if not isinstance(value, int) or value > 0:
        eng.wait_ge(sem, value)
        if not isinstance(value, int):
            eng.nop(nofuse=True)


def at_least(eng, sem, value):
    if not isinstance(value, int) or value > 0:
        eng.wait_ge(sem, value)


def sandwich(nc, x, out, weights, bools, moe0, moe1, consts, selectors, rope):
    ctx = ExitStack()
    with ctx:
        def sb(name, shape, dt=F32):
            return ctx.enter_context(nc.sbuf_tensor(name, shape, dt))

        names = """w_loaded bools_loaded sel_loaded consts_loaded x_loaded rope_loaded pair_loaded0 pair_loaded1
            out_stored y_ready x_ready h_ready centred sq_act sq_pool var_ready rstd_ready
            dve_chain act_chain zeroed raw_ready
            h1_ready d_ready mix_ready k_bank v_bank r_bank kv_ready sr_ready pp_ready d12_ready
            p_ready d34_ready eb_ready ee_ready den_ready rd_ready rw_ready decay_ready ow_bank x1_ready
            fr_bank fk_bank relu_ready kk_ready fv_bank sr2_ready
            nam_s_bank nam_relu nam_used nam_hi nam_lo_dve nam_lo_pool nam_setup nam_bias_bank nam_bias
            q_bank2 k_bank2 g1_bank g2_bank k2_ready sigq_ready q_used g1_ready gate_ready
            m_ready md_ready me_ready s_ready rs_ready vb_bank vb_used st_ready
            qm_ready qm_used og_ready nrm_ready wo_bank setup2
            f_setup a1_bank a1_relu a2_bank a2_relu a3_bank
            comb_bank comb_ready
            lg_bank lg_ready sc_bank parts_ready ct_bank ct_ready
            g_bank u_bank c_bank sg_ready t_ready hid_ready e_done
            a_ready xs_bank xs_ready conv_ready xa_ready z_bank z_ready dt_bank dt_ready dl_ready du_ready bc_bank bc_read bcp_ready
            bb_bank cb_bank bs_ready da_ready db_ready hs_done hc_ready sum_done
            x_hi_ready x_split gu_hi_ready gu_split d_hi_ready d_split hh_ready hl_ready
            sc_copied qr_ready fx_split a1_split a2_split
            yt_ready yg_ready mo_bank mo_ready sum_ready back_ready""".split()
        s = {n: ctx.enter_context(nc.semaphore(n)) for n in names}

        resid = sb("resid", [P, T])
        mean0 = sb("mean0", [P, T])
        normed = sb("normed", [P, T])
        y = sb("y", [P, T])
        sq = sb("sq", [P, T])
        rstd = sb("rstd", [P, T])
        tmp = sb("tmp", [P, T])
        with nc.sbuf_tensor("g", [P, 13, T + PAD], F32) as g:
            pass
        parts = sb("parts", [P, 13, T + PAD], F32R)
        arena = [sb(f"arena{i}", [P, ARENA[i]]) for i in range(2)]
        kbool_words = arena[1][:, 3100:3100 + 896].bitcast(mybir.dt.uint32)
        kbool = arena[1][:, 3100:3100 + 896].bitcast(U8)
        const = sb("const", [P, 3 * 128])
        sel = sb("sel", [96, 48, 128], BF16)
        ident_bf = sb("ident_bf", [P, P], BF16)
        small = sb("small", [P, 64])
        carry = sb("carry", [P, 32])
        ps = ctx.enter_context(nc.psum_tensor("ps", [P, 8, N], F32))

        ident, centring, averaging = (const[:, i * 128:(i + 1) * 128] for i in range(3))
        sel_bc, sel_coef = sel[:, 0:32, :], sel[:, 32:48, :]

        def W(layer, name, a=0, b=None):
            lo, hi = AT[layer][name]
            return arena[layer % 2][:, lo + a:(hi if b is None else lo + b)]

        def derived(layer, a, b):
            return arena[layer % 2][:, WIDTH[layer] + a:WIDTH[layer] + b]

        def G(i, c, off=0, n=N):
            return g[:, i, cols(c, off, n)]

        def turned(a, n_experts):
            per_bank = N // n_experts
            at = (a % per_bank) * n_experts
            return ps[:, 4 + a // per_bank, at:at + n_experts]

        def nam_hidden(j):
            return g[:, j // 4, (j % 4) * N:(j % 4 + 1) * N]

        def nam_parts(j):
            return [parts[:, k + j // 4, (j % 4) * N:(j % 4 + 1) * N] for k in (2, 4)]

        def nam_lo_of(j):
            return "nam_lo_dve" if j % 2 == 0 else "nam_lo_pool"

        def two_of(a, b, k):
            return g[:, a if k % 4 < 2 else b, 2 * (k % 2) * N:2 * (k % 2 + 1) * N].rearrange("p (r n) -> p r n", r=2)

        def H(c):
            return normed[:, cols(c)]

        nam_wout = [derived(1, j * 128, (j + 1) * 128) for j in range(8)]
        nam_w = [parts[:, 12, k * 1024:(k + 1) * 1024] for k in range(2)]
        nam_b1, nam_bout = small[:, 0:8], small[:, 8:9]
        scales = small[:, 9:12]
        comb_bias, comb_sum = small[:, 12:13], small[:, 52:53]
        one = small[:, 13:14]
        eps5, eps6 = small[:, 49:50], small[:, 50:51]
        sign0, sign1, sign2 = parts[:, 6, 0:512], parts[:, 7, 0:2048], parts[:, 6, 512:1024]
        hid1 = [parts[:, k, 0:T] for k in (2, 3)]
        hid2 = [parts[:, k, 0:T] for k in (4, 5)]
        comb, comb_t = derived(4, 0, 128), derived(4, 128, 256)
        wo_normed = derived(2, 0, 128)
        wout_centred = derived(6, 0, 256)
        neg_a = small[:, 16:48]
        diag_d = g[:, 12, 1536:1792].rearrange("p (i n) -> p i n", i=2)
        sc_rows = g[:, 0, 0:T]
        coef_parts = g[:, 3, 0:1536].bitcast(BF16).rearrange("p (a t r) -> p a t r", a=CHUNKS * TILES, t=2)
        coef_rows = g[0:96, 4, 0:T].bitcast(BF16).rearrange("p (t n) -> p t n", t=2)
        bc_rows = g[0:96, 12, 0:1536].bitcast(BF16)
        pair_w = [g[:, 7, i * PAIR:(i + 1) * PAIR] for i in range(2)]
        x_hi, x_lo, hid_hi, hid_lo = (parts[:, k, 0:T] for k in (8, 9, 10, 11))
        w_hi = [parts[:, 12, 2 * i * PAIR:(2 * i + 1) * PAIR] for i in range(2)]
        w_lo = [parts[:, 12, (2 * i + 1) * PAIR:2 * (i + 1) * PAIR] for i in range(2)]

        x_tiles = x.rearrange("(c a p) f -> p c a f", a=TILES, p=P)
        out_tiles = out.rearrange("(c a p) f -> p c a f", a=TILES, p=P)
        x_in = g[:, 11:13, 0:1024]

        block = ctx.enter_context(nc.Block())

        @block.sync
        def _(sp):
            for c in range(CHUNKS):
                sp.dma_start(x_in[:, c // 2, (c % 2) * 512:(c % 2 + 1) * 512]
                             .rearrange("p (a f) -> p a f", a=TILES), x_tiles[:, c]).then_inc(s["x_loaded"], 16)
                if c == 0:
                    sp.dma_start(const[:, :], consts[:, :]).then_inc(s["consts_loaded"], 16)
            lo = 0
            for layer in range(LAYERS):
                if layer >= 2:
                    sp.wait_ge(s["centred"], CHUNKS * (layer + 1))
                sp.dma_start(arena[layer % 2][:, 0:WIDTH[layer]],
                             weights[:, lo:lo + WIDTH[layer]]).then_inc(s["w_loaded"], 16)
                sp.wait_ge(s["w_loaded"], 16 * (layer + 1))
                lo += WIDTH[layer]
                if layer == 3:
                    sp.dma_start(kbool_words, bools[:, :]).then_inc(s["bools_loaded"], 16)
                if layer == 4:
                    sp.dma_start(sel[:, :, :], selectors[:, :, :]).then_inc(s["sel_loaded"], 16)
                if layer == 2:
                    sp.dma_start(g[:, 10:12, 0:T], rope[:, :, :]).then_inc(s["rope_loaded"], 16)
                for moe_layer, dram, pairs, first in ((5, moe0, 32, 0), (7, moe1, 8, 33)):
                    if layer != moe_layer:
                        continue
                    if moe_layer == 7:
                        sp.wait_ge(s["yg_ready"], CHUNKS)
                    sp.dma_start(pair_w[1], dram[0, :, :]).then_inc(s["pair_loaded1"], 16)
                    sp.dma_start(pair_w[0], dram[1, :, :]).then_inc(s["pair_loaded0"], 16)
                    with sp.Fori(0, pairs // 2 - 1) as i:
                        for k in (0, 1):
                            sp.wait_ge(s["d_split"], 2 * i + (first + 1 + k))
                            sp.dma_start(pair_w[1 - k], dram[bass.ds(2 * i + 2 + k, 1), :, :]
                                         .rearrange("a p n -> p (a n)"))\
                              .then_inc(s["pair_loaded1" if k == 0 else "pair_loaded0"], 16)
                    sp.wait_ge(s["d_split"], first + pairs - 1)
                    sp.dma_start(pair_w[1], dram[pairs, :, :]).then_inc(s["pair_loaded1"], 16)
            for c in range(CHUNKS):
                sp.wait_ge(s["back_ready"], c + 1)
                sp.dma_start(out_tiles[:, c], g[:, 10, cols(c)].rearrange("p (a f) -> p a f", a=TILES))\
                  .then_inc(s["out_stored"], 16)
            sp.wait_ge(s["out_stored"], 16 * CHUNKS)

        @block.tensor
        def _(pe):
            def mm(o, lhsT, rhs, start=True, stop=True, **kw):
                return nc.tensor.matmul(o, lhsT, rhs, start=start, stop=stop, **kw)

            def centre(base, src, bank, ready="y_ready"):
                for c in range(CHUNKS):
                    pe.wait_ge(s[ready], base + c + 1)
                    mm(ps[:, bank + c, :], centring, src(c)).then_inc(s["centred"], 1)

            def variance(name, bank=4, matrix=averaging):
                by = "sq_act" if name in ACT_SQUARES else "sq_pool"
                k = (ACT_SQUARES if name in ACT_SQUARES else POOL_SQUARES).index(name)
                for c in range(CHUNKS):
                    pe.wait_ge(s[by], k * CHUNKS + c + 1)
                    mm(ps[:, bank + c, :], matrix, sq[:, cols(c)]).then_inc(s["var_ready"], 1)

            def boundary(layer):
                if layer not in CENTRED:
                    centre(y_before(layer), lambda c: y[:, cols(c)], 0)
                if layer == 3:
                    pe.wait_ge(s["comb_ready"], 2)
                variance(f"post{layer}")
                if layer + 1 < LAYERS:
                    variance(f"pre{layer + 1}")

            def h(layer, c):
                pe.wait_ge(s["h_ready"], layer * CHUNKS + c + 1)

            def three_passes(o, w, x, start=True, stop=True):
                mm(o, w[0], x[0], start, False, skip_group_check=True)
                mm(o, w[0], x[1], False, False, skip_group_check=True)
                return mm(o, w[1], x[0], False, stop, skip_group_check=True)

            pe.wait_ge(s["consts_loaded"], 16)
            for c in range(CHUNKS):
                pe.wait_ge(s["x_loaded"], 16 * CHUNKS)
                for a in range(TILES):
                    last = nc.tensor.transpose(ps[:, c, a * P:(a + 1) * P],
                                               x_in[:, c // 2, (c % 2) * 512 + a * P:(c % 2) * 512 + (a + 1) * P],
                                               ident)
                last.then_inc(s["raw_ready"], 1)
            centre(0, lambda c: y[:, cols(c)], 4)
            variance("pre0", 0)
            variance("ln1", 0)

            pe.wait_ge(s["w_loaded"], 16)
            for c in range(CHUNKS):
                pe.wait_ge(s["mix_ready"], c + 1)
                mm(ps[:, c, :], W(0, "kw"), G(2, c)).then_inc(s["k_bank"], 1)
                mm(ps[:, 4 + c, :], W(0, "vw"), G(3, c)).then_inc(s["v_bank"], 1)
            for c in range(CHUNKS):
                pe.wait_ge(s["kv_ready"], c + 1)
                mm(ps[:, c, :], W(0, "rw"), G(4, c)).then_inc(s["r_bank"], 1)
            for c in range(CHUNKS):
                pe.wait_ge(s["rw_ready"], c + 1)
                mm(ps[:, c, :], W(0, "ow"), G(4, c)).then_inc(s["ow_bank"], 1)
            for c in range(CHUNKS):
                pe.wait_ge(s["x1_ready"], c + 1)
                mm(ps[:, 4 + c, :], centring, G(5, c)).then_inc(s["centred"], 1)
            variance("ln2", 0)
            for c in range(CHUNKS):
                pe.wait_ge(s["mix_ready"], CHUNKS + c + 1)
                mm(ps[:, c, :], W(0, "frw"), G(4, c)).then_inc(s["fr_bank"], 1)
            pe.wait_ge(s["sr2_ready"], CHUNKS)
            for c in range(CHUNKS):
                pe.wait_ge(s["relu_ready"], 4 * c)
                for m in range(4):
                    mm(ps[:, m, :], W(0, "fkw", m * 128, m * 128 + 128), G(2, c)).then_inc(s["fk_bank"], 1)
                for m in range(4):
                    pe.wait_ge(s["kk_ready"], 4 * c + m + 1)
                    last = mm(ps[:, 4 + c, :], W(0, "fvw", m * 128, m * 128 + 128),
                              g[:, 7, m * N:(m + 1) * N], m == 0, m == 3)
                last.then_inc(s["fv_bank"], 1)
            boundary(0)

            pe.wait_ge(s["w_loaded"], 32)
            pe.wait_ge(s["nam_setup"], 1)
            h(1, 3)
            mm(ps[:, 7, 0:1], W(1, "wout")[0:64], W(1, "b2")[0:64]).then_inc(s["nam_bias_bank"], 1)
            for c in range(CHUNKS):
                h(1, c)
                mm(ps[:, c, :], W(1, "win"), H(c)).then_inc(s["nam_s_bank"], 1)
            pe.wait_ge(s["nam_bias"], 1)
            for c in range(CHUNKS):
                for j in range(8):
                    pe.wait_ge(s[nam_lo_of(j)], 4 * c + j // 2 + 1)
                    three_passes(ps[:, 4 + c, :], [w[:, j * 128:(j + 1) * 128] for w in nam_w], nam_parts(j),
                                 j == 0, j == 7).then_inc(s["nam_used"], 1)
            boundary(1)

            pe.wait_ge(s["w_loaded"], 48)
            for c in range(CHUNKS):
                h(2, c)
                mm(ps[:, c, :], W(2, "wk"), H(c)).then_inc(s["k_bank2"], 1)
                mm(ps[:, 4 + c, :], W(2, "wq"), H(c)).then_inc(s["q_bank2"], 1)
            for c in range(CHUNKS):
                pe.wait_ge(s["k2_ready"], c + 1)
                mm(ps[0:8, c, :], W(2, "wg1"), H(c)).then_inc(s["g1_bank"], 1)
            for c in range(CHUNKS):
                pe.wait_ge(s["q_used"], c + 1)
                pe.wait_ge(s["g1_ready"], c + 1)
                mm(ps[:, 4 + c, :], W(2, "wg2")[0:8], tmp[0:8, cols(c)]).then_inc(s["g2_bank"], 1)
            pe.wait_ge(s["gate_ready"], CHUNKS)
            mm(ps[:, 7, 0:128], W(2, "wo"), centring).then_inc(s["wo_bank"], 1)

            def spread_v(e, c):
                pe.wait_ge(s["vb_used"], 8 * c + e + 1)
                mm(ps[:, e % 4, :], W(2, "wv", e * 128, e * 128 + 128), H(c)).then_inc(s["vb_bank"], 1)

            def features(c, more):
                for e in range(8):
                    if e < 5 or more:
                        spread_v((e + 3) % 8, c + (e + 3) // 8)
                    pe.wait_ge(s["qm_ready"], 8 * c + e + 5)
                    for r in range(2):
                        last = mm(ps[:, 4 + c, :] if isinstance(c, int) else
                                  ps[:, bass.ds(c + 4, 1), :].rearrange("p a n -> p (a n)"),
                                  W(2, "head_sum", e * 128, e * 128 + 128),
                                  g[:, 2, (2 * (e % 2) + r) * N:(2 * (e % 2) + r + 1) * N],
                                  e == 0 and r == 0, e == 7 and r == 1)
                    last.then_inc(s["qm_used"], 1)

            pe.sem_inc(s["qm_used"], 2)
            for e in range(3):
                spread_v(e, 0)
            with pe.Fori(0, CHUNKS - 1) as c:
                features(c, True)
            pe.wait_ge(s["setup2"], 1)
            features(CHUNKS - 1, False)
            variance("rms", 0, W(2, "head_mean"))
            for c in range(CHUNKS):
                pe.wait_ge(s["nrm_ready"], c + 1)
                mm(ps[:, c, :], wo_normed, G(5, c)).then_inc(s["centred"], 1)
            boundary(2)

            pe.wait_ge(s["f_setup"], 1)
            pe.wait_ge(s["x_ready"], 4 * CHUNKS)
            pe.wait_ge(s["h_ready"], 4 * CHUNKS)

            def in_parts(o, w, x, start=True, stop=True):
                mm(o, w, x[0], start, False)
                return mm(o, w, x[1], False, stop)

            def first(c):
                pe.wait_ge(s["fx_split"], c + 1)
                pe.wait_ge(s["a1_relu"], 4 * c)
                for m in range(4):
                    in_parts(ps[:, m, :], sign0[:, m * 128:m * 128 + 128],
                             (x_hi[:, cols(c)], x_lo[:, cols(c)])).then_inc(s["a1_bank"], 1)

            def tile_of(parts_of, k):
                return [p[:, k * N:(k + 1) * N] for p in parts_of]

            first(0)
            for c in range(CHUNKS):
                pe.wait_ge(s["a2_relu"], 4 * c)
                for m in range(4):
                    if m == 3:
                        pe.wait_ge(s["y_ready"], y_before(3) + c)
                    for k in range(4):
                        if m == 0:
                            pe.wait_ge(s["a1_split"], 4 * c + k + 1)
                        last = in_parts(ps[:, 4 + m, :], sign1[:, k * 512 + m * 128:k * 512 + m * 128 + 128],
                                        tile_of(hid1, k), k == 0, k == 3)
                    last.then_inc(s["a2_bank"], 1)
                if c + 1 < CHUNKS:
                    first(c + 1)
                else:
                    pe.wait_ge(s["w_loaded"], 80)
                    pe.wait_ge(s["a1_relu"], 4 * CHUNKS)
                    for k in range(8):
                        mm(ps[:, 0, 0:128], W(4, "wo", k * 128, k * 128 + 128),
                           W(4, "wv", k * 128, k * 128 + 128), k == 0, k == 7)
                    for k in range(8):
                        last = mm(ps[:, 1, 0:1], W(4, "wo", k * 128, k * 128 + 128),
                                  W(4, "bv", k, k + 1), k == 0, k == 7)
                    last.then_inc(s["comb_bank"], 1)
                pe.wait_ge(s["a2_relu"], 4 * c + 4)
                for k in range(4):
                    pe.wait_ge(s["a2_split"], 4 * c + k + 1)
                    last = in_parts(ps[:, 7, :], sign2[:, k * 128:k * 128 + 128], tile_of(hid2, k),
                                    k == 0, k == 3)
                last.then_inc(s["a3_bank"], 1)
            pe.wait_ge(s["comb_ready"], 1)
            mm(ps[:, 6, 0:128], comb_t, centring)
            mm(ps[:, 5, 0:1], centring, comb_sum).then_inc(s["comb_bank"], 1)
            boundary(3)

            for c in range(CHUNKS):
                h(4, c)
                mm(ps[:, c, :], comb, H(c)).then_inc(s["centred"], 1)
            boundary(4)

            def experts(layer, n_experts, pairs, order, r0):
                pe.wait_ge(s["w_loaded"], 16 * (layer + 1))
                pe.wait_ge(s["sel_loaded"], 16)
                for c in range(CHUNKS):
                    h(layer, c)
                    mm(ps[0:n_experts, c, :], W(layer, "router"), H(c)).then_inc(s["lg_bank"], 1)
                pe.wait_ge(s["x_ready"], CHUNKS * (layer + 1))
                for c in range(CHUNKS):
                    pe.wait_ge(s["lg_ready"], CHUNKS * order + c + 1)
                    for a in range(c * TILES, (c + 1) * TILES):
                        last = nc.tensor.transpose(turned(a, n_experts), sc_rows[0:n_experts, a * P:(a + 1) * P],
                                                   ident[0:n_experts, 0:n_experts])
                last.then_inc(s["sc_bank"], 1)
                pe.wait_ge(s["x_split"], CHUNKS * (order + 1))

                def product(o, slot, at, hi, lo, start=True, stop=True):
                    hi_w, lo_w = w_hi[slot][:, at:at + 128], w_lo[slot][:, at:at + 128]
                    mm(o, hi_w, hi, start, False, skip_group_check=True)
                    mm(o, hi_w, lo, False, False, skip_group_check=True)
                    return mm(o, lo_w, hi, False, stop, skip_group_check=True)

                def turn(n, slot, c, coef=None, down=None):
                    gb = 4 if c % 2 == 0 else 7
                    at_least(pe, s["sg_ready"], n - 1)
                    product(ps[:, gb, :], slot, 0, x_hi[:, cols(c)], x_lo[:, cols(c)]).then_inc(s["g_bank"], 1)
                    at_least(pe, s["t_ready"], n)
                    product(ps[:, 5, :], slot, 128, x_hi[:, cols(c)], x_lo[:, cols(c)]).then_inc(s["u_bank"], 1)
                    if down is not None:
                        down_product(n - 3, (c + 1) % 4, *down)
                    if coef is not None:
                        t, q = coef
                        pe.wait_ge(s["hid_ready"], n)
                        mm(ps[:, 6, :], sel_coef[:, q, :].rearrange("p a n -> p (a n)"),
                           coef_rows[:, t, cols(c)]).then_inc(s["c_bank"], 1)

                def down_product(n, c, slot, start=False, stop=False):
                    if c == 0:
                        pe.wait_ge(s["d_split"], n // 4 + 1 if isinstance(n, int) else down_round[0])
                    pe.wait_ge(s["hl_ready"], n + 1)
                    product(ps[:, c, :], slot, 256, hid_hi[:, cols(c)], hid_lo[:, cols(c)], start, stop)\
                        .then_inc(s["e_done"], 1)

                down_round = [None]

                def round_of(r, slot, coef, before, stop=False):
                    pe.wait_ge(s["gu_split"], r + 1)
                    down_round[0] = r + 1
                    for c in range(CHUNKS):
                        down = (slot, before is None, stop) if c == 3 else before
                        turn(4 * r + c, slot, c, coef, down)

                pe.wait_ge(s["sc_copied"], order + 1)
                round_of(r0, 1, None, None)
                pe.wait_ge(s["parts_ready"], order + 1)
                pe.wait_ge(s["t_ready"], 4 * r0 + 4)
                for c in range(CHUNKS):
                    for t in range(2):
                        for a in range(TILES):
                            last = nc.tensor.transpose(
                                ps[0:96, 4 + c, :].bitcast(BF16)[:, t * N + a * P:t * N + (a + 1) * P],
                                coef_parts[:, c * TILES + a, t, :], ident_bf[:, :])
                    last.then_inc(s["ct_bank"], 1)
                pe.wait_ge(s["ct_ready"], CHUNKS * (order + 1))
                round_of(r0 + 1, 0, (0, bass.ds(0, 1)), (1, True))
                with pe.Fori(0, pairs // 2 - 1) as i:
                    for k in (0, 1):
                        round_of(2 * i + (r0 + 2 + k), 1 - k, (1 - k, bass.ds(i + k, 1)), (k,))
                round_of(r0 + pairs, 1, (1, bass.ds(pairs // 2 - 1, 1)), (0,), True)
                for c in range(1, CHUNKS):
                    down_product(4 * (r0 + pairs) + c, c, 1, False, True)

            experts(5, 64, 32, 0, 0)
            boundary(5)

            pe.wait_ge(s["w_loaded"], 7 * 16)
            for c in range(CHUNKS):
                h(6, c)
                for i in range(2):
                    mm(ps[:, 4 * i + c, :], W(6, "wx", i * 128, i * 128 + 128), H(c)).then_inc(s["xs_bank"], 1)
            for c in range(CHUNKS):
                pe.wait_ge(s["xs_ready"], 2 * c + 2)
                for i in range(2):
                    mm(ps[:, 4 * i + c, :], W(6, "wz", i * 128, i * 128 + 128), H(c)).then_inc(s["z_bank"], 1)
            for c in range(CHUNKS):
                pe.wait_ge(s["z_ready"], 2 * c + 2)
                pe.wait_ge(s["xa_ready"], 2 * c + 2)
                for k in range(2):
                    last = mm(ps[0:96, c, :], W(6, "wbc", k * 96, k * 96 + 96), G(k, c), k == 0, k == 1)
                last.then_inc(s["bc_bank"], 1)
                for i in (1, 0):
                    if i == 0:
                        pe.wait_ge(s["bc_read"], c + 1)
                    for k in range(2):
                        last = mm(ps[:, 4 * i + c, :],
                                  W(6, "wdt", k * 256 + i * 128, k * 256 + i * 128 + 128), G(k, c),
                                  k == 0, k == 1)
                    last.then_inc(s["dt_bank"], 1)
            pe.wait_ge(s["dt_ready"], 2 * CHUNKS)
            for k in range(2):
                last = mm(ps[:, 0, k * 128:k * 128 + 128], W(6, "wout", k * 128, k * 128 + 128), centring)
            last.then_inc(s["mo_bank"], 1)
            pe.wait_ge(s["bcp_ready"], CHUNKS)

            def row(n):
                return sel_bc[:, bass.ds(n, 1), :].rearrange("p a n -> p (a n)")

            def spread_b(k, n, c, step):
                at_least(pe, s["bs_ready"], step - 3)
                mm(ps[:, B_BANKS[k], :], row(n), bc_rows[:, cols(c)]).then_inc(s["bb_bank"], 1)

            def spread_c(nb, n, c, step):
                at_least(pe, s["hc_ready"], step - 1)
                mm(ps[:, 4 + nb, :], row(n + 16), bc_rows[:, cols(c)]).then_inc(s["cb_bank"], 1)

            def sum_n(nb, step, stop=False):
                pe.wait_ge(s["hc_ready"], step + 1)
                for i in range(2):
                    last = mm(ps[:, i, :], ident, tmp[:, (2 * nb + i) * N:(2 * nb + i + 1) * N], False, stop,
                              skip_group_check=True)
                last.then_inc(s["sum_done"], 1)

            for k in range(4):
                spread_b(k, k, 0, k)
            spread_c(0, 0, 0, 0)
            pe.sem_inc(s["sum_done"], 2)
            with pe.Fori(0, CHUNKS) as c:
                def spread_ahead(k, n):
                    spread_b(k, n + 4, c, 16 * c + n + 4)
                    spread_c((k + 1) % 2, n + 1, c, 16 * c + n + 1)

                spread_ahead(0, 0)
                pe.wait_ge(s["mo_ready"], 1)
                pe.wait_ge(s["yt_ready"], 2 * c + 1)
                for i in range(2):
                    mm(ps[:, i, :], diag_d[:, i, :], G(i, c), True, False, skip_group_check=True)
                sum_n(0, 16 * c)
                for k in range(1, 4):
                    spread_ahead(k, k)
                    sum_n(k % 2, 16 * c + k)
                with pe.Fori(1, 3) as m:
                    for k in range(4):
                        spread_ahead(k, 4 * m + k)
                        sum_n(k % 2, 16 * c + 4 * m + k)
                for k in range(4):
                    spread_b(k, k, c + 1, 16 * c + 16 + k)
                    spread_c((k + 1) % 2, 13 + k if k < 3 else 0, c + k // 3, 16 * c + 13 + k)
                    sum_n(k % 2, 16 * c + 12 + k, True)
            pe.wait_ge(s["yt_ready"], 2 * CHUNKS + 1)
            for c in range(CHUNKS):
                pe.wait_ge(s["yg_ready"], c + 1)
                for k in range(2):
                    last = mm(ps[:, c, :], wout_centred[:, k * 128:k * 128 + 128], G(2 + k, c), k == 0, k == 1)
                last.then_inc(s["centred"], 1)
            boundary(6)

            experts(7, 16, 8, 1, 33)
            boundary(7)

            for c in range(CHUNKS):
                pe.wait_ge(s["sum_ready"], c + 1)
                for a in range(TILES):
                    last = nc.tensor.transpose(ps[:, 4 + c, a * P:(a + 1) * P],
                                               g[:, 9, c * N + a * P:c * N + (a + 1) * P], ident)
                last.then_inc(s["raw_ready"], 1)

        @block.scalar
        def _(act):
            chain = Chain(act, s["act_chain"])

            def f(o, i, func, **kw):
                return nc.scalar.activation(o, i, func, **kw)

            def use_log_exp():
                act.preload_act_table_set("natural_log_exp_and_others")

            def square(name, src, sem, base, **bias):
                k = ACT_SQUARES.index(name)
                for c in range(CHUNKS):
                    act.wait_ge(s[sem], base + c + 1)
                    f(sq[:, cols(c)], src(c), ACT.Square, **bias).then_inc(s["sq_act"], 1)

            def rstd_of(name, eps, bank=4):
                k = NORM[name]
                for c in range(CHUNKS):
                    act.wait_ge(s["var_ready"], k * CHUNKS + c + 1)
                    chain(f(rstd[:, cols(c)], ps[:, bank + c, :], ACT.Ln, bias=eps))
                    chain.wait()
                    f(rstd[:, cols(c)], rstd[:, cols(c)], ACT.Exp, scale=-0.5).then_inc(s["rstd_ready"], 1)

            def boundary(layer):
                square(f"post{layer}", lambda c: ps[:, c, :], "centred", CHUNKS * (layer + 2),
                       **(dict(bias=comb_bias) if layer == 4 else {}))
                rstd_of(f"post{layer}", eps5)
                if layer + 1 < LAYERS:
                    rstd_of(f"pre{layer + 1}", eps5)

            use_log_exp()
            act.wait_ge(s["zeroed"], 1)
            for c in range(CHUNKS):
                act.wait_ge(s["raw_ready"], c + 1)
                f(y[:, cols(c)], ps[:, c, :], ACT.Copy).then_inc(s["y_ready"], 1)
            rstd_of("pre0", eps5, 0)
            rstd_of("ln1", eps5, 0)

            act.wait_ge(s["w_loaded"], 16)
            f(small[:, 15:16], W(0, "vec", 10, 11), ACT.Exp).then_inc(s["decay_ready"], 1)
            for c in range(CHUNKS):
                act.wait_ge(s["k_bank"], c + 1)
                f(G(5, c), ps[:, c, :], ACT.Copy)
                act.wait_ge(s["v_bank"], c + 1)
                f(G(6, c), ps[:, 4 + c, :], ACT.Copy).then_inc(s["kv_ready"], 1)
            for c in range(CHUNKS):
                act.wait_ge(s["r_bank"], c + 1)
                f(G(7, c), ps[:, c, :], ACT.Sigmoid).then_inc(s["sr_ready"], 1)
            use_log_exp()
            for c in range(CHUNKS):
                act.wait_ge(s["d12_ready"], c + 1)
                f(G(11, c), G(11, c), ACT.Exp, bias=small[:, 14:15])
                f(G(12, c), G(12, c), ACT.Exp).then_inc(s["eb_ready"], 1)
                act.wait_ge(s["d34_ready"], c + 1)
                f(G(1, c), G(1, c), ACT.Exp)
                f(G(2, c), G(2, c), ACT.Exp, bias=W(0, "vec", 7, 8)).then_inc(s["ee_ready"], 1)
            for c in range(CHUNKS):
                act.wait_ge(s["den_ready"], c + 1)
                chain(f(y[:, cols(c)], y[:, cols(c)], ACT.Ln))
                chain.wait()
                f(y[:, cols(c)], y[:, cols(c)], ACT.Exp, scale=-1.0).then_inc(s["rd_ready"], 1)
            square("ln2", lambda c: ps[:, 4 + c, :], "centred", CHUNKS)
            rstd_of("ln2", eps5, 0)
            for c in range(CHUNKS):
                act.wait_ge(s["fr_bank"], c + 1)
                f(G(8, c), ps[:, c, :], ACT.Sigmoid).then_inc(s["sr2_ready"], 1)
            use_log_exp()
            for c in range(CHUNKS):
                act.wait_ge(s["kk_ready"], 4 * c)
                for m in range(4):
                    act.wait_ge(s["fk_bank"], 4 * c + m + 1)
                    f(g[:, 6, m * N:(m + 1) * N], ps[:, m, :], ACT.Relu).then_inc(s["relu_ready"], 1)
            boundary(0)

            act.wait_ge(s["nam_bias_bank"], 1)
            f(nam_bout, ps[:, 7, 0:1], ACT.Identity, bias=W(1, "bout")).then_inc(s["nam_bias"], 1)
            def nam_out(c):
                act.wait_ge(s["nam_used"], 8 * c + 8)
                act.wait_ge(s["nam_bias"], 1)
                f(y[:, cols(c)], ps[:, 4 + c, :], ACT.Identity, bias=nam_bout).then_inc(s["y_ready"], 1)

            for c in range(CHUNKS):
                act.wait_ge(s["nam_s_bank"], c + 1)
                for j in range(8):
                    if c:
                        act.wait_ge(s[nam_lo_of(j)], 4 * (c - 1) + j // 2 + 1)
                    f(nam_hidden(j), ps[:, c, :], ACT.Relu,
                      scale=W(1, "w1", j, j + 1), bias=nam_b1[:, j:j + 1]).then_inc(s["nam_relu"], 1)
                if c:
                    nam_out(c - 1)
            nam_out(CHUNKS - 1)
            boundary(1)

            for c in range(CHUNKS):
                act.wait_ge(s["k_bank2"], c + 1)
                f(G(0, c), ps[:, c, :], ACT.Copy).then_inc(s["k2_ready"], 1)
                act.wait_ge(s["q_bank2"], c + 1)
                f(G(5, c), ps[:, 4 + c, :], ACT.Sigmoid).then_inc(s["sigq_ready"], 1)
            for c in range(CHUNKS):
                act.wait_ge(s["g1_bank"], c + 1)
                f(tmp[0:8, cols(c)], ps[0:8, c, :], ACT.Copy).then_inc(s["g1_ready"], 1)
            for c in range(CHUNKS):
                act.wait_ge(s["g2_bank"], c + 1)
                f(G(12, c), ps[:, 4 + c, :], ACT.Sigmoid).then_inc(s["gate_ready"], 1)
            use_log_exp()
            for c in range(CHUNKS):
                act.wait_ge(s["md_ready"], c + 1)
                f(G(3, c), G(3, c), ACT.Exp)
                f(G(4, c), G(4, c), ACT.Exp).then_inc(s["me_ready"], 1)
            for c in range(CHUNKS):
                act.wait_ge(s["s_ready"], c + 1)
                chain(f(rstd[:, cols(c)], G(2, c, 1), ACT.Ln))
                chain.wait()
                f(rstd[:, cols(c)], rstd[:, cols(c)], ACT.Exp, scale=-1.0).then_inc(s["rs_ready"], 1)
            square("rms", lambda c: G(4, c), "og_ready", 0)
            rstd_of("rms", eps6, 0)
            boundary(2)

            act.wait_ge(s["f_setup"], 1)
            def first(c):
                act.wait_ge(s["a1_split"], 4 * c)
                for m in range(4):
                    act.wait_ge(s["a1_bank"], 4 * c + m + 1)
                    f(g[:, 0, m * N:(m + 1) * N], ps[:, m, :], ACT.Relu, scale=scales[:, 0:1])\
                        .then_inc(s["a1_relu"], 1)

            first(0)
            for c in range(CHUNKS):
                act.wait_ge(s["a2_split"], 4 * c)
                for m in range(4):
                    act.wait_ge(s["a2_bank"], 4 * c + m + 1)
                    f(g[:, 1, m * N:(m + 1) * N], ps[:, 4 + m, :], ACT.Relu, scale=scales[:, 1:2])\
                        .then_inc(s["a2_relu"], 1)
                if c + 1 < CHUNKS:
                    first(c + 1)
                else:
                    act.wait_ge(s["comb_bank"], 1)
                    f(comb_t, ps[:, 0, 0:128], ACT.Copy)
                    f(comb_sum, ps[:, 1, 0:1], ACT.Identity, bias=W(4, "bo")).then_inc(s["comb_ready"], 1)
                act.wait_ge(s["a3_bank"], c + 1)
                f(y[:, cols(c)], ps[:, 7, :], ACT.Copy, scale=scales[:, 2:3]).then_inc(s["y_ready"], 1)
            act.wait_ge(s["comb_bank"], 2)
            f(comb, ps[:, 6, 0:128], ACT.Copy)
            f(comb_bias, ps[:, 5, 0:1], ACT.Copy).then_inc(s["comb_ready"], 1)
            boundary(3)

            boundary(4)

            def experts(layer, n_experts, pairs, order, r0):
                base1, base0 = (0, 0) if layer == 5 else (17, 16)
                for c in range(CHUNKS):
                    act.wait_ge(s["h_ready"], CHUNKS * layer + c + 1)
                    f(x_hi[:, cols(c)], H(c), ACT.Copy).then_inc(s["x_hi_ready"], 1)
                    act.wait_ge(s["lg_bank"], CHUNKS * order + c + 1)
                    f(sc_rows[0:n_experts, cols(c)], ps[0:n_experts, c, :], ACT.Sigmoid).then_inc(s["lg_ready"], 1)

                def gate_up_hi(r, slot, loaded):
                    act.wait_ge(s[f"pair_loaded{slot}"], loaded)
                    at_least(act, s["u_bank"], 4 * r - 4)
                    f(w_hi[slot][:, 0:256], pair_w[slot][:, 0:256], ACT.Copy).then_inc(s["gu_hi_ready"], 1)

                def down_hi(r, slot):
                    at_least(act, s["e_done"], 4 * r - 4)
                    f(w_hi[slot][:, 256:384], pair_w[slot][:, 256:384], ACT.Copy).then_inc(s["d_hi_ready"], 1)

                def silu(n, par):
                    act.wait_ge(s["g_bank"], n + 1)
                    at_least(act, s["t_ready"], n - 1)
                    f(g[:, 5, par * N:(par + 1) * N], ps[:, 4 if par == 0 else 7, :], ACT.Silu)\
                        .then_inc(s["sg_ready"], 1)

                def hidden_hi(n, c):
                    act.wait_ge(s["hid_ready"], n + 1)
                    at_least(act, s["e_done"], n - 3)
                    f(hid_hi[:, cols(c)], g[:, 6, (c % 2) * N:(c % 2 + 1) * N], ACT.Copy).then_inc(s["hh_ready"], 1)

                def round_of(r, slot, following=None):
                    for c in range(CHUNKS):
                        silu(4 * r + c, c % 2)
                        if c or not isinstance(r, int) or r > r0:
                            hidden_hi(4 * r + (c - 1), (c - 1) % 4)
                        if following is not None and c == 0:
                            gate_up_hi(r + 1, 1 - slot, following)
                        if following is not None and c == 3:
                            down_hi(r + 1, 1 - slot)

                gate_up_hi(r0, 1, 16 * (base1 + 1))
                down_hi(r0, 1)
                act.wait_ge(s["sc_bank"], order + 1)
                w = T // P * n_experts
                f(g[:, 1, 0:w], ps[:, 4:6, :].rearrange("p b n -> p (b n)")[:, 0:w], ACT.Copy)\
                    .then_inc(s["sc_copied"], 1)
                round_of(r0, 1, 16 * (base0 + 1))
                for c in range(CHUNKS):
                    act.wait_ge(s["ct_bank"], CHUNKS * order + c + 1)
                    f(coef_rows[:, :, cols(c)], ps[0:96, 4 + c, :].bitcast(BF16).rearrange("p (t n) -> p t n", t=2),
                      ACT.Copy).then_inc(s["ct_ready"], 1)
                round_of(r0 + 1, 0, 16 * (base1 + 2))
                with act.Fori(0, pairs // 2 - 1) as i:
                    round_of(2 * i + (r0 + 2), 1, 16 * i + 16 * (base0 + 2))
                    round_of(2 * i + (r0 + 3), 0, 16 * i + 16 * (base1 + 3))
                round_of(r0 + pairs, 1)
                hidden_hi(4 * (r0 + pairs) + 3, 3)
                use_log_exp()
                for c in range(CHUNKS):
                    act.wait_ge(s["e_done"], CHUNKS * (r0 + pairs) + c + 1)
                    f(y[:, cols(c)], ps[:, c, :], ACT.Copy).then_inc(s["y_ready"], 1)

            experts(5, 64, 32, 0, 0)
            boundary(5)

            act.wait_ge(s["w_loaded"], 7 * 16)
            act.wait_ge(s["a_ready"], 1)
            f(neg_a, W(6, "a_log"), ACT.Exp).then_inc(s["a_ready"], 1)
            for c in range(CHUNKS):
                for i in range(2):
                    act.wait_ge(s["xs_bank"], 2 * c + i + 1)
                    f(g[:, 8 + i, cols(c, LEAD)], ps[:, 4 * i + c, :], ACT.Copy).then_inc(s["xs_ready"], 1)
            for c in range(CHUNKS):
                for i in range(2):
                    act.wait_ge(s["z_bank"], 2 * c + i + 1)
                    f(G(2 + i, c), ps[:, 4 * i + c, :], ACT.Silu).then_inc(s["z_ready"], 1)
                for i in range(2):
                    act.wait_ge(s["conv_ready"], 2 * c + i + 1)
                    f(G(i, c), G(4 + i, c), ACT.Silu, bias=W(6, "conv_b", i, i + 1)).then_inc(s["xa_ready"], 1)
            use_log_exp()
            for c in range(CHUNKS):
                for i in (1, 0):
                    act.wait_ge(s["dt_bank"], 2 * c + 2 - i)
                    f(G(10 + i, c), ps[:, 4 * i + c, :], ACT.Relu, bias=W(6, "dt_b", i, i + 1))
                    chain(f(G(8 + i, c), ps[:, 4 * i + c, :], ACT.Abs, bias=W(6, "dt_b", i, i + 1)))
                    chain.wait()
                    chain(f(G(8 + i, c), G(8 + i, c), ACT.Exp, scale=-1.0))
                    chain.wait()
                    f(G(8 + i, c), G(8 + i, c), ACT.Ln, bias=one).then_inc(s["dt_ready"], 1)
            act.wait_ge(s["mo_bank"], 1)
            f(wout_centred, ps[:, 0, 0:256], ACT.Copy).then_inc(s["mo_ready"], 1)
            act.wait_ge(s["dl_ready"], CHUNKS)
            act.wait_ge(s["a_ready"], 3)

            def state_step(c, k, n):
                nb = k % 2
                step = 16 * c + n
                act.wait_ge(s["bb_bank"], step + 1)
                act.wait_ge(s["db_ready"], step + 1)
                f(g[:, 8, k * N:(k + 1) * N], ps[:, B_BANKS[k], :], ACT.Copy).then_inc(s["bs_ready"], 1)
                hold(act, s["hs_done"], step + 1)
                for i in range(2):
                    f(g[:, 9, (2 * nb + i) * N:(2 * nb + i + 1) * N], G(4 + i, c), ACT.Exp,
                      scale=neg_a[:, bass.ds(n + 16 * i, 1)]).then_inc(s["da_ready"], 1)

            def states_2_to_15(c):
                for n in (2, 3):
                    state_step(c, n, n)
                with act.Fori(1, 4) as m:
                    for k in range(4):
                        state_step(c, k, 4 * m + k)

            def sums_out(c):
                hold(act, s["sum_done"], 16 * c + 18)
                for i in range(2):
                    f(G(i, c), ps[:, i, :], ACT.Copy).then_inc(s["yt_ready"], 1)

            act.sem_inc(s["yt_ready"], 1)
            for n in (0, 1):
                state_step(0, n, n)
            with act.Fori(0, CHUNKS - 1) as c:
                states_2_to_15(c)
                for n in (0, 1):
                    state_step(c + 1, n, n)
                sums_out(c)
            states_2_to_15(CHUNKS - 1)
            sums_out(CHUNKS - 1)
            boundary(6)

            experts(7, 16, 8, 1, 33)
            boundary(7)

            for c in range(CHUNKS):
                act.wait_ge(s["raw_ready"], CHUNKS + c + 1)
                f(G(10, c), ps[:, 4 + c, :], ACT.Copy).then_inc(s["back_ready"], 1)

        @block.gpsimd
        def _(pool):
            pv = nc.gpsimd

            def square(name, src, sem, base):
                for c in range(CHUNKS):
                    pool.wait_ge(s[sem], base + c + 1)
                    pv.tensor_tensor(sq[:, cols(c)], src(c), src(c), ALU.mult).then_inc(s["sq_pool"], 1)

            def R(c):
                return resid[:, cols(c)]

            square("pre0", R, "x_ready", 0)
            square("ln1", H, "h_ready", 0)

            def token_shift(base):
                for c in range(CHUNKS):
                    pool.wait_ge(s["h1_ready"], base + c + 1)
                    pv.tensor_tensor(G(1, c), G(0, c, 1), G(0, c, 0), ALU.subtract).then_inc(s["d_ready"], 1)

            token_shift(0)
            for c in range(CHUNKS):
                pool.wait_ge(s["pp_ready"], c + 1)
                pv.tensor_tensor(G(11, c), G(8, c, 0), G(8, c, 1), ALU.subtract)
                pv.tensor_tensor(G(12, c), G(5, c), G(8, c, 1), ALU.subtract).then_inc(s["d12_ready"], 1)
                pool.wait_ge(s["p_ready"], c + 1)
                pv.tensor_tensor(G(1, c), G(8, c, 0), G(3, c), ALU.subtract)
                pv.tensor_tensor(G(2, c), G(5, c), G(3, c), ALU.subtract).then_inc(s["d34_ready"], 1)
            token_shift(CHUNKS)

            def experts(layer, pairs, order, r0):
                for c in range(CHUNKS):
                    pool.wait_ge(s["x_hi_ready"], CHUNKS * order + c + 1)
                    pv.tensor_tensor(x_lo[:, cols(c)], H(c), x_hi[:, cols(c)].bitcast(F32), ALU.subtract)\
                        .then_inc(s["x_split"], 1)

                def weights_lo(r, slot, a, b, ready, done):
                    pool.wait_ge(s[ready], r + 1)
                    pv.tensor_tensor(w_lo[slot][:, a:b], pair_w[slot][:, a:b], w_hi[slot][:, a:b].bitcast(F32),
                                     ALU.subtract).then_inc(s[done], 1)

                def gate_up_lo(r, slot):
                    weights_lo(r, slot, 0, 256, "gu_hi_ready", "gu_split")

                def down_lo(r, slot):
                    weights_lo(r, slot, 256, 384, "d_hi_ready", "d_split")

                def round_of(r, slot, following=True):
                    for c in range(CHUNKS):
                        if following and c == 1:
                            gate_up_lo(r + 1, 1 - slot)
                        pool.wait_ge(s["hh_ready"], 4 * r + (c + 1))
                        pv.tensor_tensor(hid_lo[:, cols(c)], g[:, 6, (c % 2) * N:(c % 2 + 1) * N],
                                         hid_hi[:, cols(c)].bitcast(F32), ALU.subtract).then_inc(s["hl_ready"], 1)
                    if following:
                        down_lo(r + 1, 1 - slot)

                gate_up_lo(r0, 1)
                down_lo(r0, 1)
                round_of(r0, 1)
                round_of(r0 + 1, 0)
                with pool.Fori(0, pairs // 2 - 1) as i:
                    round_of(2 * i + (r0 + 2), 1)
                    round_of(2 * i + (r0 + 3), 0)
                round_of(r0 + pairs, 1, False)

            for layer in range(1, LAYERS):
                square(f"pre{layer}", R, "x_ready", CHUNKS * layer)
                if layer == 1:
                    for c in range(CHUNKS):
                        for j in range(1, 8, 2):
                            hi, lo = nam_parts(j)
                            pool.wait_ge(s["nam_hi"], 4 * c + j // 2 + 1)
                            pv.tensor_tensor(lo, nam_hidden(j), hi.bitcast(F32), ALU.subtract)\
                                .then_inc(s["nam_lo_pool"], 1)
                if layer == 5:
                    experts(5, 32, 0, 0)
                if layer == 7:
                    experts(7, 8, 1, 33)
                if layer == 2:
                    for c in range(CHUNKS):
                        pool.wait_ge(s["m_ready"], c + 1)
                        pv.tensor_tensor(G(3, c), G(1, c, 0), G(1, c, 1), ALU.subtract)
                        pv.tensor_tensor(G(4, c), G(0, c), G(1, c, 1), ALU.subtract).then_inc(s["md_ready"], 1)
                    pool.wait_ge(s["rope_loaded"], 16)
                    for c in range(CHUNKS):
                        pool.wait_ge(s["q_used"], c + 1)
                        pv.tensor_tensor(G(8, c), G(5, c), G(10, c), ALU.mult)
                        pv.tensor_tensor(G(9, c), G(5, c), G(11, c), ALU.mult).then_inc(s["qr_ready"], 1)
                    pool.wait_ge(s["qr_ready"], CHUNKS)
                    pool.sem_inc(s["qm_ready"], 4)
                    with pool.Fori(0, CHUNKS) as c:
                        for e in range(8):
                            par = e % 2
                            pool.wait_ge(s["st_ready"], 8 * c + e + 1)
                            hold(pool, s["qm_used"], 8 * c + e + 1)
                            pv.tensor_tensor(
                                g[:, 2, 2 * par * N:(2 * par + 2) * N].rearrange("p (r n) -> p r n", r=2),
                                two_of(1, 10, e), g[:, 8:10, cols(c)], ALU.mult).then_inc(s["qm_ready"], 1)
                if layer == 6:
                    pool.wait_ge(s["du_ready"], CHUNKS)
                    pool.sem_inc(s["db_ready"], 4)
                    with pool.Fori(0, CHUNKS) as c:
                        with pool.Fori(0, 4) as m:
                            for k in range(4):
                                nb = k % 2
                                step = 16 * c + 4 * m + k
                                pool.wait_ge(s["bs_ready"], step + 1)
                                hold(pool, s["hs_done"], step + 1)
                                pv.tensor_tensor(
                                    g[:, 10, 2 * nb * N:(2 * nb + 2) * N].rearrange("p (i n) -> p i n", i=2),
                                    g[:, 6:8, cols(c)],
                                    g[:, 8:9, k * N:(k + 1) * N].to_broadcast([P, 2, N]),
                                    ALU.mult).then_inc(s["db_ready"], 1)

        @block.vector
        def _(dve):
            v = nc.vector
            chain = Chain(dve, s["dve_chain"])

            def tt(o, a, b, op=ALU.mult):
                return v.tensor_tensor(o, a, b, op)

            def scale_by_rstd(name, o, src, done):
                for c in range(CHUNKS):
                    dve.wait_ge(s["rstd_ready"], NORM[name] * CHUNKS + c + 1)
                    tt(o(c), src(c), rstd[:, cols(c)]).then_inc(s[done], 1)

            def R(c):
                return resid[:, cols(c)]

            def boundary(layer):
                for c in range(CHUNKS):
                    dve.wait_ge(s["rstd_ready"], NORM[f"post{layer}"] * CHUNKS + c + 1)
                    if layer == 4:
                        chain(v.scalar_tensor_tensor(tmp[:, cols(c)], ps[:, c, :], comb_bias, rstd[:, cols(c)],
                                                     ALU.add, ALU.mult))
                    else:
                        chain(tt(tmp[:, cols(c)], ps[:, c, :], rstd[:, cols(c)]))
                    chain.wait()
                    tt(R(c), R(c), tmp[:, cols(c)], ALU.add).then_inc(s["x_ready"], 1)
                if layer + 1 < LAYERS:
                    scale_by_rstd(f"pre{layer + 1}", H, R, "h_ready")

            for k, value in ((13, 1.0), (49, 1e-5), (50, 1e-6)):
                v.memset(small[:, k:k + 1], value)
            v.memset(g[:, 0, 0:1], 0.0)
            v.memset(g[:, 8, 0:1], -1e38)
            v.memset(g[:, 9:11, 0:1], 0.0)
            chain(v.memset(carry[:, :], 0.0))
            v.memset(small[:, 51:52], 0.0).then_inc(s["zeroed"], 1)
            dve.wait_ge(s["consts_loaded"], 16)
            chain(v.tensor_copy(ident_bf[:, :], ident))

            for c in range(CHUNKS):
                dve.wait_ge(s["centred"], c + 1)
                tt(mean0[:, cols(c)], y[:, cols(c)], ps[:, 4 + c, :], ALU.subtract)
                v.tensor_copy(R(c), ps[:, 4 + c, :]).then_inc(s["x_ready"], 1)
            scale_by_rstd("pre0", H, R, "h_ready")

            vec = [W(0, "vec", k, k + 1) for k in range(12)]
            ln1_w, ln1_b, ln2_w, ln2_b, tmk, tmv, tmr, bonus, f_tmk, f_tmr = vec[:10]
            w_decay = small[:, 14:15]
            dve.wait_ge(s["decay_ready"], 1)
            chain(v.tensor_scalar(w_decay, small[:, 15:16], -1.0, None, ALU.mult))

            for c in range(CHUNKS):
                dve.wait_ge(s["rstd_ready"], NORM["ln1"] * CHUNKS + c + 1)
                chain(tt(tmp[:, cols(c)], H(c), rstd[:, cols(c)]))
                chain.wait()
                v.tensor_scalar(G(0, c, 1), tmp[:, cols(c)], ln1_w, ln1_b, ALU.mult, ALU.add)\
                    .then_inc(s["h1_ready"], 1)

            def mix(o, amount, c):
                return v.scalar_tensor_tensor(o, G(1, c), amount, G(0, c, 0), ALU.mult, ALU.add)

            for c in range(CHUNKS):
                dve.wait_ge(s["d_ready"], c + 1)
                mix(G(2, c), tmk, c)
                mix(G(3, c), tmv, c)
                mix(G(4, c), tmr, c).then_inc(s["mix_ready"], 1)
            for c in range(CHUNKS):
                dve.wait_ge(s["kv_ready"], c + 1)
                v.tensor_tensor_scan(G(8, c, 1), w_decay.to_broadcast([P, N]), G(5, c),
                                     g[:, 8, cols(c, 0, 1)], ALU.add, ALU.max).then_inc(s["pp_ready"], 1)
                dve.wait_ge(s["pp_ready"], c + 1)
                v.scalar_tensor_tensor(G(3, c), G(5, c), bonus, G(8, c, 0), ALU.add, ALU.max)\
                    .then_inc(s["p_ready"], 1)
            for c in range(CHUNKS):
                dve.wait_ge(s["eb_ready"], c + 1)
                dve.wait_ge(s["ee_ready"], c + 1)
                dve.wait_ge(s["sr_ready"], c + 1)
                chain(tt(G(3, c), G(12, c), G(6, c)))
                chain(v.tensor_tensor_scan(G(10, c, 1), G(11, c), G(12, c), g[:, 10, cols(c, 0, 1)],
                                           ALU.mult, ALU.add))
                chain.wait()
                chain(v.tensor_tensor_scan(G(9, c, 1), G(11, c), G(3, c), g[:, 9, cols(c, 0, 1)],
                                           ALU.mult, ALU.add))
                chain(tt(y[:, cols(c)], G(1, c), G(10, c, 0)))
                chain.wait()
                tt(y[:, cols(c)], y[:, cols(c)], G(2, c), ALU.add).then_inc(s["den_ready"], 1)
                chain(tt(G(4, c), G(1, c), G(9, c, 0)))
                chain(tt(tmp[:, cols(c)], G(2, c), G(6, c)))
                chain.wait()
                chain(tt(G(4, c), G(4, c), tmp[:, cols(c)], ALU.add))
            for c in range(CHUNKS):
                chain.wait()
                dve.wait_ge(s["rd_ready"], c + 1)
                chain(tt(G(4, c), G(4, c), y[:, cols(c)]))
                chain.wait()
                tt(G(4, c), G(4, c), G(7, c)).then_inc(s["rw_ready"], 1)
            for c in range(CHUNKS):
                dve.wait_ge(s["ow_bank"], c + 1)
                tt(G(5, c), H(c), ps[:, c, :], ALU.add).then_inc(s["x1_ready"], 1)
            for c in range(CHUNKS):
                dve.wait_ge(s["rstd_ready"], NORM["ln2"] * CHUNKS + c + 1)
                chain(tt(tmp[:, cols(c)], ps[:, 4 + c, :], rstd[:, cols(c)]))
                chain.wait()
                v.tensor_scalar(G(0, c, 1), tmp[:, cols(c)], ln2_w, ln2_b, ALU.mult, ALU.add)\
                    .then_inc(s["h1_ready"], 1)
            for c in range(CHUNKS):
                dve.wait_ge(s["d_ready"], CHUNKS + c + 1)
                mix(G(2, c), f_tmk, c)
                mix(G(4, c), f_tmr, c).then_inc(s["mix_ready"], 1)
            for c in range(CHUNKS):
                dve.wait_ge(s["fv_bank"], c)
                for m in range(4):
                    dve.wait_ge(s["relu_ready"], 4 * c + m + 1)
                    tt(g[:, 7, m * N:(m + 1) * N], g[:, 6, m * N:(m + 1) * N], g[:, 6, m * N:(m + 1) * N])\
                        .then_inc(s["kk_ready"], 1)
            for c in range(CHUNKS):
                dve.wait_ge(s["sr2_ready"], c + 1)
                dve.wait_ge(s["fv_bank"], c + 1)
                chain(tt(tmp[:, cols(c)], G(8, c), ps[:, 4 + c, :]))
                chain.wait()
                tt(y[:, cols(c)], G(5, c), tmp[:, cols(c)], ALU.add).then_inc(s["y_ready"], 1)

            dve.wait_ge(s["w_loaded"], 32)
            v.scalar_tensor_tensor(nam_b1, W(1, "w1"), W(1, "bin"), W(1, "b1"), ALU.mult, ALU.add)
            for j in range(8):
                last = v.tensor_scalar(nam_wout[j], W(1, "wout"), W(1, "w2", j, j + 1), None, ALU.mult)
            chain(last)
            chain.wait()
            chain(v.tensor_copy(nam_w[0], derived(1, 0, 1024)))
            chain.wait()
            tt(nam_w[1], derived(1, 0, 1024), nam_w[0].bitcast(F32), ALU.subtract).then_inc(s["nam_setup"], 1)
            boundary(0)
            for c in range(CHUNKS):
                for j in range(8):
                    dve.wait_ge(s["nam_relu"], 8 * c + j + 1)
                    if c:
                        dve.wait_ge(s["nam_used"], 8 * c - 8 + j + 1)
                    high = v.tensor_copy(nam_parts(j)[0], nam_hidden(j))
                    if j % 2 == 0:
                        chain(high)
                        continue
                    high.then_inc(s["nam_hi"], 1)
                    chain.wait()
                    hi, lo = nam_parts(j - 1)
                    tt(lo, nam_hidden(j - 1), hi.bitcast(F32), ALU.subtract).then_inc(s["nam_lo_dve"], 1)
            boundary(1)

            dve.wait_ge(s["w_loaded"], 48)
            v.memset(g[:, 1, 0:1], 0.0)
            chain(v.memset(g[:, 2, 0:1], 1.0))
            chain.wait()
            for c in range(CHUNKS):
                dve.wait_ge(s["k2_ready"], c + 1)
                v.tensor_tensor_scan(G(1, c, 1), G(0, c), G(0, c), g[:, 1, cols(c, 0, 1)],
                                     ALU.max, ALU.max).then_inc(s["m_ready"], 1)
                dve.wait_ge(s["m_ready"], c + 1)
            for c in range(CHUNKS):
                dve.wait_ge(s["sigq_ready"], c + 1)
                tt(G(5, c), G(5, c), ps[:, 4 + c, :]).then_inc(s["q_used"], 1)
            for c in range(CHUNKS):
                dve.wait_ge(s["me_ready"], c + 1)
                v.tensor_tensor_scan(G(2, c, 1), G(3, c), G(4, c), g[:, 2, cols(c, 0, 1)],
                                     ALU.mult, ALU.add).then_inc(s["s_ready"], 1)
                dve.wait_ge(s["s_ready"], c + 1)
            dve.sem_inc(s["vb_used"], 4)
            dve.wait_ge(s["wo_bank"], 1)
            v.tensor_scalar(wo_normed, ps[:, 7, 0:128], W(2, "norm_w"), None, ALU.mult).then_inc(s["setup2"], 1)
            dve.wait_ge(s["rope_loaded"], 16)
            for c in range(CHUNKS):
                dve.wait_ge(s["rs_ready"], c + 1)
                chain(tt(G(4, c), G(4, c), rstd[:, cols(c)]))
                chain.wait()
                chain(v.tensor_scalar(G(3, c), G(4, c), -1.0, 1.0, ALU.mult, ALU.add))
                tt(G(6, c), G(4, c), G(10, c))
                chain(tt(G(7, c), G(4, c), G(11, c)))
            chain.wait()
            dve.wait_ge(s["qr_ready"], CHUNKS)

            def inputs(e, c):
                hold(dve, s["vb_bank"], 8 * c + e + 1)
                tt(two_of(0, 11, e), g[:, 6:8, cols(c)],
                   ps[:, e % 4:e % 4 + 1, :].to_broadcast([P, 2, N])).then_inc(s["vb_used"], 1)

            def carry_on(e, c):
                dve.wait_ge(s["st_ready"], 8 * c + e + 1)
                chain(v.tensor_copy(carry[:, 2 * e:2 * e + 2], two_of(1, 10, e)[:, :, N - 1]))

            with chain.each(CHUNKS, 8) as c:
                inputs(0, c)
                for e in range(8):
                    if e < 7:
                        inputs(e + 1, c)
                    chain.wait(but=1)
                    dve.wait_ge(s["vb_used"], 8 * c + e + 5)
                    hold(dve, s["qm_ready"], 8 * c + e + 1)
                    for r in range(2):
                        last = v.tensor_tensor_scan(two_of(1, 10, e)[:, r, :], G(3, c), two_of(0, 11, e)[:, r, :],
                                                    carry[:, 2 * e + r:2 * e + r + 1], ALU.mult, ALU.add)
                    last.then_inc(s["st_ready"], 1)
                    if e:
                        carry_on(e - 1, c)
                carry_on(7, c)
            for c in range(CHUNKS):
                dve.wait_ge(s["qm_used"], 8 * c + 10)
                tt(G(4, c), G(12, c), ps[:, 4 + c, :]).then_inc(s["og_ready"], 1)
            scale_by_rstd("rms", lambda c: G(5, c), lambda c: G(4, c), "nrm_ready")
            dve.wait_ge(s["w_loaded"], 64)
            dve.wait_ge(s["bools_loaded"], 16)
            tt(sign0, kbool[:, 0:512], kbool[:, 512:1024], ALU.subtract)
            v.tensor_scalar(sign1, kbool[:, 1024:3072], 2.0, -1.0, ALU.mult, ALU.add)
            v.tensor_scalar(sign2, kbool[:, 3072:3584], 2.0, -1.0, ALU.mult, ALU.add)
            v.tensor_scalar(scales[:, 0:1], W(3, "s", 0, 1), 4.0, None, ALU.mult)
            v.tensor_scalar(scales[:, 1:2], W(3, "s", 1, 2), 2.0, None, ALU.mult)
            v.tensor_copy(scales[:, 2:3], W(3, "s", 2, 3)).then_inc(s["f_setup"], 1)
            boundary(2)
            def split(o, src):
                chain(v.tensor_copy(o[0], src))
                chain.wait()
                return tt(o[1], src, o[0].bitcast(F32), ALU.subtract)

            def split_input(c):
                dve.wait_ge(s["h_ready"], 3 * CHUNKS + c + 1)
                split((x_hi[:, cols(c)], x_lo[:, cols(c)]), H(c)).then_inc(s["fx_split"], 1)

            def split_hidden(o, c, buffer, used, relu, done):
                dve.wait_ge(s[used[0]], used[1])
                for k in range(4):
                    dve.wait_ge(s[relu], 4 * c + k + 1)
                    at = slice(k * N, (k + 1) * N)
                    split((o[0][:, at], o[1][:, at]), g[:, buffer, at]).then_inc(s[done], 1)

            split_input(0)
            split_input(1)
            for c in range(CHUNKS):
                split_hidden(hid1, c, 0, ("a2_bank", 4 * c), "a1_relu", "a1_split")
                if c == 0:
                    split_input(2)
                    split_input(3)
                split_hidden(hid2, c, 1, ("a3_bank", c), "a2_relu", "a2_split")
            boundary(3)
            boundary(4)

            def experts(layer, E, pairs, groups, keep_groups, top, order, r0):
                size = E // groups
                tiles = CHUNKS * TILES
                w = tiles * E
                whole = [home[:, k * 1024:(k + 1) * 1024]
                         for home in (g[:, 1, :], g[:, 2, :], tmp, y, sq, rstd) for k in range(2)]
                score, biased, equal, others, kept, replaced, coef = (b[:, 0:w] for b in whole[:7])
                better, ahead = whole[7][:, 0:tiles * groups * groups], whole[8][:, 0:tiles * groups * groups]
                G1 = tiles * groups
                best, count, second, group, two, keep = (whole[9][:, 128 * k:128 * k + G1] for k in range(6))
                top8 = whole[9][:, 768:768 + 8 * tiles].rearrange("p (a n) -> p a n", a=tiles)
                total, share = whole[9][:, 896:896 + tiles], whole[9][:, 912:912 + tiles]
                wide = 16 * (E + 4)
                if layer == 7:
                    padded = whole[10][:, 0:wide].rearrange("p (a n) -> p a n", a=tiles)
                    out_padded = whole[11][:, 0:wide].rearrange("p (a n) -> p a n", a=tiles)
                before = W(layer, "before", 0, groups * groups)
                bias = W(layer, "bias", 0, E)

                def by(ap, k):
                    return ap.rearrange("p (a e) -> p a e", e=k)

                def over(ap, n):
                    return by(ap, 1).to_broadcast([P, ap.shape[1], n])

                def square_of(ap, axis):
                    q = by(ap, groups)
                    q = q.unsqueeze(3) if axis == 2 else q.unsqueeze(2)
                    return q.to_broadcast([P, tiles, groups, groups])

                def step(ins):
                    chain(ins)
                    chain.wait()

                def glu(n, c, coef_no=None):
                    par = c % 2
                    silu_n = g[:, 5, par * N:(par + 1) * N]
                    prod = g[:, 5, (2 + par) * N:(3 + par) * N]
                    hidden = g[:, 6, par * N:(par + 1) * N]
                    dve.wait_ge(s["sg_ready"], n + 1)
                    dve.wait_ge(s["u_bank"], n + 1)
                    at_least(dve, s["hl_ready"], n - 1)
                    tt(prod, silu_n, ps[:, 5, :]).then_inc(s["t_ready"], 1)
                    dve.wait_ge(s["t_ready"], n + 1)
                    if coef_no is None:
                        v.tensor_copy(hidden, prod).then_inc(s["hid_ready"], 1)
                    else:
                        dve.wait_ge(s["c_bank"], coef_no)
                        tt(hidden, prod, ps[:, 6, :]).then_inc(s["hid_ready"], 1)

                dve.wait_ge(s["w_loaded"], 16 * (layer + 1))
                step(v.memset(g[:, 3, 0:1536], 0.0))
                dve.wait_ge(s["sc_bank"], order + 1)
                dve.wait_ge(s["sc_copied"], order + 1)
                step(tt(by(biased, E), by(score, E), bias.unsqueeze(1).to_broadcast([P, tiles, E]), ALU.add))
                step(v.tensor_reduce(best, by(biased, size), AX_X, ALU.max))
                if layer == 5:
                    step(tt(by(equal, size), by(biased, size), over(best, size), ALU.is_equal))
                    step(v.tensor_reduce(count, by(equal, size), AX_X, ALU.add))
                    step(v.scalar_tensor_tensor(others, equal, -BIG, biased, ALU.mult, ALU.add))
                    step(v.tensor_reduce(second, by(others, size), AX_X, ALU.max))
                    step(v.tensor_scalar(two, count, 2.0, None, ALU.is_ge))
                    step(tt(group, two, best))
                    step(v.tensor_scalar(two, two, -1.0, BIG, ALU.add, ALU.mult))
                    step(tt(group, group, two, ALU.add))
                    step(tt(second, second, group, ALU.max))
                    step(tt(group, best, second, ALU.add))
                else:
                    group = best
                glu(4 * r0, 0)
                glu(4 * r0 + 1, 1)
                b4 = better.rearrange("p (a i j) -> p a i j", i=groups, j=groups)
                a4 = ahead.rearrange("p (a i j) -> p a i j", i=groups, j=groups)
                chain(tt(b4, square_of(group, 3), square_of(group, 2), ALU.is_gt))
                step(tt(a4, square_of(group, 3), square_of(group, 2), ALU.is_equal))
                step(tt(by(ahead, groups * groups), by(ahead, groups * groups),
                        before.unsqueeze(1).to_broadcast([P, tiles, groups * groups])))
                step(tt(better, better, ahead, ALU.add))
                glu(4 * r0 + 2, 2)
                glu(4 * r0 + 3, 3)
                step(v.tensor_reduce(keep, by(better, groups), AX_X, ALU.add))
                step(v.tensor_scalar(keep, keep, float(keep_groups), None, ALU.is_lt))
                step(tt(by(kept, size), by(biased, size), over(keep, size)))
                if layer == 5:
                    for a in range(tiles):
                        last = v.max(top8[:, a, :], kept[:, a * E:(a + 1) * E])
                    step(last)
                    for a in range(tiles):
                        last = v.match_replace(replaced[:, a * E:(a + 1) * E], top8[:, a, :],
                                               kept[:, a * E:(a + 1) * E], BIG)
                    step(last)
                    chosen = replaced
                else:
                    step(v.tensor_scalar(keep, keep, -1.0, BIG, ALU.add, ALU.mult))
                    step(tt(by(kept, size), by(kept, size), over(keep, size), ALU.add))
                    chain(v.memset(padded[:, :, E:E + 4], -2 * BIG))
                    step(v.tensor_copy(padded[:, :, 0:E], by(kept, E)))
                    for a in range(tiles):
                        last = v.max(top8[:, a, :], kept[:, a * E:(a + 1) * E])
                    step(last)
                    step(v.memset(top8[:, :, 4:8], -2 * BIG))
                    for a in range(tiles):
                        last = v.match_replace(out_padded[:, a, :], top8[:, a, :], padded[:, a, :], BIG)
                    step(last)
                    step(v.tensor_copy(by(replaced, E), out_padded[:, :, 0:E]))
                step(v.scalar_tensor_tensor(coef, replaced, BIG, score, ALU.is_equal, ALU.mult))
                if layer == 5:
                    step(v.tensor_reduce(total, by(coef, E), AX_X, ALU.add))
                    step(v.tensor_scalar(total, total, 1e-20, None, ALU.add))
                    step(v.reciprocal(share, total))
                    step(v.tensor_scalar(share, share, 2.5, None, ALU.mult))
                    step(tt(by(coef, E), by(coef, E), over(share, E)))
                for part in range(3):
                    for t in range(2):
                        view = coef.rearrange("p (a q t r) -> p a q t r", a=tiles, t=2, r=2)[:, :, :, t, :]
                        dst = coef_parts[:, :, t, 32 * part:32 * part + E // 2]\
                            .rearrange("p a (q r) -> p a q r", r=2)
                        if part < 2:
                            chain(v.tensor_copy(dst, view))
                        else:
                            last = v.tensor_copy(dst, view)
                    if part < 2:
                        chain.wait()
                        for t in range(2):
                            view = coef.rearrange("p (a q t r) -> p a q t r", a=tiles, t=2, r=2)[:, :, :, t, :]
                            dst = coef_parts[:, :, t, 32 * part:32 * part + E // 2]\
                                .rearrange("p a (q r) -> p a q r", r=2)
                            chain(tt(view, view, dst, ALU.subtract))
                        chain.wait()
                last.then_inc(s["parts_ready"], 1)

                n0 = r0 * CHUNKS
                c0 = 0 if layer == 5 else 32 * CHUNKS
                with dve.Fori(0, pairs) as p:
                    for c in range(CHUNKS):
                        glu(p * CHUNKS + (n0 + CHUNKS + c), c, p * CHUNKS + (c0 + c + 1))

            experts(5, 64, 32, 8, 4, 8, 0, 0)
            boundary(5)

            dve.wait_ge(s["w_loaded"], 7 * 16)
            v.tensor_scalar(W(6, "a_log"), W(6, "a_log"), 80.0, None, ALU.min).then_inc(s["a_ready"], 1)
            dve.wait_ge(s["a_ready"], 2)
            v.tensor_scalar(neg_a, neg_a, -1.0, None, ALU.mult).then_inc(s["a_ready"], 1)
            for i in range(2):
                v.tensor_scalar(diag_d[:, i, :], ident, W(6, "d", i, i + 1), None, ALU.mult)
            chain(v.memset(g[:, 8:10, 0:LEAD], 0.0))
            chain.wait()
            for c in range(CHUNKS):
                dve.wait_ge(s["xs_ready"], 2 * c + 2)
                for j in range(4):
                    for i in range(2):
                        window, tap = g[:, 8 + i, cols(c, j)], W(6, "conv", 4 * i + j, 4 * i + j + 1)
                        if j == 0:
                            chain(v.tensor_scalar(G(4 + i, c), window, tap, None, ALU.mult))
                            continue
                        chain.wait(but=0 if (j, i) == (3, 1) else 1)
                        last = v.scalar_tensor_tensor(G(4 + i, c), window, tap, G(4 + i, c), ALU.mult, ALU.add)
                        if j < 3:
                            chain(last)
                        else:
                            last.then_inc(s["conv_ready"], 1)
            v.memset(g[0:96, 12, T // 2:T // 2 + N // 2], 0.0)
            chain(v.memset(carry[:, :], 0.0))
            rest = tmp[0:96, 0:N]
            mid = tmp[0:96, N:2 * N].bitcast(BF16)[:, 0:N]

            def b_and_c(c):
                high = bc_rows[0:96, cols(c)]
                dve.wait_ge(s["bc_bank"], c + 1)
                chain(v.tensor_copy(high, ps[0:96, c, :]))
                chain.wait()
                v.tensor_tensor(rest, ps[0:96, c, :], high, ALU.subtract).then_inc(s["bc_read"], 1)
                dve.wait_ge(s["bc_read"], c + 1)
                chain(v.tensor_copy(mid, rest))
                chain.wait()
                chain(v.tensor_copy(high[32:64], mid[32:64]))
                v.tensor_tensor(high[64:96], rest[64:96], mid[64:96], ALU.subtract).then_inc(s["bcp_ready"], 1)

            b_and_c(0)
            for c in range(CHUNKS):
                if c + 1 < CHUNKS:
                    b_and_c(c + 1)
                dve.wait_ge(s["dt_ready"], 2 * c + 2)
                tt(g[:, 4:6, cols(c)], g[:, 8:10, cols(c)], g[:, 10:12, cols(c)], ALU.add)\
                    .then_inc(s["dl_ready"], 1)
                dve.wait_ge(s["dl_ready"], c + 1)
                tt(g[:, 6:8, cols(c)], g[:, 4:6, cols(c)], g[:, 0:2, cols(c)]).then_inc(s["du_ready"], 1)
            chain.wait()
            dve.wait_ge(s["bcp_ready"], CHUNKS)
            dve.sem_inc(s["hs_done"], 2)
            carried = carry.rearrange("p (i n) -> p i n", i=2)

            def buffer_of(k):
                home = g[:, 11, :] if k < 2 else y
                return home[:, 2 * (k % 2) * N:2 * (k % 2 + 1) * N].rearrange("p (i n) -> p i n", i=2)

            def scan(k, n, step):
                dve.wait_ge(s["da_ready"], 2 * step + 2)
                dve.wait_ge(s["db_ready"], step + 5)
                chain.wait(but=1)
                dve.nop(nofuse=True)
                for i in range(2):
                    at = slice((2 * (k % 2) + i) * N, (2 * (k % 2) + i + 1) * N)
                    ins = v.tensor_tensor_scan(buffer_of(k)[:, i, :], g[:, 9, at], g[:, 10, at],
                                               carry[:, bass.ds(n + 16 * i, 1)], ALU.mult, ALU.add)
                ins.then_inc(s["hs_done"], 1)

            def times_c(k, n, step):
                nb = k % 2
                dve.wait_ge(s["cb_bank"], step + 1)
                dve.wait_ge(s["sum_done"], step + 1)
                hold(dve, s["hs_done"], step + 3)
                tt(tmp[:, 2 * nb * N:(2 * nb + 2) * N].rearrange("p (i n) -> p i n", i=2), buffer_of(k),
                   ps[:, 4 + nb:5 + nb, :].to_broadcast([P, 2, N])).then_inc(s["hc_ready"], 1)
                chain(v.tensor_copy(carried[:, :, bass.ds(n, 1)], buffer_of(k)[:, :, N - 1:N]))

            with chain.each(CHUNKS, 16) as c:
                scan(0, 0, 16 * c)
                with chain.each(3, 4) as m:
                    for k in range(4):
                        n = 4 * m + k
                        scan((k + 1) % 4, n + 1, 16 * c + n + 1)
                        times_c(k, n, 16 * c + n)
                for n in range(12, 15):
                    scan((n + 1) % 4, n + 1, 16 * c + n + 1)
                    times_c(n % 4, n, 16 * c + n)
                times_c(3, 15, 16 * c + 15)
            chain.wait()
            for c in range(CHUNKS):
                dve.wait_ge(s["yt_ready"], 2 * c + 3)
                tt(g[:, 2:4, cols(c)], g[:, 0:2, cols(c)], g[:, 2:4, cols(c)]).then_inc(s["yg_ready"], 1)
            boundary(6)

            experts(7, 16, 8, 4, 2, 4, 1, 33)
            boundary(7)

            for c in range(CHUNKS):
                dve.wait_ge(s["x_ready"], LAYERS * CHUNKS + c + 1)
                tt(G(9, c), R(c), mean0[:, cols(c)], ALU.add).then_inc(s["sum_ready"], 1)


def kernel(**inputs):
    import ml_dtypes
    import numpy as _np
    import concourse.bacc as _bacc
    from concourse import mybir as _mybir
    from concourse.bass_utils import run_bass_kernel_spmd as _run

    a = {k: _np.asarray(v) for k, v in inputs.items()}

    def L(layer, name):
        return a[f"L{layer // 2}_{'attn' if layer % 2 == 0 else 'ffn'}_{name}"]

    def tiled(m):
        return m.reshape(-1, P, m.shape[1]).transpose(1, 0, 2).reshape(P, -1)

    def col(v):
        return v.reshape(-1, P).T

    def rows(m):
        return _np.concatenate([m, _np.zeros((P - m.shape[0], m.shape[1]), m.dtype)], 0)

    def all_rows(v):
        return _np.broadcast_to(v.reshape(1, -1), (P, v.size))

    def twice(m):
        return _np.concatenate([m, m], 0)

    def halves(m):
        return m.reshape(64, 8, 2).transpose(2, 0, 1).reshape(P, 8)

    ch = _np.arange(P)
    f32 = _np.float32
    head_sum = _np.stack([(ch[:, None] // 8 == ch[None] // 8) & (ch[None] % 8 == e) for e in range(8)], 1)
    head_mean = (ch[:, None] // 8 == ch[None] // 8) / 8.0

    def before(n):
        i = _np.arange(n)
        m = _np.zeros(64)
        m[:n * n] = (i[None] < i[:, None]).reshape(-1)
        return all_rows(m.astype(f32))

    wv2 = L(4 - 2, "wv").reshape(P, 16, 8)
    packed = [
        dict(kw=L(0, "att_kw").T, vw=L(0, "att_vw").T, rw=L(0, "att_rw").T, ow=L(0, "att_ow").T,
             frw=L(0, "f_rw").T, fkw=L(0, "f_kw").T, fvw=tiled(L(0, "f_vw").T),
             vec=_np.stack([L(0, n) for n in ("ln1_w", "ln1_b", "ln2_w", "ln2_b", "tmk", "tmv", "tmr",
                                              "time_first", "f_tmk", "f_tmr", "time_decay")]
                           + [_np.zeros(P, f32)], 1)),
        dict(win=_np.concatenate([L(1, "Win")] * 2, 1), wout=twice(L(1, "Wout")), w1=halves(L(1, "W1")),
             b1=halves(L(1, "b1")), w2=halves(L(1, "W2")), bin=twice(L(1, "bin_")[:, None]),
             b2=twice(L(1, "b2")[:, None]), bout=col(L(1, "bout"))),
        dict(wq=L(2, "wq"), wk=L(2, "wk"),
             wv=_np.stack([_np.repeat(wv2[:, :, e], 8, 1) for e in range(8)], 1).reshape(P, -1),
             wg1=L(2, "wg1"), wg2=rows(L(2, "wg2")), wo=L(2, "wo").T, norm_w=col(L(2, "norm_w")),
             head_sum=head_sum.astype(f32).reshape(P, -1), head_mean=head_mean.astype(f32)),
        dict(s=_np.stack([_np.broadcast_to(L(3, n), (P,)) for n in ("s0", "s1", "s2")], 1)),
        dict(wv=L(4, "in_proj_weight")[2048:].reshape(8, P, P).transpose(1, 0, 2).reshape(P, -1),
             wo=tiled(L(4, "out_proj_weight").T), bv=col(L(4, "in_proj_bias")[2048:]),
             bo=col(L(4, "out_proj_bias"))),
        dict(router=L(5, "router_w").T, bias=all_rows(L(5, "e_bias")), before=before(8)),
        dict(wx=L(6, "in_proj_w")[:256].T, conv=tiled(L(6, "conv_w")[:, 0, :]),
             wz=L(6, "in_proj_w")[256:].T,
             wbc=tiled(_np.concatenate([L(6, "x_proj_w").T] * 3, 1)),
             wdt=tiled(L(6, "dt_proj_w").T), wout=L(6, "out_proj_w"), conv_b=col(L(6, "conv_b")),
             dt_b=col(L(6, "dt_proj_b")), a_log=tiled(L(6, "A_log")), d=col(L(6, "D_param"))),
        dict(router=L(7, "gate_w").T, bias=all_rows(L(7, "gate_bias")), before=before(4)),
    ]
    blocks = []
    for layer in range(8):
        for name, width in LAYOUT[layer]:
            block = packed[layer][name]
            assert block.shape == (P, width), (layer, name, block.shape)
            blocks.append(block)
    weights = _np.ascontiguousarray(_np.concatenate(blocks, 1))

    def pairs(gate, up, down):
        E, Hn, I = gate.shape
        w = [m.reshape(E // 2, 2, Hn, I).transpose(0, 2, 1, 3).reshape(E // 2, Hn, 2 * I) for m in (gate, up)]
        return _np.concatenate(w + [down.reshape(E // 2, 2 * I, Hn)], 2)

    def wide(m):
        return _np.concatenate([m, _np.zeros((P, P - m.shape[1]), m.dtype)], 1)

    shared5 = _np.concatenate([L(5, "SWg"), L(5, "SWu"), L(5, "SWd")], 1)[None]
    shared7 = _np.concatenate([wide(L(7, "ws1").T), wide(L(7, "ws3").T), rows(L(7, "ws2").T)], 1)[None]
    T_ = (0, 2, 1)
    moe0 = _np.concatenate([shared5, pairs(L(5, "Wg"), L(5, "Wu"), L(5, "Wd"))], 0)
    moe1 = _np.concatenate([shared7, pairs(L(7, "w1").transpose(T_), L(7, "w3").transpose(T_),
                                           L(7, "w2").transpose(T_))], 0)
    bools = _np.concatenate([L(3, "k0")[:P], L(3, "k0")[P:], tiled(L(3, "k1")), tiled(L(3, "k2"))], 1)
    eye = _np.eye(P)
    consts = _np.concatenate([eye, eye - 1.0 / P, _np.full((P, P), 1.0 / P)], 1).astype(f32)

    sel = _np.zeros((96, 48, P), ml_dtypes.bfloat16)
    for part in range(3):
        for n in range(32):
            sel[32 * part + n, n, :] = 1
        for q in range(16):
            sel[32 * part + 2 * q, 32 + q, :64] = 1
            sel[32 * part + 2 * q + 1, 32 + q, 64:] = 1
    theta = (10000.0 ** (-2.0 / P * _np.arange(P))).astype(f32)
    angle = (theta[:, None] * _np.arange(T, dtype=f32)[None]).astype(f32)
    rope = _np.stack([_np.cos(angle), _np.sin(angle)], 1).astype(f32)

    host = dict(x=a["L0_attn_x"].reshape(T, P), weights=weights, bools=_np.ascontiguousarray(bools).view(_np.uint32), moe0=moe0,
                moe1=moe1, consts=consts, selectors=sel, rope=rope)
    nc = _bacc.Bacc("TRN2", target_bir_lowering=False, num_devices=1)
    arrays, aps = {}, {}
    for name, m in host.items():
        m = _np.ascontiguousarray(m)
        arrays[f"in_{name}_dram"] = m
        aps[name] = nc.dram_tensor(f"in_{name}_dram", m.shape, _mybir.dt.from_np(m.dtype),
                                   kind="ExternalInput").ap()
    out = nc.dram_tensor("out_dram", (T, P), _mybir.dt.float32, kind="ExternalOutput").ap()
    sandwich(nc, aps["x"], out, aps["weights"], aps["bools"], aps["moe0"], aps["moe1"], aps["consts"],
             aps["selectors"], aps["rope"])
    r = _run(nc, [arrays], core_ids=[0])
    return r.results[0]["out_dram"].reshape(1, T, P)
```
